# Optimizing a Trainium2 kernel written in Bass

```python
import numpy as np
import jax
import jax.numpy as jnp

def _softmax(x, axis=-1):
    return jax.nn.softmax(x, axis=axis)

def _gelu(x):
    return jax.nn.gelu(x, approximate=True)

def _silu(x):
    return jax.nn.silu(x)

def _sigmoid(x):
    return jax.nn.sigmoid(x)

def _layernorm(x, axis=-1, eps=1e-05):
    m = jnp.mean(x, axis=axis, keepdims=True)
    v = jnp.var(x, axis=axis, keepdims=True)
    return (x - m) / jnp.sqrt(v + eps)

def _scatter_add(tgt, idx, src, axis=0):
    return tgt.at[idx].add(src)

def _segment_sum(src, seg, n):
    return jax.ops.segment_sum(src, seg, n)
kernel_name = 'mk_adaln_d2_jaxref_r4_6343f1'

def setup_inputs(seed: int=0):
    np.random.seed(seed)
    _w = jnp.asarray

    def _L0_attn_setup():
        import jax, jax.numpy as jnp
        import numpy as np
        DIM = 256
        H = 16
        HD = DIM // H
        EPS_DENOM = 1e-06
        EPS_LN = 1e-05
        key = jax.random.key(seed)
        ks = jax.random.split(key, 8)
        B, N = (4, 1024)
        s = 1.0 / np.sqrt(DIM)
        return {'x': jax.random.normal(ks[0], (B, N, DIM), dtype=jnp.float32), 'Wq': jax.random.normal(ks[1], (DIM, DIM), dtype=jnp.float32) * s, 'bq': jnp.zeros((DIM,), dtype=jnp.float32), 'Wk': jax.random.normal(ks[2], (DIM, DIM), dtype=jnp.float32) * s, 'bk': jnp.zeros((DIM,), dtype=jnp.float32), 'Wv': jax.random.normal(ks[3], (DIM, DIM), dtype=jnp.float32) * s, 'bv': jnp.zeros((DIM,), dtype=jnp.float32), 'gamma': jnp.ones((DIM,), dtype=jnp.float32), 'beta': jnp.zeros((DIM,), dtype=jnp.float32)}
    _L0_attn_in = _L0_attn_setup()

    def _L0_ffn_setup():
        import jax, jax.numpy as jnp
        import numpy as np
        TOP_K = 2
        key = jax.random.key(seed)
        k1, k2, k3, k4, k5 = jax.random.split(key, 5)
        B, S, D, F, E = (2, 256, 256, 512, 8)
        return {'x': jax.random.normal(k1, (B, S, D), dtype=jnp.float32), 'router_kernel_DE': jax.random.normal(k2, (D, E), dtype=jnp.float32) * 0.02, 'kernel_gating_EDF': jax.random.normal(k3, (E, D, F), dtype=jnp.float32) * 0.02, 'kernel_up_EDF': jax.random.normal(k4, (E, D, F), dtype=jnp.float32) * 0.02, 'kernel_down_EFD': jax.random.normal(k5, (E, F, D), dtype=jnp.float32) * 0.02}
    _L0_ffn_in = _L0_ffn_setup()
    _L0_c = _w((lambda *s: np.random.randn(*s).astype(np.float32) * 0.05)(2, 256))
    _L0_wmod = _w((lambda *s: np.random.randn(*s).astype(np.float32) * 0.05)(256, 6 * 256) * 256 ** (-0.5))

    def _L1_attn_setup():
        import jax, jax.numpy as jnp
        import numpy as np
        B, L, D = (2, 512, 256)
        H = 16
        DH = D // H

        def rope_tables(seq_len, dim):
            inv_freq = 1.0 / 10000.0 ** (jnp.arange(0, dim, 2, dtype=jnp.float32) / dim)
            t = jnp.arange(seq_len, dtype=jnp.float32)
            freqs = jnp.outer(t, inv_freq)
            emb = jnp.concatenate([freqs, freqs], -1)
            return (jnp.cos(emb), jnp.sin(emb))

        def rotate_half(x):
            x1, x2 = (x[..., :x.shape[-1] // 2], x[..., x.shape[-1] // 2:])
            return jnp.concatenate([-x2, x1], axis=-1)
        key = jax.random.key(seed)
        k1, k2, k3 = jax.random.split(key, 3)
        x = jax.random.normal(k1, (B, L, D), dtype=jnp.float32)
        Wqkv = jax.random.normal(k2, (D, 3 * D), dtype=jnp.float32) / np.sqrt(D)
        Wo = jax.random.normal(k3, (D, D), dtype=jnp.float32) / np.sqrt(D)
        return {'x': x, 'Wqkv': Wqkv, 'Wo': Wo}
    _L1_attn_in = _L1_attn_setup()

    def _L1_ffn_setup():
        import jax, jax.numpy as jnp
        import numpy as np
        DIM = 256
        HEADS = 8
        NUM_EXPERTS = 16384
        NUM_KEYS = 64
        DIM_KEY = 128
        PK_TOPK = 16
        FINAL_TOPK = 1
        BATCH, SEQ = (4, 512)
        key = jax.random.key(seed)
        k1, k2, k3, k4, k5 = jax.random.split(key, 5)
        x = jax.random.normal(k1, (BATCH, SEQ, DIM), jnp.float32)
        w_q = jax.random.normal(k2, (DIM, 2 * HEADS * DIM_KEY), jnp.float32) * 0.02
        keys = jax.random.normal(k3, (HEADS, NUM_KEYS, 2, DIM_KEY), jnp.float32) * 0.02
        w_down = jax.random.normal(k4, (NUM_EXPERTS, DIM), jnp.float32) * 0.02
        w_up = jax.random.normal(k5, (NUM_EXPERTS, DIM), jnp.float32) * 0.02
        return {'x': x, 'w_q': w_q, 'keys': keys, 'w_down': w_down, 'w_up': w_up}
    _L1_ffn_in = _L1_ffn_setup()
    _L1_c = _w((lambda *s: np.random.randn(*s).astype(np.float32) * 0.05)(2, 256))
    _L1_wmod = _w((lambda *s: np.random.randn(*s).astype(np.float32) * 0.05)(256, 6 * 256) * 256 ** (-0.5))
    _d = {'L0_attn_x': _L0_attn_in['x'], 'L0_attn_Wq': _L0_attn_in['Wq'], 'L0_attn_bq': _L0_attn_in['bq'], 'L0_attn_Wk': _L0_attn_in['Wk'], 'L0_attn_bk': _L0_attn_in['bk'], 'L0_attn_Wv': _L0_attn_in['Wv'], 'L0_attn_bv': _L0_attn_in['bv'], 'L0_attn_gamma': _L0_attn_in['gamma'], 'L0_attn_beta': _L0_attn_in['beta'], 'L0_ffn_router_kernel_DE': _L0_ffn_in['router_kernel_DE'], 'L0_ffn_kernel_gating_EDF': _L0_ffn_in['kernel_gating_EDF'], 'L0_ffn_kernel_up_EDF': _L0_ffn_in['kernel_up_EDF'], 'L0_ffn_kernel_down_EFD': _L0_ffn_in['kernel_down_EFD'], 'L0_c': _L0_c, 'L0_wmod': _L0_wmod, 'L1_attn_Wqkv': _L1_attn_in['Wqkv'], 'L1_attn_Wo': _L1_attn_in['Wo'], 'L1_ffn_w_q': _L1_ffn_in['w_q'], 'L1_ffn_keys': _L1_ffn_in['keys'], 'L1_ffn_w_down': _L1_ffn_in['w_down'], 'L1_ffn_w_up': _L1_ffn_in['w_up'], 'L1_c': _L1_c, 'L1_wmod': _L1_wmod}
    _x0 = _d['L0_attn_x']
    _d['L0_attn_x'] = jax.random.normal(jax.random.fold_in(jax.random.key(seed), 1), (2, 2048, 256), dtype=_x0.dtype)
    del _x0
    return _d

def reference(L0_attn_x, L0_attn_Wq, L0_attn_bq, L0_attn_Wk, L0_attn_bk, L0_attn_Wv, L0_attn_bv, L0_attn_gamma, L0_attn_beta, L0_ffn_router_kernel_DE, L0_ffn_kernel_gating_EDF, L0_ffn_kernel_up_EDF, L0_ffn_kernel_down_EFD, L0_c, L0_wmod, L1_attn_Wqkv, L1_attn_Wo, L1_ffn_w_q, L1_ffn_keys, L1_ffn_w_down, L1_ffn_w_up, L1_c, L1_wmod):

    def _L0_attn_ref(x, Wq, bq, Wk, bk, Wv, bv, gamma, beta):
        import jax, jax.numpy as jnp
        import numpy as np
        DIM = 256
        H = 16
        HD = DIM // H
        EPS_DENOM = 1e-06
        EPS_LN = 1e-05
        B, N, C = x.shape
        q = (x @ Wq.T + bq).reshape(B, N, H, HD)
        k = (x @ Wk.T + bk).reshape(B, N, H, HD)
        v = (x @ Wv.T + bv).reshape(B, N, H, HD)
        q = jax.nn.relu(q)
        k = jax.nn.relu(k)
        kv = jnp.einsum('bnhd,bnhp->bhdp', k, v)
        k_sum = k.sum(axis=1)
        denom = jnp.einsum('bnhd,bhd->bnh', q, k_sum)
        denom = jnp.maximum(denom, EPS_DENOM)[..., None]
        ctx = jnp.einsum('bnhd,bhdp->bnhp', q, kv)
        out = (ctx / denom).reshape(B, N, C)
        y = out + x
        mu = y.mean(axis=-1, keepdims=True)
        var = y.var(axis=-1, keepdims=True)
        return (y - mu) / jnp.sqrt(var + EPS_LN) * gamma + beta

    def _L0_ffn_ref(x, router_kernel_DE, kernel_gating_EDF, kernel_up_EDF, kernel_down_EFD):
        import jax, jax.numpy as jnp
        import numpy as np
        TOP_K = 2
        E = router_kernel_DE.shape[-1]
        x = x.astype(jnp.float32)
        logits_BSE = jnp.einsum('BSD,DE->BSE', x, router_kernel_DE)
        probs_BSE = jax.nn.softmax(logits_BSE.astype(jnp.float32), axis=-1)
        weights_BSK, indices_BSK = jax.lax.top_k(probs_BSE, TOP_K)
        norm_weights_BSK = jax.nn.softmax(weights_BSK, axis=-1)
        one_hot_BSKE = jax.nn.one_hot(indices_BSK, num_classes=E, dtype=x.dtype)
        full_weights_BSE = jnp.sum(one_hot_BSKE * norm_weights_BSK[..., None], axis=2)
        gating_BSEF = jnp.einsum('BSD,EDF->BSEF', x, kernel_gating_EDF)
        act_BSEF = jax.nn.silu(gating_BSEF)
        up_BSEF = jnp.einsum('BSD,EDF->BSEF', x, kernel_up_EDF)
        fuse_BSEF = act_BSEF * up_BSEF
        down_BSED = jnp.einsum('BSEF,EFD->BSED', fuse_BSEF, kernel_down_EFD)
        out_BSD = jnp.einsum('BSED,BSE->BSD', down_BSED, full_weights_BSE)
        return out_BSD.astype(jnp.float32)

    def _L1_attn_ref(x, Wqkv, Wo):
        import jax, jax.numpy as jnp
        import numpy as np
        B, L, D = (2, 512, 256)
        H = 16
        DH = D // H

        def rope_tables(seq_len, dim):
            inv_freq = 1.0 / 10000.0 ** (jnp.arange(0, dim, 2, dtype=jnp.float32) / dim)
            t = jnp.arange(seq_len, dtype=jnp.float32)
            freqs = jnp.outer(t, inv_freq)
            emb = jnp.concatenate([freqs, freqs], -1)
            return (jnp.cos(emb), jnp.sin(emb))

        def rotate_half(x):
            x1, x2 = (x[..., :x.shape[-1] // 2], x[..., x.shape[-1] // 2:])
            return jnp.concatenate([-x2, x1], axis=-1)
        b, l, d = x.shape
        qkv = (x @ Wqkv).reshape(b, l, 3, H, DH)
        q, k, v = (qkv[:, :, 0], qkv[:, :, 1], qkv[:, :, 2])
        cos, sin = rope_tables(l, DH)
        cos = cos[:, None, :]
        sin = sin[:, None, :]
        q = q * cos + rotate_half(q) * sin
        k = k * cos + rotate_half(k) * sin
        scale = DH ** (-0.5)
        scores = jnp.einsum('bqhd,bkhd->bhqk', q, k) * scale
        attn = jax.nn.softmax(scores, axis=-1)
        out = jnp.einsum('bhqk,bkhd->bqhd', attn, v)
        out = out.reshape(b, l, d)
        return out @ Wo

    def _L1_ffn_ref(x, w_q, keys, w_down, w_up):
        import jax, jax.numpy as jnp
        import numpy as np
        DIM = 256
        HEADS = 8
        NUM_EXPERTS = 16384
        NUM_KEYS = 64
        DIM_KEY = 128
        PK_TOPK = 16
        FINAL_TOPK = 1
        BATCH, SEQ = (4, 512)
        b, n, d = x.shape
        q = (x @ w_q).reshape(b, n, 2, HEADS, DIM_KEY).transpose(2, 0, 1, 3, 4)
        sim = jnp.einsum('pbnhd,hkpd->pbnhk', q, keys)
        vals, idx = jax.lax.top_k(sim, PK_TOPK)
        sx, sy = (vals[0], vals[1])
        ix, iy = (idx[0], idx[1])
        all_scores = (sx[..., :, None] + sy[..., None, :]).reshape(b, n, HEADS, PK_TOPK * PK_TOPK)
        all_indices = (ix[..., :, None] * NUM_KEYS + iy[..., None, :]).reshape(b, n, HEADS, PK_TOPK * PK_TOPK)
        scores, pk_indices = jax.lax.top_k(all_scores, FINAL_TOPK)
        indices = jnp.take_along_axis(all_indices, pk_indices, axis=-1)
        weights_down = w_down[indices]
        weights_up = w_up[indices]
        h = jnp.einsum('bnd,bnhkd->bnhk', x, weights_down)
        h = jax.nn.gelu(h, approximate=False)
        h = h * jax.nn.relu(scores)
        return jnp.einsum('bnhk,bnhkd->bnd', h, weights_up)
    x = L0_attn_x
    mod = (_silu(L0_c) @ L0_wmod).reshape(L0_c.shape[0], 6, 1, -1)
    sa, ca, ga, sb, cb, gb = (mod[:, 0], mod[:, 1], mod[:, 2], mod[:, 3], mod[:, 4], mod[:, 5])
    ga = (2 * (ga >= 0) - 1) * jnp.maximum(jnp.abs(ga), 0.25)
    gb = (2 * (gb >= 0) - 1) * jnp.maximum(jnp.abs(gb), 0.25)
    h = _layernorm(x, axis=-1) * (1 + ca) + sa
    x = x + ga * _L0_attn_ref(h, L0_attn_Wq, L0_attn_bq, L0_attn_Wk, L0_attn_bk, L0_attn_Wv, L0_attn_bv, L0_attn_gamma, L0_attn_beta)
    h = _layernorm(x, axis=-1) * (1 + cb) + sb
    x = x + gb * _L0_ffn_ref(h, L0_ffn_router_kernel_DE, L0_ffn_kernel_gating_EDF, L0_ffn_kernel_up_EDF, L0_ffn_kernel_down_EFD)
    mod = (_silu(L1_c) @ L1_wmod).reshape(L1_c.shape[0], 6, 1, -1)
    sa, ca, ga, sb, cb, gb = (mod[:, 0], mod[:, 1], mod[:, 2], mod[:, 3], mod[:, 4], mod[:, 5])
    ga = (2 * (ga >= 0) - 1) * jnp.maximum(jnp.abs(ga), 0.25)
    gb = (2 * (gb >= 0) - 1) * jnp.maximum(jnp.abs(gb), 0.25)
    h = _layernorm(x, axis=-1) * (1 + ca) + sa
    x = x + ga * _L1_attn_ref(h, L1_attn_Wqkv, L1_attn_Wo)
    h = _layernorm(x, axis=-1) * (1 + cb) + sb
    x = x + gb * _L1_ffn_ref(h, L1_ffn_w_q, L1_ffn_keys, L1_ffn_w_down, L1_ffn_w_up)
    return x

_drawn_inputs = setup_inputs


def setup_inputs(seed=0):
    import zlib

    import numpy as np

    out = dict(_drawn_inputs(seed))
    spreads = {'L0_attn_bq': (0.0, 0.8),
     'L0_attn_bk': (0.0, 0.8),
     'L0_attn_bv': (0.0, 0.319),
     'L0_attn_gamma': (1.0, 0.2),
     'L0_attn_beta': (0.0, 0.355)}
    factors = {'L0_attn_Wq': 7.16,
     'L0_attn_Wk': 5.721,
     'L0_attn_Wv': 5.102,
     'L0_ffn_router_kernel_DE': 8.0,
     'L0_ffn_kernel_gating_EDF': 8.0,
     'L0_ffn_kernel_up_EDF': 8.0,
     'L0_ffn_kernel_down_EFD': 8.0,
     'L1_attn_Wqkv': 3.843,
     'L1_attn_Wo': 3.767,
     'L1_ffn_w_q': 8.0,
     'L1_ffn_keys': 8.0,
     'L1_ffn_w_down': 8.0,
     'L1_ffn_w_up': 8.0,
     'L1_c': 3.772,
     'L1_wmod': 4.12}
    for name, (base, spread) in spreads.items():
        noise = np.random.default_rng([zlib.crc32(name.encode()), seed]).standard_normal(out[name].shape)
        drawn = base * np.exp(spread * noise) if base else spread * noise
        out[name] = jnp.asarray(drawn.astype(out[name].dtype))
    for name, factor in factors.items():
        out[name] = (out[name] * factor).astype(out[name].dtype)
    return out
```

```python
from contextlib import ExitStack

import numpy as np

import concourse.bass as bass
from concourse import mybir

F32 = mybir.dt.float32
BF16 = mybir.dt.bfloat16
I32 = mybir.dt.int32
U32 = mybir.dt.uint32
ALU = mybir.AluOpType
ACT = mybir.ActivationFunctionType
AX = mybir.AxisListType

P = 128
B, S, D = 2, 2048, 256
T = B * S
NT = T // P
G = 4
GT = G * P
NG = NT // G
GB = NG // B
DC = D // P
H, DH = 16, 16
HC = P // DH
E, F = 8, 512
FC = F // P
LN_EPS = 1e-5
DENOM_EPS = 1e-6
GATE_MIN = 0.25
SA, CA, GA, SB, CB, GBI = range(6)


class Order:

    def __init__(self, eng, sem):
        self.eng, self.sem, self.base, self.n = eng, sem, 0, 0

    def mark(self, instruction):
        self.n += 1
        return instruction.then_inc(self.sem, 1)

    def settle(self):
        self.eng.wait_ge(self.sem, self.base + self.n)

    def settle_alone(self):
        wait_alone(self.eng, self.sem, self.base + self.n)

    def turn(self, i, start, per):
        self.base, self.n = i * per + start, 0


def wait_alone(eng, sem, value):
    r = eng.to_reg(value)
    eng.wait_ge(sem, 1)
    eng.wait_ge(sem, r)


class Kernel:
    pass


def setup(nc, ctx, io):
    k = Kernel()
    k.nc, k.ctx, k.io = nc, ctx, io

    def sb(name, shape, dt=F32):
        return ctx.enter_context(nc.sbuf_tensor(name, shape, dt))

    k.x = sb("x_res", [P, NT, D])
    k.mods = sb("mods", [P, B, 6, D])
    k.ident = sb("ident", [P, P])
    k.identb = sb("identb", [P, P], BF16)
    k.eps = sb("eps", [P, 1])
    k.modrow_dram = [nc.dram_tensor(f"modrow_dram{l}", [B, 6, D], F32, kind="Internal").ap() for l in range(2)]
    k.h_dram = nc.dram_tensor("h_dram", [T, D], F32, kind="Internal").ap()
    k.qT_dram = nc.dram_tensor("qT_dram", [DC, P, T], F32, kind="Internal").ap()
    return k


def stage_modulation(k):
    nc, io = k.nc, k.io
    with ExitStack() as ctx:
        def sb(name, shape, dt=F32):
            return ctx.enter_context(nc.sbuf_tensor(name, shape, dt))

        def sem(name):
            return k.ctx.enter_context(nc.semaphore(name))

        cT = sb("cT", [P, 2, DC, B])
        scT = sb("scT", [P, 2, DC, B])
        wmod = sb("wmod", [P, 2, DC, 6 * D])
        row = sb("modrow", [B, 2, 6, D])
        sign = sb("modsign", [B, 2, 2, D])
        neg = sb("modneg", [B, 2, 2, D])
        ps = ctx.enter_context(nc.psum_tensor("mod_ps", [P, 6, 512], F32))
        c_in, w_in, x_in, id_in = sem("m_c_in"), sem("m_w_in"), sem("m_x_in"), sem("m_id_in")
        silu_done, mod_done, evac_done = sem("m_silu"), sem("m_mod"), sem("m_evac")
        dve_steps, row_ready, row_out, bc_in = sem("m_dve"), sem("m_row"), sem("m_rowout"), sem("m_bc")
        with nc.Block() as block:
            @block.sync
            def _(sp):
                for l in range(2):
                    for c in range(DC):
                        sp.dma_start(cT[:, l, c, :], io[f"L{l}_cT"][c * P:(c + 1) * P, :]).then_inc(c_in, 16)
                for l in range(2):
                    sp.dma_start(wmod[:, l, :, :], io[f"L{l}_wmod"].rearrange("(c p) n -> p c n", p=P)).then_inc(w_in, 16)
                sp.dma_start(k.ident[:], io["ident"]).then_inc(id_in, 16)
                sp.dma_start(k.x[:], io["L0_attn_x"].rearrange("b (t p) d -> p (b t) d", p=P)).then_inc(x_in, 16)
                for l in range(2):
                    sp.wait_ge(row_ready, l + 1)
                    sp.dma_start(k.modrow_dram[l], row[:, l, :, :]).then_inc(row_out, 16)
                sp.wait_ge(row_out, 32)
                sp.dma_start(k.mods[:].rearrange("p b m d -> p (b m d)"),
                             k.modrow_dram[0].rearrange("b m d -> (b m d)").partition_broadcast(P)).then_inc(bc_in, 16)
                sp.wait_ge(bc_in, 16)
                sp.wait_ge(x_in, 16)

            @block.scalar
            def _(act):
                act.wait_ge(c_in, 64)
                nc.scalar.activation(scT[:], cT[:], ACT.Silu).then_inc(silu_done, 1)

            @block.tensor
            def _(pe):
                pe.wait_ge(silu_done, 1)
                pe.wait_ge(w_in, 32)
                for l in range(2):
                    for n in range(3):
                        for c in range(DC):
                            mm = nc.tensor.matmul(ps[0:B, 3 * l + n, :], scT[:, l, c, :], wmod[:, l, c, n * 512:(n + 1) * 512],
                                                  start=(c == 0), stop=(c == DC - 1))
                    mm.then_inc(mod_done, 1)

            @block.vector
            def _(dve):
                o = Order(dve, dve_steps)
                o.mark(nc.vector.memset(k.eps[:], LN_EPS))
                dve.wait_ge(id_in, 16)
                o.mark(nc.vector.tensor_copy(k.identb[:], k.ident[:]))
                for l in range(2):
                    dve.wait_ge(mod_done, l + 1)
                    o.mark(nc.vector.tensor_copy(row[:, l, :, :].rearrange("b m d -> b (m d)"),
                                                 ps[0:B, 3 * l:3 * l + 3, :].rearrange("b n f -> b (n f)")))
                    o.settle()
                    scales = row[:, l, CA:CB + 1:3, :]
                    gates = row[:, l, GA:GBI + 1:3, :]
                    o.mark(nc.vector.tensor_scalar_add(scales, scales, 1.0))
                    o.mark(nc.vector.tensor_scalar(sign[:, l], gates, 0.0, 2.0, ALU.is_ge, ALU.mult))
                    o.mark(nc.vector.scalar_tensor_tensor(neg[:, l], gates, -1.0, gates, ALU.mult, ALU.max))
                    o.settle()
                    o.mark(nc.vector.tensor_scalar_max(neg[:, l], neg[:, l], GATE_MIN))
                    o.settle()
                    nc.vector.scalar_tensor_tensor(gates, sign[:, l], 1.0, neg[:, l], ALU.subtract, ALU.mult).then_inc(row_ready, 1)


def stage_linear_attention_sums(k):
    nc, io = k.nc, k.io
    with ExitStack() as ctx:
        def sb(name, shape, dt=F32):
            return ctx.enter_context(nc.sbuf_tensor(name, shape, dt))

        def psum(name, shape):
            return ctx.enter_context(nc.psum_tensor(name, shape, F32))

        def sem(name):
            return k.ctx.enter_context(nc.semaphore(name))

        KV = P + 1
        wq = sb("wq", [P, DC, D])
        wkv = sb("wkv", [P, DC, 2 * D])
        bq = sb("bq", [P, DC])
        bkv = sb("bkv", [P, 2 * D])
        stats = sb("a_stats", [P, G, 6])
        mv = sb("a_mv", [P, G, 2])
        std = sb("a_std", [P, G])
        xn = sb("a_xn", [P, G, D])
        h = sb("a_h", [P, G, D])
        hT = sb("a_hT", [P, DC, GT])
        qT = sb("a_qT", [P, DC, GT])
        kv = sb("a_kv", [P, 2, 2 * D + 1])
        hT_ps = psum("hT_ps", [P, DC, 512])
        q_ps = psum("q_ps", [P, DC, 512])
        kv_ps = psum("kv_ps", [P, 2, 512])
        sum_ps = psum("sum_ps", [P, DC, 512])

        w_in, const_ready = sem("a_w_in"), sem("a_const")
        dve_steps, stats_ready, std_ready, h_ready = sem("a_dve"), sem("a_stats"), sem("a_std"), sem("a_h")
        hT_done, hT_c0, hT_c1 = sem("a_hT"), sem("a_hTc0"), sem("a_hTc1")
        q_done, q_c0, q_c1 = sem("a_q"), sem("a_qc0"), sem("a_qc1")
        kv_done, kv_added, kv_ready = sem("a_kvd"), sem("a_kva"), sem("a_kvr")
        sums_done, sums_read = sem("a_sd"), sem("a_sr")
        h_out, q_out = sem("a_ho"), sem("a_qo")
        W_IN = 16 * (3 + DC + 2)

        with nc.Block() as block:
            @block.sync
            def _(sp):
                sp.dma_start(wq[:], io["L0_WqT"].rearrange("(c p) n -> p c n", p=P)).then_inc(w_in, 16)
                sp.dma_start(wkv[:, :, 0:D], io["L0_WkT"].rearrange("(c p) n -> p c n", p=P)).then_inc(w_in, 16)
                sp.dma_start(wkv[:, :, D:2 * D], io["L0_WvT"].rearrange("(c p) n -> p c n", p=P)).then_inc(w_in, 16)
                for c in range(DC):
                    sp.dma_start(bq[:, c:c + 1], io["L0_attn_bq"][c * P:(c + 1) * P].rearrange("(p o) -> p o", o=1)).then_inc(w_in, 16)
                sp.dma_start(bkv[:, 0:D], io["L0_attn_bk"].partition_broadcast(P)).then_inc(w_in, 16)
                sp.dma_start(bkv[:, D:2 * D], io["L0_attn_bv"].partition_broadcast(P)).then_inc(w_in, 16)
                sp.nop().then_inc(h_out, 16)
                sp.nop().then_inc(q_out, 16)
                with sp.Fori(0, NG) as g:
                    sp.wait_ge(h_ready, g + 1)
                    sp.dma_start(k.h_dram[bass.ts(g, GT), :].rearrange("(s p) d -> p s d", p=P), h[:]).then_inc(h_out, 16)
                    wait_alone(sp, q_c0, g + 1)
                    wait_alone(sp, q_c1, g + 1)
                    sp.dma_start(k.qT_dram[:, :, bass.ts(g, GT)].rearrange("c p n -> p c n"), qT[:]).then_inc(q_out, 16)
                sp.wait_ge(h_out, 16 * (NG + 1))
                sp.wait_ge(q_out, 16 * (NG + 1))

            @block.vector
            def _(dve):
                o = Order(dve, dve_steps)
                nc.vector.memset(k.kvsum[:], 0.0).then_inc(const_ready, 1)
                nc.vector.memset(kv[:, :, 2 * D:], 1.0).then_inc(const_ready, 1)
                dve.wait_ge(w_in, W_IN)
                dve.wait_ge(const_ready, 2)
                LN_STEPS = G + 1 + G + 1

                def normalise(g):
                    for s in range(G):
                        o.mark(nc.vector.bn_stats(stats[:, s, :], k.x[:, bass.ds(g * G + s, 1), :]))
                    o.settle_alone()
                    for s in range(G):
                        nc.vector.bn_aggr(mv[:, s, :], stats[:, s, :]).then_inc(stats_ready, 1)
                    dve.wait_ge(std_ready, g + 1)
                    o.mark(nc.vector.reciprocal(std[:], std[:]))
                    o.settle()
                    for s in range(G):
                        o.mark(nc.vector.tensor_scalar(xn[:, s, :], k.x[:, bass.ds(g * G + s, 1), :], mv[:, s, 0:1],
                                                       std[:, s:s + 1], ALU.subtract, ALU.mult))
                    o.settle()
                    scale = k.mods[:, bass.ds(g // GB, 1), CA, :].to_broadcast([P, G, D])
                    o.mark(nc.vector.tensor_tensor(xn[:], xn[:], scale, ALU.mult))

                def shift(g):
                    o.settle()
                    dve.wait_ge(h_out, 16 * (g + 1))
                    by = k.mods[:, bass.ds(g // GB, 1), SA, :].to_broadcast([P, G, D])
                    nc.vector.tensor_tensor(h[:], xn[:], by, ALU.add).then_inc(h_ready, 1)

                def group(g, ahead):
                    dve.wait_ge(hT_done, g + 1)
                    nc.vector.tensor_copy(hT[:, 0, :], hT_ps[:, 0, :]).then_inc(hT_c0, 1)
                    dve.wait_ge(q_done, g + 1)
                    dve.wait_ge(q_out, 16 * (g + 1))
                    nc.vector.tensor_scalar(qT[:, 0, :], q_ps[:, 0, :], bq[:, 0:1], 0.0, ALU.add, ALU.max).then_inc(q_c0, 1)
                    for s in range(G):
                        dve.wait_ge(kv_done, g * G + s + 1)
                        if s >= 2:
                            dve.wait_ge(sums_done, g * G + s - 1)
                        nc.vector.tensor_tensor(kv[:, s % 2, 0:2 * D], kv_ps[:, s % 2, :], bkv[:], ALU.add).then_inc(kv_added, 1)
                        if s == 1 and ahead:
                            shift(g + 1)
                        dve.wait_ge(kv_added, g * G + s + 1)
                        nc.vector.tensor_scalar_max(kv[:, s % 2, 0:D], kv[:, s % 2, 0:D], 0.0).then_inc(kv_ready, 1)
                    dve.wait_ge(sums_done, (g + 1) * G)
                    acc = k.kvsum[:, bass.ds(g // GB, 1), :, :]
                    nc.vector.tensor_tensor(acc, sum_ps[:, :, 0:KV], acc, ALU.add).then_inc(sums_read, 1)
                    dve.wait_ge(sums_read, g + 1)

                normalise(0)
                shift(0)
                with dve.Fori(0, NG - 1) as g:
                    o.turn(g, LN_STEPS, LN_STEPS)
                    normalise(g + 1)
                    group(g, True)
                    assert o.n == LN_STEPS
                group(NG - 1, False)

            @block.scalar
            def _(act):
                act.wait_ge(w_in, W_IN)

                def deviation(g):
                    act.wait_ge(stats_ready, (g + 1) * G)
                    nc.scalar.activation(std[:], mv[:, :, 1], ACT.Sqrt, bias=k.eps[:, 0:1]).then_inc(std_ready, 1)

                def group(g):
                    act.wait_ge(hT_done, g + 1)
                    nc.scalar.copy(hT[:, 1, :], hT_ps[:, 1, :]).then_inc(hT_c1, 1)
                    act.wait_ge(q_done, g + 1)
                    act.wait_ge(q_out, 16 * (g + 1))
                    nc.scalar.activation(qT[:, 1, :], q_ps[:, 1, :], ACT.Relu, bias=bq[:, 1:2]).then_inc(q_c1, 1)

                deviation(0)
                with act.Fori(0, NG - 1) as g:
                    deviation(g + 1)
                    group(g)
                group(NG - 1)

            @block.tensor
            def _(pe):
                pe.wait_ge(w_in, W_IN)
                with pe.Fori(0, NG) as g:
                    pe.wait_ge(h_ready, g + 1)
                    for c in range(DC):
                        for s in range(G):
                            mm = nc.tensor.transpose(hT_ps[:, c, s * P:(s + 1) * P], h[:, s, c * P:(c + 1) * P], k.ident[:])
                    mm.then_inc(hT_done, 1)
                    pe.wait_ge(hT_c0, g + 1)
                    pe.wait_ge(hT_c1, g + 1)
                    for m in range(DC):
                        for c in range(DC):
                            mm = nc.tensor.matmul(q_ps[:, m, :], wq[:, c, m * P:(m + 1) * P], hT[:, c, :],
                                                  start=(c == 0), stop=(c == DC - 1))
                    mm.then_inc(q_done, 1)

                    def sums(s):
                        pe.wait_ge(kv_ready, g * G + s + 1)
                        for c in range(DC):
                            for lo, hi, col in ((0, P, D + c * P), (P, KV, 2 * D)):
                                mm = nc.tensor.matmul(sum_ps[:, c, lo:hi], kv[:, s % 2, c * P:(c + 1) * P],
                                                      kv[:, s % 2, col:col + hi - lo], start=(s == 0 and lo == 0),
                                                      stop=(s == G - 1), skip_group_check=True)
                        mm.then_inc(sums_done, 1)

                    for s in range(G):
                        if s >= 2:
                            pe.wait_ge(kv_added, g * G + s - 1)
                        for c in range(DC):
                            mm = nc.tensor.matmul(kv_ps[:, s % 2, :], hT[:, c, s * P:(s + 1) * P], wkv[:, c, :],
                                                  start=(c == 0), stop=(c == DC - 1))
                        mm.then_inc(kv_done, 1)
                        if s >= 1:
                            sums(s - 1)
                    sums(G - 1)
                    pe.wait_ge(sums_read, g + 1)


def scratch(k, ctx):
    nc = k.nc

    def sb(name, shape, dt=F32):
        return ctx.enter_context(nc.sbuf_tensor(name, shape, dt))

    def psum(name, shape, dt=F32):
        return ctx.enter_context(nc.psum_tensor(name, shape, dt))

    def sem(name):
        return k.ctx.enter_context(nc.semaphore(name))

    return sb, psum, sem


def stage_linear_attention_apply(k):
    nc, io = k.nc, k.io
    with ExitStack() as ctx:
        sb, psum, sem = scratch(k, ctx)
        mask = sb("b_mask", [P, P + HC])
        kvd = sb("b_kvd", [P, B, DC, P + HC])
        router = sb("b_router", [P, DC, E])
        gamma = sb("b_gamma", [P, B, D])
        beta = sb("b_beta", [P, B, D])
        h = sb("b_h", [P, G, D])
        qT = sb("b_qT", [P, DC, GT])
        rden = sb("b_rden", [P, G, H])
        y = sb("b_y", [P, G, D])
        stats = sb("b_stats", [P, G, 6])
        mv = sb("b_mv", [P, G, 2])
        std = sb("b_std", [P, G])
        xn = sb("b_xn", [P, G, D])
        h2 = sb("b_h2", [P, G, D])
        h2T = sb("b_h2T", [P, DC, GT])
        zeros = sb("b_zeros", [P, D])
        ctx_ps = psum("ctx_ps", [P, G, 512])
        hT_ps = psum("b_hT_ps", [P, DC, 512])
        lg_ps = psum("lg_ps", [P, 512])

        w_in, z_ready, z_out = sem("b_w_in"), sem("b_z"), sem("b_zo")
        dve_steps, kvd_ready, beta_ready, x_based = sem("b_dve"), sem("b_kvd"), sem("b_beta"), sem("b_xb")
        h_in, q_in, ctx_done, ctx_read, h_used = sem("b_hin"), sem("b_qin"), sem("b_ctx"), sem("b_ctxr"), sem("b_hu")
        stats_ready, std_ready, h2_ready, h2_out = sem("b_stats"), sem("b_std"), sem("b_h2"), sem("b_h2o")
        hT_done, hT_c0, hT_c1, lg_done, lg_read = sem("b_hT"), sem("b_c0"), sem("b_c1"), sem("b_lg"), sem("b_lgr")

        with nc.Block() as block:
            @block.sync
            def _(sp):
                sp.dma_start(mask[:], io["head_mask"]).then_inc(w_in, 16)
                sp.dma_start(router[:], io["L0_router"].rearrange("(c p) n -> p c n", p=P)).then_inc(w_in, 16)
                for b in range(B):
                    sp.dma_start(gamma[:, b, :], io["L0_attn_gamma"].partition_broadcast(P)).then_inc(w_in, 16)
                    sp.dma_start(beta[:, b, :], io["L0_attn_beta"].partition_broadcast(P)).then_inc(w_in, 16)
                sp.wait_ge(z_ready, 1)
                sp.dma_start(k.xs_dram.rearrange("(j p) d -> p j d", p=P),
                             zeros[:].unsqueeze(1).to_broadcast([P, k.XS_TILES, D])).then_inc(z_out, 16)
                sp.nop().then_inc(h2_out, 16)
                with sp.Fori(0, NG) as g:
                    sp.wait_ge(h_used, g + 1)
                    sp.dma_start(h[:], k.h_dram[bass.ts(g, GT), :].rearrange("(s p) d -> p s d", p=P)).then_inc(h_in, 16)
                    wait_alone(sp, ctx_done, g + 1)
                    sp.dma_start(qT[:], k.qT_dram[:, :, bass.ts(g, GT)].rearrange("c p n -> p c n")).then_inc(q_in, 16)
                    sp.wait_ge(h2_ready, g + 1)
                    sp.dma_start(k.h2_dram[bass.ts(g, GT), :].rearrange("(s p) d -> p s d", p=P), h2[:]).then_inc(h2_out, 16)
                sp.wait_ge(h2_out, 16 * (NG + 1))
                sp.wait_ge(z_out, 16)

            @block.gpsimd
            def _(pool):
                nc.gpsimd.memset(zeros[:], 0.0).then_inc(z_ready, 1)
                pool.wait_ge(beta_ready, 1)
                with pool.Fori(0, NG) as g:
                    by = beta[:, bass.ds(g // GB, 1), :].to_broadcast([P, G, D])
                    xg = k.x[:, bass.ds(g * G, G), :]
                    nc.gpsimd.tensor_tensor(xg, xg, by, ALU.add).then_inc(x_based, 1)

            @block.vector
            def _(dve):
                o = Order(dve, dve_steps)
                dve.wait_ge(w_in, 16 * (2 + 2 * B))
                for b in range(B):
                    for c in range(DC):
                        nc.vector.tensor_tensor(kvd[:, b, c, 0:P], k.kvsum[:, b, c, 0:P], mask[:, 0:P], ALU.mult).then_inc(kvd_ready, 1)
                        nc.vector.tensor_scalar_mul(kvd[:, b, c, P:], mask[:, P:], k.kvsum[:, b, c, P:P + 1]).then_inc(kvd_ready, 1)
                    o.mark(nc.vector.tensor_tensor(gamma[:, b, :], gamma[:, b, :], k.mods[:, b, GA, :], ALU.mult))
                nc.vector.tensor_tensor(beta[:], beta[:], k.mods[:, :, GA, :], ALU.mult).then_inc(beta_ready, 1)
                START, TURN = B, 5 + 2 * (G + 1 + G)

                def normalise(src, turn):
                    for s in range(G):
                        o.mark(nc.vector.bn_stats(stats[:, s, :], src(s)))
                    o.settle_alone()
                    for s in range(G):
                        nc.vector.bn_aggr(mv[:, s, :], stats[:, s, :]).then_inc(stats_ready, 1)
                    dve.wait_ge(std_ready, turn + 1)
                    o.mark(nc.vector.reciprocal(std[:], std[:]))
                    o.settle()
                    for s in range(G):
                        o.mark(nc.vector.tensor_scalar(xn[:, s, :], src(s), mv[:, s, 0:1], std[:, s:s + 1], ALU.subtract, ALU.mult))
                    o.settle()

                with dve.Fori(0, NG) as g:
                    o.turn(g, START, TURN)
                    dve.wait_ge(ctx_done, g + 2)
                    den = ctx_ps[:, :, D:D + H]
                    o.mark(nc.vector.tensor_scalar_max(rden[:], den, DENOM_EPS))
                    o.settle()
                    o.mark(nc.vector.reciprocal(rden[:], rden[:]))
                    o.settle()
                    nc.vector.tensor_tensor(y[:].rearrange("p s (h d) -> p s h d", d=DH),
                                            ctx_ps[:, :, 0:D].rearrange("p s (h d) -> p s h d", d=DH),
                                            rden[:].unsqueeze(3).to_broadcast([P, G, H, DH]), ALU.mult).then_inc(ctx_read, 1)
                    dve.wait_ge(ctx_read, g + 1)
                    dve.wait_ge(h_in, 16 * (g + 1))
                    nc.vector.tensor_tensor(y[:], y[:], h[:], ALU.add).then_inc(h_used, 1)
                    dve.wait_ge(h_used, g + 2)
                    normalise(lambda s: y[:, s, :], 2 * g)
                    by = gamma[:, bass.ds(g // GB, 1), :].to_broadcast([P, G, D])
                    xg = k.x[:, bass.ds(g * G, G), :]
                    o.mark(nc.vector.tensor_tensor(xn[:], xn[:], by, ALU.mult))
                    o.settle()
                    dve.wait_ge(x_based, g + 1)
                    o.mark(nc.vector.tensor_tensor(xg, xg, xn[:], ALU.add))
                    o.settle_alone()
                    normalise(lambda s: k.x[:, bass.ds(g * G + s, 1), :], 2 * g + 1)
                    o.mark(nc.vector.tensor_tensor(xn[:], xn[:], k.mods[:, bass.ds(g // GB, 1), CB, :].to_broadcast([P, G, D]), ALU.mult))
                    o.settle()
                    dve.wait_ge(h2_out, 16 * (g + 1))
                    nc.vector.tensor_tensor(h2[:], xn[:], k.mods[:, bass.ds(g // GB, 1), SB, :].to_broadcast([P, G, D]), ALU.add).then_inc(h2_ready, 1)
                    dve.wait_ge(hT_done, g + 1)
                    nc.vector.tensor_copy(h2T[:, 0, :], hT_ps[:, 0, :]).then_inc(hT_c0, 1)
                    dve.wait_ge(lg_done, g + 1)
                    nc.vector.tensor_copy(k.logits[:, bass.ds(g * G, G), :], lg_ps[:, 0:G * E].rearrange("p (s e) -> p s e", e=E)).then_inc(lg_read, 1)
                    assert o.n == TURN, (o.n, TURN)

            @block.scalar
            def _(act):
                with act.Fori(0, NG) as g:
                    for turn in range(2):
                        act.wait_ge(stats_ready, (2 * g + turn + 1) * G)
                        nc.scalar.activation(std[:], mv[:, :, 1], ACT.Sqrt, bias=k.eps[:, 0:1]).then_inc(std_ready, 1)
                    act.wait_ge(hT_done, g + 1)
                    nc.scalar.copy(h2T[:, 1, :], hT_ps[:, 1, :]).then_inc(hT_c1, 1)

            @block.tensor
            def _(pe):
                pe.wait_ge(w_in, 16 * (2 + 2 * B))
                pe.wait_ge(kvd_ready, B * DC * 2)
                pe.nop().then_inc(ctx_done, 1)
                pe.nop().then_inc(h_used, 1)
                with pe.Fori(0, NG) as g:
                    pe.wait_ge(q_in, 16 * (g + 1))
                    pe.wait_ge(h_used, g + 1)
                    for s in range(G):
                        for c in range(DC):
                            q = qT[:, c, s * P:(s + 1) * P]
                            nc.tensor.matmul(ctx_ps[:, s, c * P:(c + 1) * P], q, kvd[:, bass.ds(g // GB, 1), c, 0:P],
                                             start=True, stop=True, skip_group_check=True)
                            mm = nc.tensor.matmul(ctx_ps[:, s, D + c * HC:D + (c + 1) * HC], q, kvd[:, bass.ds(g // GB, 1), c, P:],
                                                  start=True, stop=True, skip_group_check=True)
                    mm.then_inc(ctx_done, 1)
                    pe.wait_ge(h2_ready, g + 1)
                    for c in range(DC):
                        for s in range(G):
                            mm = nc.tensor.transpose(hT_ps[:, c, s * P:(s + 1) * P], h2[:, s, c * P:(c + 1) * P], k.ident[:])
                    mm.then_inc(hT_done, 1)
                    pe.wait_ge(hT_c0, g + 1)
                    pe.wait_ge(hT_c1, g + 1)
                    for s in range(G):
                        for c in range(DC):
                            mm = nc.tensor.matmul(lg_ps[:, s * E:(s + 1) * E], h2T[:, c, s * P:(s + 1) * P], router[:, c, :],
                                                  start=(c == 0), stop=(c == DC - 1), skip_group_check=True)
                    mm.then_inc(lg_done, 1)
                    pe.wait_ge(lg_read, g + 1)


def stage_route(k):
    nc, io = k.nc, k.io
    with ExitStack() as ctx:
        sb, psum, sem = scratch(k, ctx)
        tri = sb("r_tri", [P, P])
        ones = sb("r_ones", [P, P])
        rank = sb("r_rank", [P, E])
        start = sb("r_start", [1, k.XS_TILES])
        m = sb("r_m", [P, 4, NT])
        prob = sb("r_prob", [P, NT, E])
        key = sb("r_key", [P, NT, E])
        hot = sb("r_hot", [P, 2, NT, E])
        both = sb("r_both", [P, NT, E])
        run = sb("r_run", [P, 2, NT, E])
        cnt = sb("r_cnt", [P, 4, E])
        cnti = sb("r_cnti", [P, E], I32)
        slotf = sb("r_slotf", [P, NT, 2])
        cmp = sb("r_cmp", [1, k.XS_TILES, E])
        eidf = sb("r_eidf", [1, k.XS_TILES])
        h2 = sb("r_h2", [P, 2, G, D])
        sl = sb("r_sl", [P, 2, G, 2], I32)
        cnt_ps = psum("cnt_ps", [P, 2, NT * E])
        w_in, steps, exped, both_ready, cnt_done = sem("r_w"), sem("r_steps"), sem("r_exp"), sem("r_both"), sem("r_cnt")
        slots_ready = sem("r_slots")
        h2_in = [sem(f"r_in{u}") for u in range(2)]
        sl_ready = sem("r_sl")
        scattered = [sem(f"r_sc{u}") for u in range(2)]

        with nc.Block() as block:
            @block.sync
            def _(sp):
                for t, n in ((tri, "tri"), (ones, "ones"), (rank, "rank"), (start, "tile_start")):
                    sp.dma_start(t[:], io[n]).then_inc(w_in, 16)
                with sp.Fori(0, NG // 2) as i:
                    for u in range(2):
                        sp.wait_ge(sl_ready, i * 2 + u + 1)
                        sp.dma_start(h2[:, u], k.h2_dram[bass.ts(i * 2 + u, GT), :].rearrange("(s p) d -> p s d", p=P)).then_inc(h2_in[u], 16)
                for u in range(2):
                    sp.wait_ge(h2_in[u], 16 * NG // 2)
                sp.wait_ge(k.w_moe_in, 48)

            @block.gpsimd
            def _(pool):
                with pool.Fori(0, NG // 2) as i:
                    for u in range(2):
                        pool.wait_ge(h2_in[u], 16 * (i + 1))
                        wait_alone(pool, sl_ready, i * 2 + u + 1)
                        for s in range(G):
                            for c in range(2):
                                nc.gpsimd.indirect_dma_start(
                                    k.xs_dram, bass.IndirectOffsetOnAxis(ap=sl[:, u, s, c:c + 1], axis=0), h2[:, u, s, :], None,
                                ).then_inc(scattered[u], 16)
                for u in range(2):
                    pool.wait_ge(scattered[u], 16 * 2 * G * NG // 2)

            @block.scalar
            def _(act):
                for n, t in (("L0_gate", k.wg), ("L0_up", k.wu), ("L0_down", k.wd)):
                    act.dma_start(t[:].rearrange("p e c f -> p (e c) f"), io[n].rearrange("e (c p) f -> p (e c) f", p=P)).then_inc(k.w_moe_in, 16)
                act.wait_ge(exped, 1)
                nc.scalar.activation(prob[:], prob[:], ACT.Exp).then_inc(exped, 1)
                act.wait_ge(exped, 3)
                nc.scalar.activation(k.wts[:, 1, :], m[:, 3, :], ACT.Exp).then_inc(exped, 1)

            @block.tensor
            def _(pe):
                pe.wait_ge(w_in, 64)
                pe.wait_ge(both_ready, 1)
                flat = both[:].rearrange("p t e -> p (t e)")
                nc.tensor.matmul(cnt_ps[:, 0, :], tri[:], flat, start=True, stop=True, skip_group_check=True)
                nc.tensor.matmul(cnt_ps[:, 1, :], ones[:], flat, start=True, stop=True, skip_group_check=True).then_inc(cnt_done, 1)

            @block.vector
            def _(dve):
                o = Order(dve, steps)

                def step(instruction):
                    o.mark(instruction)
                    o.settle()

                V = nc.vector
                wide = [P, NT, E]
                dve.wait_ge(w_in, 64)
                step(V.reduce_max(m[:, 0, :], k.logits[:], AX.X))
                V.tensor_tensor(prob[:], k.logits[:], m[:, 0, :].unsqueeze(2).to_broadcast(wide), ALU.subtract).then_inc(exped, 1)
                dve.wait_ge(exped, 2)
                step(V.reduce_sum(m[:, 1, :], prob[:], AX.X))
                step(V.reciprocal(m[:, 1, :], m[:, 1, :]))
                step(V.tensor_tensor(prob[:], prob[:], m[:, 1, :].unsqueeze(2).to_broadcast(wide), ALU.mult))
                for c in range(2):
                    top = m[:, 2 * c, :]
                    step(V.reduce_max(top, prob[:], AX.X))
                    step(V.tensor_tensor(key[:], prob[:], top.unsqueeze(2).to_broadcast(wide), ALU.is_equal))
                    step(V.tensor_tensor(key[:], key[:], rank[:].unsqueeze(1).to_broadcast(wide), ALU.mult))
                    step(V.reduce_max(m[:, 3, :], key[:], AX.X))
                    step(V.tensor_tensor(hot[:, c], key[:], m[:, 3, :].unsqueeze(2).to_broadcast(wide), ALU.is_equal))
                    if c == 0:
                        step(V.scalar_tensor_tensor(prob[:], hot[:, 0], -2.0, prob[:], ALU.mult, ALU.add))
                V.tensor_tensor(both[:], hot[:, 0], hot[:, 1], ALU.add).then_inc(both_ready, 1)
                V.tensor_tensor(m[:, 3, :], m[:, 2, :], m[:, 0, :], ALU.subtract).then_inc(exped, 1)
                dve.wait_ge(exped, 4)
                step(V.tensor_scalar_add(m[:, 1, :], k.wts[:, 1, :], 1.0))
                step(V.reciprocal(k.wts[:, 0, :], m[:, 1, :]))
                step(V.tensor_tensor(k.wts[:, 1, :], k.wts[:, 1, :], k.wts[:, 0, :], ALU.mult))
                dve.wait_ge(cnt_done, 1)
                counts = cnt_ps[:, 1, :].rearrange("p (t e) -> p t e", e=E)
                step(V.tensor_copy(run[:, 0], counts))
                at, by = 0, 1
                while by < NT:
                    o.mark(V.tensor_copy(run[:, 1 - at, 0:by, :], run[:, at, 0:by, :]))
                    step(V.tensor_tensor(run[:, 1 - at, by:, :], run[:, at, by:, :], run[:, at, 0:NT - by, :], ALU.add))
                    at, by = 1 - at, 2 * by
                step(V.tensor_scalar_add(cnt[:, 0, :], run[:, at, NT - 1, :], float(P - 1)))
                step(V.tensor_copy(cnti[:], cnt[:, 0, :]))
                step(V.tensor_scalar(cnti[:], cnti[:], 7, 7, ALU.arith_shift_right, ALU.logical_shift_left))
                step(V.tensor_copy(cnt[:, 3, :], cnti[:]))
                step(V.tensor_copy(cnt[:, 0, :], cnt[:, 3, :]))
                a, by = 0, 1
                while by < E:
                    o.mark(V.tensor_copy(cnt[:, 1 - a, 0:by], cnt[:, a, 0:by]))
                    step(V.tensor_tensor(cnt[:, 1 - a, by:], cnt[:, a, by:], cnt[:, a, 0:E - by], ALU.add))
                    a, by = 1 - a, 2 * by
                end = cnt[:, a, :]
                step(V.tensor_tensor(cnt[:, 2, :], end, cnt[:, 3, :], ALU.subtract))
                step(V.tensor_tensor(run[:, at], run[:, at], counts, ALU.subtract))
                step(V.tensor_tensor(run[:, at], run[:, at], cnt_ps[:, 0, :].rearrange("p (t e) -> p t e", e=E), ALU.add))
                step(V.tensor_tensor(run[:, at], run[:, at], cnt[:, 2, :].unsqueeze(1).to_broadcast(wide), ALU.add))
                for c in range(2):
                    step(V.tensor_tensor(key[:], hot[:, c], run[:, at], ALU.mult))
                    step(V.reduce_sum(slotf[:, :, c], key[:], AX.X))
                step(V.tensor_copy(k.slots[:], slotf[:]))
                row = [1, k.XS_TILES, E]
                step(V.tensor_tensor(cmp[:], start[:].unsqueeze(2).to_broadcast(row), end[0:1, :].unsqueeze(1).to_broadcast(row), ALU.is_ge))
                step(V.reduce_sum(eidf[:], cmp[:], AX.X))
                step(V.tensor_scalar_min(eidf[:], eidf[:], float(E - 1)))
                step(V.tensor_copy(k.eid[:], eidf[:]))
                for u in range(2):
                    V.tensor_copy(sl[:, u], k.slots[:, u * G:(u + 1) * G, :]).then_inc(sl_ready, 1)
                with dve.Fori(1, NG // 2) as i:
                    for u in range(2):
                        dve.wait_ge(scattered[u], 16 * 2 * G * i)
                        V.tensor_copy(sl[:, u], k.slots[:, bass.ds((i * 2 + u) * G, G), :]).then_inc(sl_ready, 1)


def stage_experts(k):
    nc = k.nc
    with ExitStack() as ctx:
        sb, psum, sem = scratch(k, ctx)
        X = sb("e_x", [P, D])
        XT = sb("e_xT", [P, DC, P])
        act_g = sb("e_silu", [P, F])
        fuse = sb("e_fuse", [P, F])
        fuseT = sb("e_fuseT", [P, FC, P])
        Y = sb("e_y", [P, D])
        xT_ps = psum("e_xT_ps", [P, DC, P])
        g_ps = psum("e_g_ps", [P, F])
        u_ps = psum("e_u_ps", [P, F])
        fT_ps = psum("e_fT_ps", [P, FC, P])
        y_ps = psum("e_y_ps", [P, 512])
        x_in, xT_done, xT_ready = sem("e_xin"), sem("e_xTd"), sem("e_xTr")
        g_done, u_done, silu_done, fuse_ready = sem("e_gd"), sem("e_ud"), sem("e_sd"), sem("e_fr")
        fT_done, fT_ready, y_done, y_ready, y_out = sem("e_fTd"), sem("e_fTr"), sem("e_yd"), sem("e_yr"), sem("e_yo")
        TILES = k.TILES

        with nc.Block() as block:
            @block.sync
            def _(sp):
                sp.dma_start(X[:], k.xs_dram[0:P, :]).then_inc(x_in, 16)
                with sp.Fori(0, TILES) as j:
                    sp.wait_ge(xT_done, j + 1)
                    sp.dma_start(X[:], k.xs_dram[bass.ts(j + 1, P), :]).then_inc(x_in, 16)
                sp.wait_ge(x_in, 16 * (TILES + 1))

            @block.tensor
            def _(pe):
                pe.wait_ge(k.w_moe_in, 48)

                def transpose_x(j):
                    pe.wait_ge(x_in, 16 * (j + 1))
                    for c in range(DC):
                        mm = nc.tensor.transpose(xT_ps[:, c, :], X[:, c * P:(c + 1) * P], k.ident[:])
                    mm.then_inc(xT_done, 1)

                def into(j):
                    e = pe.value_load(k.eid[0:1, bass.ds(j, 1)], min_val=0, max_val=E - 1)
                    pe.wait_ge(xT_ready, j + 1)
                    for ps, w, done in ((g_ps, k.wg, g_done), (u_ps, k.wu, u_done)):
                        for c in range(DC):
                            mm = nc.tensor.matmul(ps[:], XT[:, c, :], w[:, bass.ds(e, 1), c, :], start=(c == 0), stop=(c == DC - 1))
                        mm.then_inc(done, 1)

                def out_of(j, first):
                    e = pe.value_load(k.eid[0:1, bass.ds(j, 1)], min_val=0, max_val=E - 1)
                    pe.wait_ge(fT_ready, j + 1)
                    if not first:
                        pe.wait_ge(y_ready, j)
                    for c in range(FC):
                        mm = nc.tensor.matmul(y_ps[:, 0:D], fuseT[:, c, :], k.wd[:, bass.ds(e, 1), c, :], start=(c == 0), stop=(c == FC - 1))
                    mm.then_inc(y_done, 1)

                def transpose_fuse(j):
                    pe.wait_ge(fuse_ready, j + 1)
                    for c in range(FC):
                        mm = nc.tensor.transpose(fT_ps[:, c, :], fuse[:, c * P:(c + 1) * P], k.ident[:])
                    mm.then_inc(fT_done, 1)

                transpose_x(0)
                into(0)
                transpose_x(1)
                transpose_fuse(0)
                into(1)
                out_of(0, True)
                transpose_x(2)
                transpose_fuse(1)
                with pe.Fori(2, TILES) as j:
                    into(j)
                    out_of(j - 1, False)
                    transpose_x(j + 1)
                    transpose_fuse(j)
                out_of(TILES - 1, False)

            @block.scalar
            def _(act):
                def silu(j):
                    act.wait_ge(g_done, j + 1)
                    nc.scalar.activation(act_g[:], g_ps[:], ACT.Silu).then_inc(silu_done, 1)

                def store(j, first):
                    act.wait_ge(y_done, j + 1)
                    if not first:
                        act.wait_ge(y_out, 16 * j)
                    nc.scalar.copy(Y[:], y_ps[:, 0:D]).then_inc(y_ready, 1)
                    act.wait_ge(y_ready, j + 1)
                    act.dma_start(k.ys_dram[bass.ts(j, P), :], Y[:]).then_inc(y_out, 16)

                silu(0)
                act.wait_ge(fuse_ready, 1)
                silu(1)
                store(0, True)
                with act.Fori(2, TILES) as j:
                    act.wait_ge(fuse_ready, j)
                    silu(j)
                    store(j - 1, False)
                store(TILES - 1, False)
                act.wait_ge(y_out, 16 * TILES)

            @block.vector
            def _(dve):
                def x_copy(j):
                    dve.wait_ge(xT_done, j + 1)
                    nc.vector.tensor_copy(XT[:], xT_ps[:]).then_inc(xT_ready, 1)

                def fuse_mul(j):
                    dve.wait_ge(silu_done, j + 1)
                    dve.wait_ge(u_done, j + 1)
                    nc.vector.tensor_tensor(fuse[:], u_ps[:], act_g[:], ALU.mult).then_inc(fuse_ready, 1)

                def fuse_copy(j):
                    dve.wait_ge(fT_done, j + 1)
                    nc.vector.tensor_copy(fuseT[:], fT_ps[:]).then_inc(fT_ready, 1)

                x_copy(0)
                with dve.Fori(0, TILES) as j:
                    fuse_mul(j)
                    x_copy(j + 1)
                    fuse_copy(j)


PARTS = 3


def stage_project(k):
    nc, io = k.nc, k.io
    with ExitStack() as ctx:
        sb, psum, sem = scratch(k, ctx)
        gb0 = sb("c_gb0", [P, B, D])
        wqkv = sb("c_wqkv", [P, DC, 3 * D])
        rope = sb("c_rope", [P, 2, S // P, DH])
        Y = sb("c_y", [P, 2, G, 2, D])
        sl = sb("c_sl", [P, 2, G * 2], I32)
        mix = sb("c_mix", [P, G, D])
        stats = sb("c_stats", [P, G, 6])
        mv = sb("c_mv", [P, G, 2])
        std = sb("c_std", [P, G])
        xn = sb("c_xn", [P, G, D])
        h = sb("c_h", [P, G, D])
        hT = sb("c_hT", [P, DC, GT])
        t1 = sb("c_t1", [P, 2 * H, DH])
        t2 = sb("c_t2", [P, 2 * H, DH])
        rot = sb("c_rot", [P, 2, 2 * D])
        rest = sb("c_rest", [P, 2, GT])
        parts = sb("c_parts", [P, 2 * DC, PARTS, GT], BF16)
        hT_ps = psum("c_hT_ps", [P, DC, 512])
        qk_ps = psum("c_qk_ps", [P, 512])
        v_ps = psum("c_v_ps", [P, 512])
        T_ps = psum("c_T_ps", [P, 2 * DC, 512])
        HALF = DH // 2

        w_in, steps, sl_ready, y_used = sem("c_w"), sem("c_steps"), sem("c_sl"), sem("c_yu")
        y_in = [sem(f"c_yin{u}") for u in range(2)]
        stats_ready, std_ready, h_ready = sem("c_st"), sem("c_std"), sem("c_h")
        hT_done, hT_c0, hT_c1 = sem("c_hT"), sem("c_c0"), sem("c_c1")
        qk_done, v_done, v_read, qk_read, rot_ready, T_done = sem("c_qk"), sem("c_v"), sem("c_vr"), sem("c_qkr"), sem("c_rot"), sem("c_T")
        hi_ready, rest_ready, mid_ready, low_ready, parts_out = sem("c_hi"), sem("c_rest"), sem("c_mid"), sem("c_low"), sem("c_po")

        with nc.Block() as block:
            @block.sync
            def _(sp):
                sp.dma_start(gb0[:], k.modrow_dram[0][:, GBI, :].partition_broadcast(P)).then_inc(w_in, 16)
                sp.dma_start(k.mods[:].rearrange("p b m d -> p (b m d)"),
                             k.modrow_dram[1].rearrange("b m d -> (b m d)").partition_broadcast(P)).then_inc(w_in, 16)
                sp.dma_start(wqkv[:], io["L1_Wqkv"].rearrange("(c p) n -> p c n", p=P)).then_inc(w_in, 16)
                sp.dma_start(rope[:].rearrange("p a t d -> p (a t) d"), io["rope"].rearrange("a (t p) d -> p (a t) d", p=P)).then_inc(w_in, 16)
                sp.nop().then_inc(parts_out, 16 * 2 * DC)
                with sp.Fori(0, NG) as g:
                    for c in range(2 * DC):
                        sp.wait_ge(low_ready, g * 2 * DC + c + 1)
                        sp.dma_start(k.qk_dram[c, :, :, bass.ts(g, GT)].rearrange("a p n -> p a n"), parts[:, c]).then_inc(parts_out, 16)
                sp.wait_ge(parts_out, 16 * 2 * DC * (NG + 1))

            @block.gpsimd
            def _(pool):
                def gather(i, u):
                    wait_alone(pool, sl_ready, i * 2 + u + 1)
                    for s in range(G):
                        for c in range(2):
                            nc.gpsimd.indirect_dma_start(Y[:, u, s, c, :], None, k.ys_dram,
                                                         bass.IndirectOffsetOnAxis(ap=sl[:, u, s * 2 + c:s * 2 + c + 1], axis=0),
                                                         ).then_inc(y_in[u], 16)

                def middle(g):
                    for c in range(2 * DC):
                        wait_alone(pool, rest_ready, g * 2 * DC + c + 1)
                        nc.gpsimd.tensor_copy(parts[:, c, 1, :], rest[:, c % 2, :]).then_inc(mid_ready, 1)

                gather(0, 0)
                with pool.Fori(0, NG // 2 - 1) as i:
                    gather(i, 1)
                    middle(i * 2)
                    gather(i + 1, 0)
                    middle(i * 2 + 1)
                gather(NG // 2 - 1, 1)
                middle(NG - 2)
                middle(NG - 1)

            @block.vector
            def _(dve):
                o = Order(dve, steps)
                V = nc.vector
                dve.wait_ge(w_in, 64)

                def ask(g, u):
                    V.tensor_copy(sl[:, u, :], k.slots[:, bass.ds(g * G, G), :].rearrange("p t c -> p (t c)")).then_inc(sl_ready, 1)

                def group(i, u, more):
                    g = i * 2 + u
                    dve.wait_ge(y_in[u], 16 * 2 * G * (i + 1))
                    for s in range(G):
                        o.mark(V.tensor_scalar_mul(mix[:, s, :], Y[:, u, s, 0, :], k.wts[:, 0, bass.ds(g * G + s, 1)]))
                    o.settle()
                    for s in range(G):
                        o.mark(V.scalar_tensor_tensor(mix[:, s, :], Y[:, u, s, 1, :], k.wts[:, 1, bass.ds(g * G + s, 1)],
                                                      mix[:, s, :], ALU.mult, ALU.add))
                    o.settle()
                    if more:
                        ask(g + 2, u)
                    xg = k.x[:, bass.ds(g * G, G), :]
                    mod = lambda t, m: t[:, bass.ds(g // GB, 1), m, :].to_broadcast([P, G, D])
                    o.mark(V.tensor_tensor(mix[:], mix[:], gb0[:, bass.ds(g // GB, 1), :].to_broadcast([P, G, D]), ALU.mult))
                    o.settle()
                    o.mark(V.tensor_tensor(xg, xg, mix[:], ALU.add))
                    o.settle_alone()
                    for s in range(G):
                        o.mark(V.bn_stats(stats[:, s, :], k.x[:, bass.ds(g * G + s, 1), :]))
                    o.settle_alone()
                    for s in range(G):
                        V.bn_aggr(mv[:, s, :], stats[:, s, :]).then_inc(stats_ready, 1)
                    dve.wait_ge(std_ready, g + 1)
                    o.mark(V.reciprocal(std[:], std[:]))
                    o.settle()
                    for s in range(G):
                        o.mark(V.tensor_scalar(xn[:, s, :], k.x[:, bass.ds(g * G + s, 1), :], mv[:, s, 0:1], std[:, s:s + 1],
                                               ALU.subtract, ALU.mult))
                    o.settle()
                    o.mark(V.tensor_tensor(xn[:], xn[:], mod(k.mods, CA), ALU.mult))
                    o.settle()
                    V.tensor_tensor(h[:], xn[:], mod(k.mods, SA), ALU.add).then_inc(h_ready, 1)
                    dve.wait_ge(hT_done, g + 1)
                    V.tensor_copy(hT[:, 0, :], hT_ps[:, 0, :]).then_inc(hT_c0, 1)
                    for s in range(G):
                        dve.wait_ge(qk_done, g * G + s + 1)
                        qk = qk_ps[:].rearrange("p (h d) -> p h d", d=DH)
                        tab = lambda a, lo, hi: rope[:, a, bass.ds((g % GB) * G + s, 1), lo:hi].to_broadcast([P, 2 * H, hi - lo])
                        o.mark(V.tensor_tensor(t1[:], qk, tab(0, 0, DH), ALU.mult))
                        o.mark(V.tensor_tensor(t2[:, :, 0:HALF], qk[:, :, HALF:], tab(1, 0, HALF), ALU.mult))
                        o.mark(V.tensor_tensor(t2[:, :, HALF:], qk[:, :, 0:HALF], tab(1, HALF, DH), ALU.mult))
                        o.settle()
                        if s >= 2:
                            dve.wait_ge(T_done, g * G + s - 1)
                        V.tensor_tensor(rot[:, s % 2, :].rearrange("p (h d) -> p h d", d=DH), t1[:], t2[:], ALU.add).then_inc(rot_ready, 1)
                        dve.wait_ge(rot_ready, g * G + s + 1)
                    dve.wait_ge(T_done, (g + 1) * G)
                    for c in range(2 * DC):
                        scale = 0.25 if c < DC else 1.0
                        dve.wait_ge(hi_ready, g * 2 * DC + c + 1)
                        V.scalar_tensor_tensor(rest[:, c % 2, :], T_ps[:, c, :], scale, parts[:, c, 0, :],
                                               ALU.mult, ALU.subtract).then_inc(rest_ready, 1)
                        if c >= 1:
                            low(g, c - 1)
                    low(g, 2 * DC - 1)

                def low(g, c):
                    dve.wait_ge(mid_ready, g * 2 * DC + c + 1)
                    V.tensor_tensor(parts[:, c, 2, :], rest[:, c % 2, :], parts[:, c, 1, :], ALU.subtract).then_inc(low_ready, 1)
                    dve.wait_ge(low_ready, g * 2 * DC + c + 1)

                ask(0, 0)
                ask(1, 1)
                TURN = 2 * (G + G + 2 + G + 1 + G + 1 + 3 * G)
                with dve.Fori(0, NG // 2 - 1) as i:
                    o.turn(i, 0, TURN)
                    group(i, 0, True)
                    group(i, 1, True)
                    assert o.n == TURN, (o.n, TURN)
                o.turn(NG // 2 - 1, 0, TURN)
                group(NG // 2 - 1, 0, False)
                group(NG // 2 - 1, 1, False)

            @block.scalar
            def _(act):
                with act.Fori(0, NG) as g:
                    act.wait_ge(stats_ready, (g + 1) * G)
                    nc.scalar.activation(std[:], mv[:, :, 1], ACT.Sqrt, bias=k.eps[:, 0:1]).then_inc(std_ready, 1)
                    act.wait_ge(hT_done, g + 1)
                    nc.scalar.copy(hT[:, 1, :], hT_ps[:, 1, :]).then_inc(hT_c1, 1)
                    for s in range(G):
                        act.wait_ge(v_done, g * G + s + 1)
                        nc.scalar.copy(k.v[:, bass.ds(g * G + s, 1), :, :].rearrange("p t h d -> p (t h d)"), v_ps[:, 0:D]).then_inc(v_read, 1)
                    act.wait_ge(T_done, (g + 1) * G)
                    act.wait_ge(parts_out, 16 * 2 * DC * (g + 1))
                    for c in range(2 * DC):
                        nc.scalar.activation(parts[:, c, 0, :], T_ps[:, c, :], ACT.Copy, scale=0.25 if c < DC else 1.0).then_inc(hi_ready, 1)

            @block.tensor
            def _(pe):
                pe.wait_ge(w_in, 64)
                with pe.Fori(0, NG) as g:
                    pe.wait_ge(h_ready, g + 1)
                    for c in range(DC):
                        for s in range(G):
                            mm = nc.tensor.transpose(hT_ps[:, c, s * P:(s + 1) * P], h[:, s, c * P:(c + 1) * P], k.ident[:])
                    mm.then_inc(hT_done, 1)
                    pe.wait_ge(hT_c0, g + 1)
                    pe.wait_ge(hT_c1, g + 1)

                    def turn_channels(s):
                        pe.wait_ge(rot_ready, g * G + s + 1)
                        for c in range(2 * DC):
                            mm = nc.tensor.transpose(T_ps[:, c, s * P:(s + 1) * P], rot[:, s % 2, c * P:(c + 1) * P], k.ident[:])
                        mm.then_inc(T_done, 1)

                    for s in range(G):
                        if s >= 1:
                            pe.wait_ge(rot_ready, g * G + s)
                        for c in range(DC):
                            mm = nc.tensor.matmul(qk_ps[:], hT[:, c, s * P:(s + 1) * P], wqkv[:, c, 0:2 * D], start=(c == 0), stop=(c == DC - 1))
                        mm.then_inc(qk_done, 1)
                        if s >= 1:
                            pe.wait_ge(v_read, g * G + s)
                        for c in range(DC):
                            mm = nc.tensor.matmul(v_ps[:, 0:D], hT[:, c, s * P:(s + 1) * P], wqkv[:, c, 2 * D:], start=(c == 0), stop=(c == DC - 1))
                        mm.then_inc(v_done, 1)
                        if s >= 1:
                            turn_channels(s - 1)
                    turn_channels(G - 1)
                    pe.wait_ge(rest_ready, (g + 1) * 2 * DC)
                    pe.wait_ge(v_read, (g + 1) * G)


Q_BLOCKS = (0, 1, 2, 0, 1, 0)
K_BLOCKS = (0, 0, 0, 1, 1, 2)
Q_LOADS = ((0, 0, 3), (3, 0, 2), (5, 0, 1))
K_LOADS = tuple((n, part, 1) for n, part in enumerate(K_BLOCKS))
SLOTS = 4


def stage_attention(k):
    nc, io = k.nc, k.io
    ROWS = len(Q_BLOCKS) * DH
    KT, QB = S // P, S // 512
    HEADS = B * H
    VW = 2 * DH
    LEAD = 5
    STORED = 16 * QB
    LOADS_PER = len(Q_LOADS) + len(K_LOADS)
    with ExitStack() as ctx:
        sb, psum, sem = scratch(k, ctx)
        q = sb("t_q", [P, SLOTS, S], BF16)
        kk = sb("t_k", [P, SLOTS, S], BF16)
        v = sb("t_v", [P, SLOTS, KT, VW])
        probs = sb("t_p", [P, 2, S])
        peak = sb("t_peak", [P, 2, KT, QB])
        top = sb("t_top", [P, 2, KT])
        neg = sb("t_neg", [P, 2, KT])
        negparts = sb("t_negp", [P, PARTS, KT], BF16)
        negT = sb("t_negT", [PARTS * KT, P], BF16)
        o_sb = sb("t_o", [P, 512])
        sT_ps = psum("t_sT_ps", [P, 2, 2, 512])
        mx_ps = psum("t_mx_ps", [P, 2, 512])
        pv_ps = psum("t_pv_ps", [P, 512])
        nT_ps = psum("t_nT_ps", [PARTS * KT, P], BF16)

        qk_in = [sem(f"t_in{u}") for u in range(SLOTS)]
        ones_ready, v_ready = sem("t_ones"), sem("t_vr")
        mx_done, mx_read, top_ready, neg_steps, neg_ready = sem("t_mxd"), sem("t_mxr"), sem("t_top"), sem("t_ns"), sem("t_nr")
        nT_done, nT_ready, row_in = sem("t_nTd"), sem("t_nTr"), sem("t_row")
        s_done, e_done, pv_done, o_ready, o_out = sem("t_s"), sem("t_e"), sem("t_pv"), sem("t_or"), sem("t_oo")

        def turns(eng, turn):
            with eng.Fori(0, HEADS // SLOTS - 1) as i:
                for u in range(SLOTS):
                    turn(i * SLOTS + u, i, u, 2)
            i = HEADS // SLOTS - 1
            for u in range(SLOTS):
                turn(i * SLOTS + u, i, u, min(2, SLOTS - 1 - u))

        def later(i, u, by):
            return i + (u + by) // SLOTS, (u + by) % SLOTS

        with nc.Block() as block:
            @block.sync
            def _(sp):
                def load(n, u):
                    b, hd = n // H, n % H
                    for t, which, blocks in ((q, 0, Q_LOADS), (kk, 1, K_LOADS)):
                        src = k.qk_dram[bass.ds(which * DC + hd // HC, 1), :, bass.ds((hd % HC) * DH, DH), bass.ds(b * S, S)]
                        for at, part, count in blocks:
                            sp.dma_start(t[at * DH:(at + count) * DH, u, :],
                                         src[:, part:part + count].rearrange("o a d n -> (o a) d n")).then_inc(qk_in[u], 16)

                sp.nop().then_inc(o_out, STORED)
                load(0, 0)
                load(1, 1)

                def rows(n, u):
                    sp.wait_ge(nT_ready, n + 1)
                    sp.dma_start(q[ROWS:ROWS + PARTS, u, :].rearrange("a (t n) -> a t n", n=P), negT[:]).then_inc(row_in, 16)

                rows(0, 0)

                def turn(n, i, u, ahead):
                    sp.wait_ge(pv_done, n * KT + 2)
                    if ahead >= 2:
                        load(n + 2, (u + 2) % SLOTS)
                    if ahead >= 1:
                        rows(n + 1, (u + 1) % SLOTS)
                    sp.wait_ge(o_ready, n + 2)
                    b, hd = n // H, n % H
                    for j in range(QB):
                        cols = bass.ds(b * S + j * 512, 512)
                        sp.dma_start(k.od_dram[:, bass.ds(hd * DH, DH), cols], o_sb[j * VW:(j + 1) * VW, :]).then_inc(o_out, 16)

                turns(sp, turn)
                sp.wait_ge(o_out, STORED * (HEADS + 1))
                for u in range(SLOTS):
                    sp.wait_ge(qk_in[u], 16 * LOADS_PER * HEADS // SLOTS)

            @block.gpsimd
            def _(pool):
                for u in range(SLOTS):
                    nc.gpsimd.memset(kk[ROWS:ROWS + PARTS, u, :], 1.0).then_inc(ones_ready, 1)
                pool.wait_ge(ones_ready, SLOTS)
                nc.gpsimd.memset(v[:, :, :, DH:], 1.0).then_inc(ones_ready, 1)

                def copy_v(n, u):
                    b, hd = n // H, n % H
                    nc.gpsimd.tensor_copy(v[:, u, :, 0:DH], k.v[:, bass.ds(b * KT, KT), bass.ds(hd, 1), :].rearrange("p t o d -> p t (o d)")).then_inc(v_ready, 1)

                def split(n, u):
                    wait_alone(pool, top_ready, n + 1)
                    w = u % 2
                    g = nc.gpsimd
                    g.tensor_scalar_mul(neg[:, 0], top[:, w], -1.0).then_inc(neg_steps, 1)
                    pool.wait_ge(nT_done, n + 1)
                    wait_alone(pool, neg_steps, n * 4 + 1)
                    g.tensor_copy(negparts[:, 0], neg[:, 0]).then_inc(neg_steps, 1)
                    pool.wait_ge(neg_steps, n * 4 + 2)
                    g.tensor_tensor(neg[:, 1], neg[:, 0], negparts[:, 0], ALU.subtract).then_inc(neg_steps, 1)
                    wait_alone(pool, neg_steps, n * 4 + 3)
                    g.tensor_copy(negparts[:, 1], neg[:, 1]).then_inc(neg_steps, 1)
                    pool.wait_ge(neg_steps, n * 4 + 4)
                    g.tensor_tensor(negparts[:, 2], neg[:, 1], negparts[:, 1], ALU.subtract).then_inc(neg_ready, 1)
                    pool.wait_ge(neg_ready, n + 1)

                copy_v(0, 0)
                copy_v(1, 1)
                split(0, 0)

                def turn(n, i, u, ahead):
                    pool.wait_ge(pv_done, n * KT + 2)
                    if ahead >= 2:
                        copy_v(n + 2, (u + 2) % SLOTS)
                    if ahead >= 1:
                        split(n + 1, (u + 1) % SLOTS)

                turns(pool, turn)

            @block.vector
            def _(dve):
                dve.nop().then_inc(mx_read, 2)

                def maxima(n, w, m):
                    for kb in range(QB):
                        t = (n * KT + m) * QB + kb
                        dve.wait_ge(mx_done, t + 1)
                        nc.vector.reduce_max(peak[:, w, m, kb:kb + 1], mx_ps[:, kb % 2, :], AX.X).then_inc(mx_read, 1)
                    if m == KT - 1:
                        dve.wait_ge(mx_read, (n + 1) * KT * QB + 2)
                        nc.vector.reduce_max(top[:, w], peak[:, w], AX.X).then_inc(top_ready, 1)

                def turned(n):
                    dve.wait_ge(nT_done, n + 2)
                    dve.wait_ge(row_in, 16 * (n + 1))
                    nc.vector.tensor_copy(negT[:], nT_ps[:]).then_inc(nT_ready, 1)

                for m in range(KT):
                    maxima(0, 0, m)
                turned(0)
                for m in range(LEAD):
                    maxima(1, 1, m)

                def turn(n, i, u, ahead):
                    for kt in range(KT):
                        m = kt + LEAD
                        if m < KT and ahead >= 1:
                            maxima(n + 1, (u + 1) % 2, m)
                        if m >= KT and ahead >= 2:
                            maxima(n + 2, u % 2, m - KT)
                        if kt == KT - LEAD + 2 and ahead >= 1:
                            turned(n + 1)

                turns(dve, turn)

            @block.scalar
            def _(act):
                act.nop().then_inc(e_done, 2)

                def exps(n, kt):
                    for hf in range(2):
                        act.wait_ge(s_done, (n * KT + kt) * 2 + hf + 1)
                        if hf == 0:
                            act.wait_ge(pv_done, n * KT + kt + 1)
                        nc.scalar.activation(probs[:, kt % 2, hf * 1024:(hf + 1) * 1024].rearrange("p (j n) -> p j n", n=512),
                                             sT_ps[:, hf], ACT.Exp).then_inc(e_done, 1)

                exps(0, 0)

                def turn(n, i, u, ahead):
                    for kt in range(1, KT):
                        exps(n, kt)
                    if ahead >= 1:
                        exps(n + 1, 0)
                    act.wait_ge(pv_done, (n + 1) * KT + 2)
                    act.wait_ge(o_out, STORED * (n + 1))
                    nc.scalar.copy(o_sb[:], pv_ps[:]).then_inc(o_ready, 1)

                turns(act, turn)

            @block.tensor
            def _(pe):
                pe.wait_ge(ones_ready, SLOTS + 1)
                pe.nop().then_inc(pv_done, 2)
                pe.nop().then_inc(o_ready, 1)
                pe.nop().then_inc(nT_done, 1)
                pe.nop().then_inc(row_in, 16)

                def maxima(n, u, m):
                    for kb in range(QB):
                        t = (n * KT + m) * QB + kb
                        pe.wait_ge(mx_read, t + 1)
                        nc.tensor.matmul(mx_ps[:, kb % 2, :], q[0:ROWS, u, m * P:(m + 1) * P], kk[0:ROWS, u, kb * 512:(kb + 1) * 512],
                                         start=True, stop=True).then_inc(mx_done, 1)

                def scores(n, u, kt):
                    for hf in range(2):
                        pe.wait_ge(e_done, (n * KT + kt) * 2 + hf + 1)
                        for j in range(2):
                            qb = 2 * hf + j
                            mm = nc.tensor.matmul(sT_ps[:, hf, j, :], kk[0:ROWS + PARTS, u, kt * P:(kt + 1) * P],
                                                  q[0:ROWS + PARTS, u, qb * 512:(qb + 1) * 512], start=True, stop=True)
                        mm.then_inc(s_done, 1)

                def weigh(n, u, kt):
                    pe.wait_ge(e_done, (n * KT + kt) * 2 + 4)
                    if kt == 0:
                        pe.wait_ge(v_ready, n + 1)
                        pe.wait_ge(o_ready, n + 1)
                    for j in range(QB):
                        mm = nc.tensor.matmul(pv_ps[j * VW:(j + 1) * VW, :], v[:, u, kt, :], probs[:, kt % 2, j * 512:(j + 1) * 512],
                                              start=(kt == 0), stop=(kt == KT - 1), tile_position=(0, j * VW))
                    mm.then_inc(pv_done, 1)

                def turn_maxima(n):
                    wait_alone(pe, neg_ready, n + 1)
                    nc.tensor.transpose(nT_ps[:], negparts[:].rearrange("p a t -> p (a t)"), k.identb[:]).then_inc(nT_done, 1)

                pe.wait_ge(qk_in[0], 16 * LOADS_PER)
                for m in range(KT):
                    maxima(0, 0, m)
                turn_maxima(0)
                pe.wait_ge(qk_in[1], 16 * LOADS_PER)
                for m in range(LEAD):
                    maxima(1, 1, m)
                pe.wait_ge(row_in, 32)
                scores(0, 0, 0)

                def turn(n, i, u, ahead):
                    for kt in range(KT):
                        if kt + 1 < KT:
                            scores(n, u, kt + 1)
                        elif ahead >= 1:
                            pe.wait_ge(row_in, 16 * (n + 3))
                            scores(n + 1, (u + 1) % SLOTS, 0)
                        m = kt + LEAD
                        if m < KT and ahead >= 1:
                            maxima(n + 1, (u + 1) % SLOTS, m)
                        if m >= KT and ahead >= 2:
                            if m == KT:
                                i2, u2 = later(i, u, 2)
                                pe.wait_ge(qk_in[u2], 16 * LOADS_PER * (i2 + 1))
                            maxima(n + 2, (u + 2) % SLOTS, m - KT)
                        if kt == KT - LEAD + 2 and ahead >= 1:
                            turn_maxima(n + 1)
                        weigh(n, u, kt)

                turns(pe, turn)


KEYS = 64
PH = 8
NEXP = KEYS * KEYS * 4


def stage_peer(k):
    nc, io = k.nc, k.io
    SIMS = 2 * PH * KEYS
    SLOTS_Y = 4
    with ExitStack() as ctx:
        sb, psum, sem = scratch(k, ctx)
        wo = sb("p_wo", [P, DC, D])
        wsim = sb("p_wsim", [P, DC, SIMS])
        od = sb("p_od", [P, 2, DC, GT])
        at = sb("p_at", [P, DC, GT])
        upd = sb("p_upd", [P, G, D])
        stats = sb("p_stats", [P, G, 6])
        mv = sb("p_mv", [P, G, 2])
        std = sb("p_std", [P, G])
        xn = sb("p_xn", [P, G, D])
        h = sb("p_h", [P, G, D])
        hu = sb("p_hu", [P, G, D])
        hT = sb("p_hT", [P, DC, GT])
        val = sb("p_val", [P, 2, PH])
        arg = sb("p_arg", [P, 2, PH, 8], U32)
        score = sb("p_score", [P, SLOTS_Y, PH])
        sl = sb("p_sl", [P, SLOTS_Y, PH], I32)
        Y = sb("p_Y", [P, SLOTS_Y, PH, 2 * D])
        dump = sb("p_dump", [P, PH, D])
        dot = sb("p_dot", [P, 2, PH])
        act_dot = sb("p_gelu", [P, 2, PH])
        gk = sb("p_gk", [P, 2, PH])
        diag = sb("p_diag", [P, 2, PH, P])
        part = sb("p_part", [P, D])

        w_in, ws_done, ws_ready = sem("p_w"), sem("p_wsd"), sem("p_wsr")
        od_in, at_ready, proj_done, steps = sem("p_od"), sem("p_at"), sem("p_proj"), sem("p_steps")
        stats_ready, std_ready, h_ready, h_kept = sem("p_st"), sem("p_std"), sem("p_h"), sem("p_hk")
        hT_done, hT_ready, sim_done, val_ready, arg_ready, idx_ready = sem("p_hTd"), sem("p_hTr"), sem("p_sim"), sem("p_val"), sem("p_arg"), sem("p_idx")
        y_in = [sem(f"p_y{u}") for u in range(SLOTS_Y)]
        dots_done, gelu_ready, gk_ready, diag_ready, sums_done, part_ready, x_ready, x_out = (
            sem("p_dots"), sem("p_gelu"), sem("p_gk"), sem("p_diag"), sem("p_sums"), sem("p_part"), sem("p_x"), sem("p_xo"))

        with nc.Block() as block:
            with ExitStack() as pre:
                wq = pre.enter_context(nc.sbuf_tensor("p_wq", [P, 2 * PH, D], F32))
                keys = pre.enter_context(nc.sbuf_tensor("p_keys", [P, 2 * PH, KEYS], F32))
                ws_ps = pre.enter_context(nc.psum_tensor("p_ws_ps", [P, DC, SIMS], F32))
                @block.sync
                def _(sp):
                    sp.dma_start(wq[:], io["L1_wqT"].rearrange("(a p) d -> p a d", p=P)).then_inc(w_in, 16)
                    sp.dma_start(keys[:], io["L1_keysT"].rearrange("(a p) n -> p a n", p=P)).then_inc(w_in, 16)
                    sp.dma_start(wo[:], io["L1_Wo"].rearrange("(c p) n -> p c n", p=P)).then_inc(w_in, 16)

                @block.tensor
                def _(pe):
                    pe.wait_ge(w_in, 48)
                    for c in range(DC):
                        for a in range(2 * PH):
                            mm = nc.tensor.matmul(ws_ps[:, c, a * KEYS:(a + 1) * KEYS], wq[:, a, c * P:(c + 1) * P], keys[:, a, :],
                                                  start=True, stop=True)
                    mm.then_inc(ws_done, 1)

                @block.scalar
                def _(act):
                    act.wait_ge(ws_done, 1)
                    nc.scalar.copy(wsim[:], ws_ps[:]).then_inc(ws_ready, 1)

        tmp_ps = psum("p_tmp_ps", [P, 2, 512])
        sim_ps = psum("p_sim_ps", [P, 2, SIMS])
        out_ps = psum("p_out_ps", [P, 512])

        def inside(g, u):
            return not isinstance(g, int) or 0 <= g * G + u < NT

        def run(eng, step, ahead):
            for u in range(G):
                step(0, u)
                ahead(0, u)
            with eng.Fori(1, NG - 1) as g:
                for u in range(G):
                    step(g, u)
                    ahead(g, u)
            for u in range(G):
                step(NG - 1, u)
            for u in range(3):
                step(NG, u)

        with nc.Block() as block:
            @block.sync
            def _(sp):
                def load(g):
                    cols = bass.ds(g * GT, GT)
                    for a in range(2):
                        sp.dma_start(od[:, a], k.od_dram[a][:, cols].rearrange("(c p) n -> p c n", p=P)).then_inc(od_in, 16)

                def store(g):
                    sp.wait_ge(x_ready, (g + 1) * G)
                    sp.dma_start(k.out.rearrange("b (t p) d -> p (b t) d", p=P)[:, bass.ds(g * G, G), :],
                                 k.x[:, bass.ds(g * G, G), :]).then_inc(x_out, 16)

                load(0)
                sp.wait_ge(at_ready, 1)
                load(1)
                with sp.Fori(0, NG - 2) as g:
                    sp.wait_ge(at_ready, g + 2)
                    load(g + 2)
                    store(g)
                store(NG - 2)
                store(NG - 1)
                sp.wait_ge(x_out, 16 * NG)

            @block.gpsimd
            def _(pool):
                def step(g, u):
                    if not inside(g, u):
                        return
                    t = g * G + u
                    if inside(g, u - SLOTS_Y):
                        pool.wait_ge(sums_done, t - SLOTS_Y + 1)
                    wait_alone(pool, idx_ready, t + 1)
                    for j in range(PH):
                        nc.gpsimd.indirect_dma_start(Y[:, u, j, :], None, io["L1_table"],
                                                     bass.IndirectOffsetOnAxis(ap=sl[:, u, j:j + 1], axis=0)).then_inc(y_in[u], 16)

                run(pool, step, lambda g, u: None)

            @block.vector
            def _(dve):
                o = Order(dve, steps)
                V = nc.vector
                mod = lambda g, m: k.mods[:, bass.ds(g // GB, 1), m, :]

                def attended(g):
                    dve.wait_ge(od_in, 32 * (g + 1))
                    o.mark(V.reciprocal(od[:, 1], od[:, 1]))
                    o.settle()
                    V.tensor_tensor(at[:], od[:, 0], od[:, 1], ALU.mult).then_inc(at_ready, 1)

                def residual(g):
                    dve.wait_ge(proj_done, g + 1)
                    xg = k.x[:, bass.ds(g * G, G), :]
                    o.mark(V.tensor_tensor(upd[:], tmp_ps[:].rearrange("p a (s d) -> p (a s) d", d=D),
                                           mod(g, GA).to_broadcast([P, G, D]), ALU.mult))
                    o.settle()
                    o.mark(V.tensor_tensor(xg, xg, upd[:], ALU.add))
                    o.settle_alone()
                    for s in range(G):
                        o.mark(V.bn_stats(stats[:, s, :], k.x[:, bass.ds(g * G + s, 1), :]))
                    o.settle_alone()
                    for s in range(G):
                        V.bn_aggr(mv[:, s, :], stats[:, s, :]).then_inc(stats_ready, 1)

                def normalise(g):
                    dve.wait_ge(std_ready, g + 1)
                    o.mark(V.reciprocal(std[:], std[:]))
                    o.settle()
                    for s in range(G):
                        o.mark(V.tensor_scalar(xn[:, s, :], k.x[:, bass.ds(g * G + s, 1), :], mv[:, s, 0:1], std[:, s:s + 1],
                                               ALU.subtract, ALU.mult))
                    o.settle()
                    o.mark(V.tensor_tensor(xn[:], xn[:], mod(g, CB).to_broadcast([P, G, D]), ALU.mult))
                    o.settle()
                    if not isinstance(g, int) or g > 0:
                        dve.wait_ge(h_kept, 2 * g)
                    V.tensor_tensor(h[:], xn[:], mod(g, SB).to_broadcast([P, G, D]), ALU.add).then_inc(h_ready, 1)

                def dots(g, u):
                    v, t = u % SLOTS_Y, g * G + u
                    turn = g + u // SLOTS_Y
                    dve.wait_ge(y_in[v], 16 * PH * (turn + 1))
                    dve.wait_ge(h_kept, 2 * turn + 1 + v // 2)
                    for j in range(PH):
                        V.tensor_tensor_reduce(dump[:, j, :], hu[:, v, :], Y[:, v, j, 0:D], 1.0, 0.0, ALU.mult, ALU.add,
                                               dot[:, v % 2, j:j + 1]).then_inc(dots_done, 1)

                def choose(g, u):
                    t = g * G + u
                    dve.wait_ge(sim_done, t + 1)
                    sims = sim_ps[:, u % 2, :].rearrange("p (a n) -> p a n", n=KEYS)
                    V.reduce_max(val[:].rearrange("p a j -> p (a j)"), sims, AX.X).then_inc(val_ready, 1)
                    wait_alone(dve, val_ready, t + 1)
                    for a in range(2):
                        for j in range(PH):
                            V.max_index(arg[:, a, j, :], val[:, a, j:j + 1].to_broadcast([P, 8]), sims[:, a * PH + j, :]).then_inc(arg_ready, 1)
                    o.mark(V.tensor_tensor(score[:, u, :], val[:, 0, :], val[:, 1, :], ALU.add))
                    dve.wait_ge(arg_ready, 2 * PH * (t + 1))
                    V.scalar_tensor_tensor(sl[:, u, :], arg[:, 0, :, 0], float(KEYS), arg[:, 1, :, 0], ALU.mult, ALU.add).then_inc(idx_ready, 1)

                def weights(g, u):
                    v, t = u % SLOTS_Y, g * G + u
                    dve.wait_ge(gelu_ready, t + 1)
                    V.scalar_tensor_tensor(gk[:, v % 2, :], score[:, v, :], 0.0, act_dot[:, v % 2, :], ALU.max, ALU.mult).then_inc(gk_ready, 1)

                def finish(g, u):
                    t = g * G + u
                    dve.wait_ge(sums_done, t + 1)
                    V.tensor_tensor(part[:], out_ps[:, 0:D], k.mods[:, bass.ds(t // (NT // B), 1), GBI, :].rearrange("p o d -> p (o d)"), ALU.mult).then_inc(part_ready, 1)
                    dve.wait_ge(part_ready, t + 1)
                    xt = k.x[:, bass.ds(t, 1), :].rearrange("p o d -> p (o d)")
                    V.tensor_tensor(xt, xt, part[:], ALU.add).then_inc(x_ready, 1)
                    dve.wait_ge(x_ready, t + 1)

                def step(g, u):
                    if inside(g, u - 2):
                        dots(g, u - 2)
                    if inside(g, u):
                        choose(g, u)
                    if inside(g, u - 2):
                        weights(g, u - 2)
                    if inside(g, u - 3):
                        finish(g, u - 3)

                AHEAD = 1 + 2 + G + 1 + G + 1 + G

                def ahead(g, u):
                    if u == 0:
                        attended(g + 1)
                    if u == 1:
                        residual(g + 1)
                    if u == 2:
                        normalise(g + 1)

                attended(0)
                residual(0)
                normalise(0)
                first = o.n

                def counted(g, u):
                    if u == 0:
                        o.turn(g, first, AHEAD)
                    step(g, u)

                run(dve, counted, ahead)

            @block.scalar
            def _(act):
                act.wait_ge(ws_ready, 1)

                def deviation(g):
                    act.wait_ge(stats_ready, (g + 1) * G)
                    nc.scalar.activation(std[:], mv[:, :, 1], ACT.Sqrt, bias=k.eps[:, 0:1]).then_inc(std_ready, 1)

                def turned(g, last):
                    act.wait_ge(hT_done, g + 1)
                    if last:
                        act.wait_ge(sim_done, g * G)
                    nc.scalar.copy(hT[:], tmp_ps[:]).then_inc(hT_ready, 1)

                def keep(g, half):
                    if inside(g, 2 * half - G):
                        act.wait_ge(dots_done, PH * (g * G + 2 * half - 2))
                    nc.scalar.copy(hu[:, 2 * half:2 * half + 2, :], h[:, 2 * half:2 * half + 2, :]).then_inc(h_kept, 1)

                def step(g, u):
                    if inside(g, u - 2):
                        v, t = (u - 2) % SLOTS_Y, g * G + u - 2
                        act.wait_ge(dots_done, PH * (t + 1))
                        nc.scalar.activation(act_dot[:, v % 2, :], dot[:, v % 2, :], ACT.Gelu).then_inc(gelu_ready, 1)
                        act.wait_ge(gk_ready, t + 1)
                        if inside(g, u - 4):
                            act.wait_ge(sums_done, t - 1)
                        for j in range(PH):
                            nc.scalar.activation(diag[:, v % 2, j, :], k.ident[:], ACT.Copy, scale=gk[:, v % 2, j:j + 1]).then_inc(diag_ready, 1)
                    if inside(g, u) and u == 1:
                        keep(g, 1)

                def ahead(g, u):
                    if u == 1:
                        deviation(g + 1)
                    if u == 2:
                        turned(g + 1, True)
                    if u == 3:
                        keep(g + 1, 0)

                deviation(0)
                turned(0, False)
                keep(0, 0)
                run(act, step, ahead)

            @block.tensor
            def _(pe):
                pe.wait_ge(ws_ready, 1)

                def project(g):
                    pe.wait_ge(at_ready, g + 1)
                    if not isinstance(g, int) or g > 0:
                        pe.wait_ge(hT_ready, g)
                    for s in range(G):
                        for c in range(DC):
                            mm = nc.tensor.matmul(tmp_ps[:, s // 2, (s % 2) * D:(s % 2 + 1) * D], at[:, c, s * P:(s + 1) * P], wo[:, c, :],
                                                  start=(c == 0), stop=(c == DC - 1))
                    mm.then_inc(proj_done, 1)

                def transposes(g):
                    pe.wait_ge(h_ready, g + 1)
                    for c in range(DC):
                        for s in range(G):
                            mm = nc.tensor.transpose(tmp_ps[:, c, s * P:(s + 1) * P], h[:, s, c * P:(c + 1) * P], k.ident[:])
                    mm.then_inc(hT_done, 1)

                def similarities(g, u):
                    t = g * G + u
                    if u == 0:
                        pe.wait_ge(hT_ready, g + 1)
                    if inside(g, u - 2):
                        pe.wait_ge(arg_ready, 2 * PH * (t - 1))
                    for n in range(2):
                        for c in range(DC):
                            mm = nc.tensor.matmul(sim_ps[:, u % 2, n * 512:(n + 1) * 512], hT[:, c, u * P:(u + 1) * P],
                                                  wsim[:, c, n * 512:(n + 1) * 512], start=(c == 0), stop=(c == DC - 1))
                    mm.then_inc(sim_done, 1)

                def sums(g, u):
                    v, t = u % SLOTS_Y, g * G + u
                    pe.wait_ge(diag_ready, PH * (t + 1))
                    if inside(g, u - 1):
                        pe.wait_ge(part_ready, t)
                    for j in range(PH):
                        mm = nc.tensor.matmul(out_ps[:, 0:D], diag[:, v % 2, j, :], Y[:, v, j, D:], start=(j == 0), stop=(j == PH - 1))
                    mm.then_inc(sums_done, 1)

                def step(g, u):
                    if u < G - 1 and inside(g, u + 1):
                        similarities(g, u + 1)
                    elif u == G - 1 and inside(g + 1, 0):
                        similarities(g + 1, 0)
                    if inside(g, u - 2):
                        sums(g, u - 2)

                def ahead(g, u):
                    if u == 0:
                        project(g + 1)
                    if u == 2:
                        transposes(g + 1)

                project(0)
                transposes(0)
                similarities(0, 0)
                run(pe, step, ahead)


def build(nc, io, out, upto=99):
    ctx = ExitStack()
    with ctx:
        k = setup(nc, ctx, io)
        k.out = out
        k.TILES = 2 * NT + E
        k.XS_TILES = k.TILES + 1
        dram = lambda name, shape, dt=F32: nc.dram_tensor(name, shape, dt, kind="Internal").ap()
        k.h2_dram = dram("h2_dram", [T, D])
        k.xs_dram = dram("xs_dram", [k.XS_TILES * P, D])
        k.ys_dram = dram("ys_dram", [k.TILES * P, D])
        k.qk_dram = dram("qk_dram", [2 * DC, PARTS, P, T], BF16)
        k.od_dram = dram("od_dram", [2, D, T])
        k.w_moe_in = ctx.enter_context(nc.semaphore("w_moe_in"))
        k.slots = ctx.enter_context(nc.sbuf_tensor("slots", [P, NT, 2], I32))
        k.wts = ctx.enter_context(nc.sbuf_tensor("wts", [P, 2, NT], F32))
        k.eid = ctx.enter_context(nc.sbuf_tensor("eid", [1, k.XS_TILES], I32))
        with ExitStack() as l0:
            def sb(name, shape):
                return l0.enter_context(nc.sbuf_tensor(name, shape, F32))
            k.kvsum = sb("kvsum", [P, B, DC, P + 1])
            k.logits = sb("logits", [P, NT, E])
            stage_modulation(k)
            stage_linear_attention_sums(k)
            stage_linear_attention_apply(k)
            if upto >= 3:
                k.wg = sb("wg", [P, E, DC, F])
                k.wu = sb("wu", [P, E, DC, F])
                k.wd = sb("wd", [P, E, FC, D])
                stage_route(k)
            if upto >= 4:
                stage_experts(k)
        if upto >= 5:
            with ExitStack() as l1:
                k.v = l1.enter_context(nc.sbuf_tensor("v", [P, NT, H, DH], F32))
                stage_project(k)
                if upto >= 6:
                    stage_attention(k)
        if upto >= 7:
            stage_peer(k)


def layout(inputs):
    def plain(a):
        return np.ascontiguousarray(np.asarray(a))

    arrays = {"L0_attn_x": plain(inputs["L0_attn_x"])}
    for l in (0, 1):
        arrays[f"L{l}_cT"] = plain(np.asarray(inputs[f"L{l}_c"]).T)
        arrays[f"L{l}_wmod"] = plain(inputs[f"L{l}_wmod"])
    for n in "qkv":
        arrays[f"L0_W{n}T"] = plain(np.asarray(inputs[f"L0_attn_W{n}"]).T)
        arrays[f"L0_attn_b{n}"] = plain(inputs[f"L0_attn_b{n}"])
    for n in ("gamma", "beta"):
        arrays[f"L0_attn_{n}"] = plain(inputs[f"L0_attn_{n}"])
    arrays["L0_router"] = plain(inputs["L0_ffn_router_kernel_DE"])
    for n, source in (("gate", "gating_EDF"), ("up", "up_EDF"), ("down", "down_EFD")):
        arrays[f"L0_{n}"] = plain(inputs[f"L0_ffn_kernel_{source}"])
    arrays["L1_Wqkv"] = plain(inputs["L1_attn_Wqkv"])
    arrays["L1_Wo"] = plain(inputs["L1_attn_Wo"])
    arrays["L1_wqT"] = plain(np.asarray(inputs["L1_ffn_w_q"]).T)
    arrays["L1_keysT"] = plain(np.asarray(inputs["L1_ffn_keys"]).transpose(2, 0, 3, 1).reshape(2 * PH * P, KEYS))
    arrays["L1_table"] = plain(np.concatenate([np.asarray(inputs["L1_ffn_w_down"]), np.asarray(inputs["L1_ffn_w_up"])], axis=1))

    lane = np.arange(P)
    arrays["ident"] = np.eye(P, dtype=np.float32)
    arrays["ones"] = np.ones((P, P), np.float32)
    arrays["tri"] = np.triu(np.ones((P, P), np.float32), 1)
    arrays["head_mask"] = np.concatenate([lane[:, None] // DH == lane[None, :] // DH,
                                          lane[:, None] // DH == np.arange(HC)[None, :]], axis=1).astype(np.float32)
    arrays["rank"] = np.tile(E - np.arange(E, dtype=np.float32), (P, 1))
    arrays["tile_start"] = (np.arange(2 * NT + E + 1, dtype=np.float32) * P)[None]
    freq = (1.0 / np.float32(10000.0) ** (np.arange(0, DH, 2, dtype=np.float32) / np.float32(DH))).astype(np.float32)
    angle = np.outer(np.arange(S, dtype=np.float32), freq).astype(np.float32)
    arrays["rope"] = np.stack([np.concatenate([np.cos(angle), np.cos(angle)], 1),
                               np.concatenate([-np.sin(angle), np.sin(angle)], 1)]).astype(np.float32)
    return arrays


def kernel(**inputs):
    import concourse.bacc as bacc
    from concourse.bass_utils import run_bass_kernel_spmd

    nc = bacc.Bacc("TRN2", target_bir_lowering=False, num_devices=1)
    arrays, io = {}, {}
    for name, a in layout(inputs).items():
        arrays[f"in_{name}_dram"] = a
        io[name] = nc.dram_tensor(f"in_{name}_dram", a.shape, mybir.dt.from_np(a.dtype), kind="ExternalInput").ap()
    out = nc.dram_tensor("out_0_dram", (B, S, D), F32, kind="ExternalOutput").ap()
    build(nc, io, out)
    r = run_bass_kernel_spmd(nc, [arrays], core_ids=[0])
    return r.results[0]["out_0_dram"]
```

```python
from contextlib import ExitStack

import numpy as np

import concourse.bass as bass
from concourse import mybir

F32 = mybir.dt.float32
BF16 = mybir.dt.bfloat16
I32 = mybir.dt.int32
U32 = mybir.dt.uint32
ALU = mybir.AluOpType
ACT = mybir.ActivationFunctionType
AX = mybir.AxisListType

P = 128
B, S, D = 2, 2048, 256
T = B * S
NT = T // P
G = 4
GT = G * P
NG = NT // G
GB = NG // B
DC = D // P
H, DH = 16, 16
HC = P // DH
E, F = 8, 512
FC = F // P
KEYS, PH = 64, 8
SIMS = 2 * PH * KEYS
LN_EPS = 1e-5
DENOM_EPS = 1e-6
GATE_MIN = 0.25
SA, CA, GA, SB, CB, GBI = range(6)


class Order:

    def __init__(self, eng, sem):
        self.eng, self.sem, self.base, self.n = eng, sem, 0, 0

    def mark(self, instruction):
        self.n += 1
        return instruction.then_inc(self.sem, 1)

    def settle(self):
        self.eng.wait_ge(self.sem, self.base + self.n)

    def settle_alone(self):
        wait_alone(self.eng, self.sem, self.base + self.n)

    def turn(self, i, start, per):
        self.base, self.n = i * per + start, 0


def wait_alone(eng, sem, value):
    r = eng.to_reg(value)
    eng.wait_ge(sem, 1)
    eng.wait_ge(sem, r)


class Kernel:
    pass


def setup(nc, ctx, io):
    k = Kernel()
    k.nc, k.ctx, k.io = nc, ctx, io

    def sb(name, shape, dt=F32):
        return ctx.enter_context(nc.sbuf_tensor(name, shape, dt))

    k.x = sb("x_res", [P, NT, D])
    k.mods = sb("mods", [P, B, 6, D])
    k.ident = sb("ident", [P, P])
    k.identb = sb("identb", [P, P], BF16)
    k.eps = sb("eps", [P, 1])
    k.modrow_dram = [nc.dram_tensor(f"modrow_dram{l}", [B, 6, D], F32, kind="Internal").ap() for l in range(2)]
    k.h_dram = nc.dram_tensor("h_dram", [T, D], F32, kind="Internal").ap()
    k.qT_dram = nc.dram_tensor("qT_dram", [DC, P, T], F32, kind="Internal").ap()
    return k


def stage_modulation(k):
    nc, io = k.nc, k.io
    with ExitStack() as ctx:
        def sb(name, shape, dt=F32):
            return ctx.enter_context(nc.sbuf_tensor(name, shape, dt))

        def sem(name):
            return k.ctx.enter_context(nc.semaphore(name))

        cT = sb("cT", [P, 2, DC, B])
        scT = sb("scT", [P, 2, DC, B])
        wmod = sb("wmod", [P, 2, DC, 6 * D])
        row = sb("modrow", [B, 2, 6, D])
        sign = sb("modsign", [B, 2, 2, D])
        neg = sb("modneg", [B, 2, 2, D])
        ps = ctx.enter_context(nc.psum_tensor("mod_ps", [P, 6, 512], F32))
        w_in = [sem(f"m_w_in{l}") for l in range(2)]
        c_in, x_in, id_in = sem("m_c_in"), sem("m_x_in"), sem("m_id_in")
        silu_done, mod_done, evac_done = sem("m_silu"), sem("m_mod"), sem("m_evac")
        dve_steps, row_ready, row_out, bc_in = sem("m_dve"), sem("m_row"), sem("m_rowout"), sem("m_bc")
        with nc.Block() as block:
            @block.sync
            def _(sp):
                for l in range(2):
                    for c in range(DC):
                        sp.dma_start(cT[:, l, c, :], io[f"L{l}_cT"][c * P:(c + 1) * P, :]).then_inc(c_in, 16)
                for l in range(2):
                    sp.dma_start(wmod[:, l, :, :], io[f"L{l}_wmod"].rearrange("(c p) n -> p c n", p=P)).then_inc(w_in[l], 16)
                sp.dma_start(k.ident[:], io["ident"]).then_inc(id_in, 16)
                sp.dma_start(k.x[:], io["L0_attn_x"].rearrange("b (t p) d -> p (b t) d", p=P)).then_inc(x_in, 16)
                sp.wait_ge(row_ready, 1)
                sp.dma_start(k.modrow_dram[0], row[:, 0, :, :]).then_inc(row_out, 16)
                sp.wait_ge(row_out, 16)
                sp.dma_start(k.mods[:].rearrange("p b m d -> p (b m d)"),
                             k.modrow_dram[0].rearrange("b m d -> (b m d)").partition_broadcast(P)).then_inc(bc_in, 16)
                sp.wait_ge(row_ready, 2)
                sp.dma_start(k.modrow_dram[1], row[:, 1, :, :]).then_inc(row_out, 16)
                sp.wait_ge(row_out, 32)
                sp.wait_ge(bc_in, 16)
                sp.wait_ge(x_in, 16)

            @block.scalar
            def _(act):
                act.wait_ge(c_in, 64)
                nc.scalar.activation(scT[:], cT[:], ACT.Silu).then_inc(silu_done, 1)

            @block.tensor
            def _(pe):
                pe.wait_ge(silu_done, 1)
                for l in range(2):
                    pe.wait_ge(w_in[l], 16)
                    for n in range(3):
                        for c in range(DC):
                            mm = nc.tensor.matmul(ps[0:B, 3 * l + n, :], scT[:, l, c, :], wmod[:, l, c, n * 512:(n + 1) * 512],
                                                  start=(c == 0), stop=(c == DC - 1))
                    mm.then_inc(mod_done, 1)

            @block.vector
            def _(dve):
                o = Order(dve, dve_steps)
                o.mark(nc.vector.memset(k.eps[:], LN_EPS))
                for l in range(2):
                    dve.wait_ge(mod_done, l + 1)
                    o.mark(nc.vector.tensor_copy(row[:, l, :, :].rearrange("b m d -> b (m d)"),
                                                 ps[0:B, 3 * l:3 * l + 3, :].rearrange("b n f -> b (n f)")))
                    o.settle()
                    scales = row[:, l, CA:CB + 1:3, :]
                    gates = row[:, l, GA:GBI + 1:3, :]
                    o.mark(nc.vector.tensor_scalar_add(scales, scales, 1.0))
                    o.mark(nc.vector.tensor_scalar(sign[:, l], gates, 0.0, 2.0, ALU.is_ge, ALU.mult))
                    o.mark(nc.vector.scalar_tensor_tensor(neg[:, l], gates, -1.0, gates, ALU.mult, ALU.max))
                    o.settle()
                    o.mark(nc.vector.tensor_scalar_max(neg[:, l], neg[:, l], GATE_MIN))
                    o.settle()
                    nc.vector.scalar_tensor_tensor(gates, sign[:, l], 1.0, neg[:, l], ALU.subtract, ALU.mult).then_inc(row_ready, 1)
                dve.wait_ge(id_in, 16)
                nc.vector.tensor_copy(k.identb[:], k.ident[:])


def stage_linear_attention_sums(k):
    nc, io = k.nc, k.io
    with ExitStack() as ctx:
        def sb(name, shape, dt=F32):
            return ctx.enter_context(nc.sbuf_tensor(name, shape, dt))

        def psum(name, shape):
            return ctx.enter_context(nc.psum_tensor(name, shape, F32))

        def sem(name):
            return k.ctx.enter_context(nc.semaphore(name))

        KV = P + 1
        wq = sb("wq", [P, DC, D])
        wkv = sb("wkv", [P, DC, 2 * D])
        bq = sb("bq", [P, DC])
        bkv = sb("bkv", [P, 2 * D])
        stats = sb("a_stats", [P, G, 6])
        mv = sb("a_mv", [P, G, 2])
        std = sb("a_std", [P, G])
        xn = sb("a_xn", [P, G, D])
        h = sb("a_h", [P, G, D])
        hT = sb("a_hT", [P, DC, GT])
        qT = sb("a_qT", [P, DC, GT])
        kv = sb("a_kv", [P, 2, 2 * D + 1])
        hT_ps = psum("hT_ps", [P, DC, 512])
        q_ps = psum("q_ps", [P, DC, 512])
        kv_ps = psum("kv_ps", [P, 2, 512])
        sum_ps = psum("sum_ps", [P, DC, 512])

        w_in, const_ready = sem("a_w_in"), sem("a_const")
        dve_steps, stats_ready, std_ready, h_ready = sem("a_dve"), sem("a_stats"), sem("a_std"), sem("a_h")
        hT_done, hT_ready, q_done, q_ready = sem("a_hT"), sem("a_hTr"), sem("a_q"), sem("a_qr")
        kv_done, kv_added, kv_ready = sem("a_kvd"), sem("a_kva"), sem("a_kvr")
        sums_done, sums_read = sem("a_sd"), sem("a_sr")
        h_out, q_out = sem("a_ho"), sem("a_qo")
        W_IN = 16 * (3 + DC + 2)
        with nc.Block() as block:
            @block.sync
            def _(sp):
                sp.dma_start(wq[:], io["L0_WqT"].rearrange("(c p) n -> p c n", p=P)).then_inc(w_in, 16)
                sp.dma_start(wkv[:, :, 0:D], io["L0_WkT"].rearrange("(c p) n -> p c n", p=P)).then_inc(w_in, 16)
                sp.dma_start(wkv[:, :, D:2 * D], io["L0_WvT"].rearrange("(c p) n -> p c n", p=P)).then_inc(w_in, 16)
                for c in range(DC):
                    sp.dma_start(bq[:, c:c + 1], io["L0_attn_bq"][c * P:(c + 1) * P].rearrange("(p o) -> p o", o=1)).then_inc(w_in, 16)
                sp.dma_start(bkv[:, 0:D], io["L0_attn_bk"].partition_broadcast(P)).then_inc(w_in, 16)
                sp.dma_start(bkv[:, D:2 * D], io["L0_attn_bv"].partition_broadcast(P)).then_inc(w_in, 16)
                sp.nop().then_inc(h_out, 16)
                sp.nop().then_inc(q_out, 16)
                with sp.Fori(0, NG) as g:
                    sp.wait_ge(h_ready, g + 1)
                    sp.dma_start(k.h_dram[bass.ts(g, GT), :].rearrange("(s p) d -> p s d", p=P), h[:]).then_inc(h_out, 16)
                    wait_alone(sp, q_ready, DC * (g + 1))
                    sp.dma_start(k.qT_dram[:, :, bass.ts(g, GT)].rearrange("c p n -> p c n"), qT[:]).then_inc(q_out, 16)
                sp.wait_ge(h_out, 16 * (NG + 1))
                sp.wait_ge(q_out, 16 * (NG + 1))

            @block.vector
            def _(dve):
                o = Order(dve, dve_steps)
                nc.vector.memset(k.kvsum[:], 0.0).then_inc(const_ready, 1)
                nc.vector.memset(kv[:, :, 2 * D:], 1.0).then_inc(const_ready, 1)
                dve.wait_ge(const_ready, 2)
                LN_STEPS = G + 1 + G + 1

                def statistics(g):
                    for s in range(G):
                        o.mark(nc.vector.bn_stats(stats[:, s, :], k.x[:, bass.ds(g * G + s, 1), :]))
                    o.settle_alone()
                    for s in range(G):
                        nc.vector.bn_aggr(mv[:, s, :], stats[:, s, :]).then_inc(stats_ready, 1)

                def normalise(g):
                    dve.wait_ge(std_ready, g + 1)
                    o.mark(nc.vector.reciprocal(std[:], std[:]))
                    o.settle()
                    for s in range(G):
                        o.mark(nc.vector.tensor_scalar(xn[:, s, :], k.x[:, bass.ds(g * G + s, 1), :], mv[:, s, 0:1],
                                                       std[:, s:s + 1], ALU.subtract, ALU.mult))

                def scale(g):
                    o.settle()
                    by = k.mods[:, bass.ds(g // GB, 1), CA, :].to_broadcast([P, G, D])
                    o.mark(nc.vector.tensor_tensor(xn[:], xn[:], by, ALU.mult))

                def shift(g):
                    o.settle()
                    dve.wait_ge(h_out, 16 * (g + 1))
                    by = k.mods[:, bass.ds(g // GB, 1), SA, :].to_broadcast([P, G, D])
                    nc.vector.tensor_tensor(h[:], xn[:], by, ALU.add).then_inc(h_ready, 1)

                def tile(g, s):
                    dve.wait_ge(kv_done, g * G + s + 1)
                    if s >= 2:
                        dve.wait_ge(sums_done, g * G + s - 1)
                    nc.vector.tensor_tensor(kv[:, s % 2, 0:2 * D], kv_ps[:, s % 2, :], bkv[:], ALU.add).then_inc(kv_added, 1)
                    dve.wait_ge(kv_added, g * G + s + 1)
                    nc.vector.tensor_scalar_max(kv[:, s % 2, 0:D], kv[:, s % 2, 0:D], 0.0).then_inc(kv_ready, 1)

                def collect(g):
                    dve.wait_ge(sums_done, (g + 1) * G)
                    acc = k.kvsum[:, bass.ds(g // GB, 1), :, :]
                    nc.vector.tensor_tensor(acc, sum_ps[:, :, 0:KV], acc, ALU.add).then_inc(sums_read, 1)
                    dve.wait_ge(sums_read, g + 1)

                statistics(0)
                normalise(0)
                scale(0)
                shift(0)
                dve.wait_ge(w_in, W_IN)
                with dve.Fori(0, NG - 1) as g:
                    o.turn(g, LN_STEPS, LN_STEPS)
                    statistics(g + 1)
                    tile(g, 0)
                    normalise(g + 1)
                    tile(g, 1)
                    scale(g + 1)
                    tile(g, 2)
                    shift(g + 1)
                    tile(g, 3)
                    collect(g)
                    assert o.n == LN_STEPS
                for s in range(G):
                    tile(NG - 1, s)
                collect(NG - 1)

            @block.scalar
            def _(act):

                def deviation(g):
                    act.wait_ge(stats_ready, (g + 1) * G)
                    nc.scalar.activation(std[:], mv[:, :, 1], ACT.Sqrt, bias=k.eps[:, 0:1]).then_inc(std_ready, 1)

                def turned(g):
                    act.wait_ge(hT_done, g + 1)
                    nc.scalar.copy(hT[:], hT_ps[:]).then_inc(hT_ready, 1)

                def queries(g):
                    act.wait_ge(q_done, g + 1)
                    act.wait_ge(q_out, 16 * (g + 1))
                    for c in range(DC):
                        nc.scalar.activation(qT[:, c, :], q_ps[:, c, :], ACT.Relu, bias=bq[:, c:c + 1]).then_inc(q_ready, 1)

                deviation(0)
                turned(0)
                act.wait_ge(w_in, W_IN)
                with act.Fori(0, NG - 1) as g:
                    deviation(g + 1)
                    queries(g)
                    turned(g + 1)
                queries(NG - 1)

            @block.tensor
            def _(pe):

                def transposes(g):
                    pe.wait_ge(h_ready, g + 1)
                    for c in range(DC):
                        for s in range(G):
                            mm = nc.tensor.transpose(hT_ps[:, c, s * P:(s + 1) * P], h[:, s, c * P:(c + 1) * P], k.ident[:])
                    mm.then_inc(hT_done, 1)

                def queries(g):
                    pe.wait_ge(hT_ready, g + 1)
                    if not (isinstance(g, int) and g == 0):
                        pe.wait_ge(q_ready, DC * g)
                    for m in range(DC):
                        for c in range(DC):
                            mm = nc.tensor.matmul(q_ps[:, m, :], wq[:, c, m * P:(m + 1) * P], hT[:, c, :],
                                                  start=(c == 0), stop=(c == DC - 1))
                    mm.then_inc(q_done, 1)

                def sums(g, s):
                    pe.wait_ge(kv_ready, g * G + s + 1)
                    for c in range(DC):
                        for lo, hi, col in ((0, P, D + c * P), (P, KV, 2 * D)):
                            mm = nc.tensor.matmul(sum_ps[:, c, lo:hi], kv[:, s % 2, c * P:(c + 1) * P],
                                                  kv[:, s % 2, col:col + hi - lo], start=(s == 0 and lo == 0),
                                                  stop=(s == G - 1), skip_group_check=True)
                    mm.then_inc(sums_done, 1)

                def keys_values(g, s):
                    if s >= 2:
                        pe.wait_ge(kv_added, g * G + s - 1)
                    for c in range(DC):
                        mm = nc.tensor.matmul(kv_ps[:, s % 2, :], hT[:, c, s * P:(s + 1) * P], wkv[:, c, :],
                                              start=(c == 0), stop=(c == DC - 1))
                    mm.then_inc(kv_done, 1)

                def group(g, ahead):
                    for s in range(G):
                        keys_values(g, s)
                        if s == 1 and not (isinstance(g, int) and g == 0):
                            pe.wait_ge(sums_read, g)
                        if s >= 1:
                            sums(g, s - 1)
                    if ahead:
                        transposes(g + 1)
                    sums(g, G - 1)
                    if ahead:
                        queries(g + 1)

                transposes(0)
                pe.wait_ge(w_in, W_IN)
                queries(0)
                group(0, True)
                with pe.Fori(1, NG - 1) as g:
                    group(g, True)
                group(NG - 1, False)


def scratch(k, ctx):
    nc = k.nc

    def sb(name, shape, dt=F32):
        return ctx.enter_context(nc.sbuf_tensor(name, shape, dt))

    def psum(name, shape, dt=F32):
        return ctx.enter_context(nc.psum_tensor(name, shape, dt))

    def sem(name):
        return k.ctx.enter_context(nc.semaphore(name))

    return sb, psum, sem


def stage_linear_attention_apply(k):
    nc, io = k.nc, k.io
    with ExitStack() as ctx:
        sb, psum, sem = scratch(k, ctx)
        mask = sb("b_mask", [P, P + HC])
        kvd = sb("b_kvd", [P, B, DC, P + HC])
        router = sb("b_router", [P, DC, E])
        gamma = sb("b_gamma", [P, B, D])
        beta = sb("b_beta", [P, B, D])
        h = sb("b_h", [P, G, D])
        qT = sb("b_qT", [P, DC, GT])
        rden = sb("b_rden", [P, G, H])
        y = sb("b_y", [P, G, D])
        stats = sb("b_stats", [P, G, 6])
        mv = sb("b_mv", [P, G, 2])
        std = sb("b_std", [P, G])
        xn = sb("b_xn", [P, G, D])
        h2 = sb("b_h2", [P, G, D])
        h2T = sb("b_h2T", [P, DC, GT])
        ctx_ps = psum("ctx_ps", [P, G, 512])
        hT_ps = psum("b_hT_ps", [P, DC, 512])
        lg_ps = psum("lg_ps", [P, 512])

        w_in = sem("b_w_in")
        dve_steps, kvd_ready, beta_ready, x_based = sem("b_dve"), sem("b_kvd"), sem("b_beta"), sem("b_xb")
        h_in, q_in, ctx_done, ctx_read, h_used = sem("b_hin"), sem("b_qin"), sem("b_ctx"), sem("b_ctxr"), sem("b_hu")
        stats_ready, std_ready, h2_ready, h2_out = sem("b_stats"), sem("b_std"), sem("b_h2"), sem("b_h2o")
        hT_done, hT_ready, lg_done, lg_read = sem("b_hT"), sem("b_hTr"), sem("b_lg"), sem("b_lgr")

        with nc.Block() as block:
            @block.sync
            def _(sp):
                sp.dma_start(mask[:], io["head_mask"]).then_inc(w_in, 16)
                sp.dma_start(router[:], io["L0_router"].rearrange("(c p) n -> p c n", p=P)).then_inc(w_in, 16)
                for b in range(B):
                    sp.dma_start(gamma[:, b, :], io["L0_attn_gamma"].partition_broadcast(P)).then_inc(w_in, 16)
                    sp.dma_start(beta[:, b, :], io["L0_attn_beta"].partition_broadcast(P)).then_inc(w_in, 16)
                sp.nop().then_inc(h2_out, 16)

                def load(g):
                    sp.wait_ge(h_used, g + 1)
                    sp.dma_start(h[:], k.h_dram[bass.ts(g, GT), :].rearrange("(s p) d -> p s d", p=P)).then_inc(h_in, 16)
                    wait_alone(sp, ctx_done, g + 1)
                    sp.dma_start(qT[:], k.qT_dram[:, :, bass.ts(g, GT)].rearrange("c p n -> p c n")).then_inc(q_in, 16)

                def store(g):
                    sp.wait_ge(h2_ready, g + 1)
                    sp.dma_start(k.h2_dram[bass.ts(g, GT), :].rearrange("(s p) d -> p s d", p=P), h2[:]).then_inc(h2_out, 16)

                def weights(e):
                    if not isinstance(e, int):
                        sp.wait_ge(k.w_moe_in, 48 * e)
                    for n, t in (("L0_gate", k.wg), ("L0_up", k.wu), ("L0_down", k.wd)):
                        sp.dma_start(t[:, bass.ds(e, 1)].rearrange("p e c f -> p (e c) f"),
                                     io[n][bass.ds(e, 1)].rearrange("e (c p) f -> p (e c) f", p=P)).then_inc(k.w_moe_in, 16)

                load(0)
                weights(0)
                with sp.Fori(1, NG) as g:
                    load(g)
                    weights(g)
                    store(g - 1)
                store(NG - 1)
                sp.wait_ge(k.w_moe_in, 48 * E)
                sp.wait_ge(h2_out, 16 * (NG + 1))

            @block.gpsimd
            def _(pool):
                pool.wait_ge(beta_ready, 1)
                with pool.Fori(0, NG) as g:
                    by = beta[:, bass.ds(g // GB, 1), :].to_broadcast([P, G, D])
                    xg = k.x[:, bass.ds(g * G, G), :]
                    nc.gpsimd.tensor_tensor(xg, xg, by, ALU.add).then_inc(x_based, 1)

            @block.vector
            def _(dve):
                o = Order(dve, dve_steps)
                dve.wait_ge(w_in, 16 * (2 + 2 * B))
                for b in range(B):
                    for c in range(DC):
                        nc.vector.tensor_tensor(kvd[:, b, c, 0:P], k.kvsum[:, b, c, 0:P], mask[:, 0:P], ALU.mult).then_inc(kvd_ready, 1)
                        nc.vector.tensor_scalar_mul(kvd[:, b, c, P:], mask[:, P:], k.kvsum[:, b, c, P:P + 1]).then_inc(kvd_ready, 1)
                    o.mark(nc.vector.tensor_tensor(gamma[:, b, :], gamma[:, b, :], k.mods[:, b, GA, :], ALU.mult))
                nc.vector.tensor_tensor(beta[:], beta[:], k.mods[:, :, GA, :], ALU.mult).then_inc(beta_ready, 1)
                START, TURN = B, 5 + 2 * (G + 1 + G)

                def normalise(src, turn):
                    for s in range(G):
                        o.mark(nc.vector.bn_stats(stats[:, s, :], src(s)))
                    o.settle_alone()
                    for s in range(G):
                        nc.vector.bn_aggr(mv[:, s, :], stats[:, s, :]).then_inc(stats_ready, 1)
                    dve.wait_ge(std_ready, turn + 1)
                    o.mark(nc.vector.reciprocal(std[:], std[:]))
                    o.settle()
                    for s in range(G):
                        o.mark(nc.vector.tensor_scalar(xn[:, s, :], src(s), mv[:, s, 0:1], std[:, s:s + 1], ALU.subtract, ALU.mult))
                    o.settle()

                def logits(g):
                    dve.wait_ge(lg_done, g + 1)
                    nc.vector.tensor_copy(k.logits[:, bass.ds(g * G, G), :], lg_ps[:, 0:G * E].rearrange("p (s e) -> p s e", e=E)).then_inc(lg_read, 1)

                def group(g):
                    o.turn(g, START, TURN)
                    dve.wait_ge(ctx_done, g + 2)
                    den = ctx_ps[:, :, D:D + H]
                    o.mark(nc.vector.tensor_scalar_max(rden[:], den, DENOM_EPS))
                    o.settle()
                    o.mark(nc.vector.reciprocal(rden[:], rden[:]))
                    o.settle()
                    nc.vector.tensor_tensor(y[:].rearrange("p s (h d) -> p s h d", d=DH),
                                            ctx_ps[:, :, 0:D].rearrange("p s (h d) -> p s h d", d=DH),
                                            rden[:].unsqueeze(3).to_broadcast([P, G, H, DH]), ALU.mult).then_inc(ctx_read, 1)
                    dve.wait_ge(ctx_read, g + 1)
                    dve.wait_ge(h_in, 16 * (g + 1))
                    nc.vector.tensor_tensor(y[:], y[:], h[:], ALU.add).then_inc(h_used, 1)
                    dve.wait_ge(h_used, g + 2)
                    normalise(lambda s: y[:, s, :], 2 * g)
                    by = gamma[:, bass.ds(g // GB, 1), :].to_broadcast([P, G, D])
                    xg = k.x[:, bass.ds(g * G, G), :]
                    o.mark(nc.vector.tensor_tensor(xn[:], xn[:], by, ALU.mult))
                    o.settle()
                    dve.wait_ge(x_based, g + 1)
                    o.mark(nc.vector.tensor_tensor(xg, xg, xn[:], ALU.add))
                    if not (isinstance(g, int) and g == 0):
                        logits(g - 1)
                    o.settle_alone()
                    normalise(lambda s: k.x[:, bass.ds(g * G + s, 1), :], 2 * g + 1)
                    o.mark(nc.vector.tensor_tensor(xn[:], xn[:], k.mods[:, bass.ds(g // GB, 1), CB, :].to_broadcast([P, G, D]), ALU.mult))
                    o.settle()
                    dve.wait_ge(h2_out, 16 * (g + 1))
                    dve.wait_ge(hT_done, g + 1)
                    nc.vector.tensor_tensor(h2[:], xn[:], k.mods[:, bass.ds(g // GB, 1), SB, :].to_broadcast([P, G, D]), ALU.add).then_inc(h2_ready, 1)
                    assert o.n == TURN, (o.n, TURN)

                group(0)
                with dve.Fori(1, NG) as g:
                    group(g)
                logits(NG - 1)

            @block.scalar
            def _(act):
                with act.Fori(0, NG) as g:
                    for turn in range(2):
                        act.wait_ge(stats_ready, (2 * g + turn + 1) * G)
                        nc.scalar.activation(std[:], mv[:, :, 1], ACT.Sqrt, bias=k.eps[:, 0:1]).then_inc(std_ready, 1)
                    act.wait_ge(hT_done, g + 2)
                    nc.scalar.copy(h2T[:], hT_ps[:]).then_inc(hT_ready, 1)

            @block.tensor
            def _(pe):
                pe.wait_ge(w_in, 16 * (2 + 2 * B))
                pe.wait_ge(kvd_ready, B * DC * 2)
                pe.nop().then_inc(ctx_done, 1)
                pe.nop().then_inc(h_used, 1)
                pe.nop().then_inc(hT_done, 1)
                pe.nop().then_inc(lg_read, 1)

                def context(g):
                    pe.wait_ge(q_in, 16 * (g + 1))
                    pe.wait_ge(h_used, g + 1)
                    for s in range(G):
                        for c in range(DC):
                            q = qT[:, c, s * P:(s + 1) * P]
                            nc.tensor.matmul(ctx_ps[:, s, c * P:(c + 1) * P], q, kvd[:, bass.ds(g // GB, 1), c, 0:P],
                                             start=True, stop=True, skip_group_check=True)
                            mm = nc.tensor.matmul(ctx_ps[:, s, D + c * HC:D + (c + 1) * HC], q, kvd[:, bass.ds(g // GB, 1), c, P:],
                                                  start=True, stop=True, skip_group_check=True)
                    mm.then_inc(ctx_done, 1)

                def route(g):
                    pe.wait_ge(h2_ready, g + 1)
                    for c in range(DC):
                        for s in range(G):
                            mm = nc.tensor.transpose(hT_ps[:, c, s * P:(s + 1) * P], h2[:, s, c * P:(c + 1) * P], k.ident[:])
                    mm.then_inc(hT_done, 1)
                    pe.wait_ge(hT_ready, g + 1)
                    pe.wait_ge(lg_read, g + 1)
                    for s in range(G):
                        for c in range(DC):
                            mm = nc.tensor.matmul(lg_ps[:, s * E:(s + 1) * E], h2T[:, c, s * P:(s + 1) * P], router[:, c, :],
                                                  start=(c == 0), stop=(c == DC - 1), skip_group_check=True)
                    mm.then_inc(lg_done, 1)

                context(0)
                with pe.Fori(0, NG - 1) as g:
                    context(g + 1)
                    route(g)
                route(NG - 1)


def stage_route(k):
    nc, io = k.nc, k.io
    with ExitStack() as ctx:
        sb, psum, sem = scratch(k, ctx)
        tri = sb("r_tri", [P, P])
        ones = sb("r_ones", [P, P])
        rank = sb("r_rank", [P, E])
        start = sb("r_start", [1, k.COLS])
        m = sb("r_m", [P, 4, NT])
        prob = sb("r_prob", [P, NT, E])
        key = sb("r_key", [P, NT, E])
        hot = sb("r_hot", [P, 2, NT, E])
        both = sb("r_both", [P, NT, E])
        run = sb("r_run", [P, 2, NT, E])
        cnt = sb("r_cnt", [P, 4, E])
        cnti = sb("r_cnti", [P, E], I32)
        slotf = sb("r_slotf", [P, NT, 2])
        cmp = sb("r_cmp", [1, k.COLS, E])
        eidf = sb("r_eidf", [1, k.COLS])
        iota = sb("r_iota", [P, P])
        ids = sb("r_ids", [P, NT])
        tilei = sb("r_tilei", [P, NT, 2], I32)
        tilef = sb("r_tilef", [P, NT, 2])
        place = sb("r_place", [P, NT, 2])
        at_place = sb("r_at_place", [P, 2, G, P])
        at_tile = sb("r_at_tile", [P, 2, G, k.COLS])
        wq = sb("r_wq", [P, 2 * PH, D])
        keys = sb("r_keys", [P, 2 * PH, KEYS])
        cnt_ps = psum("cnt_ps", [P, 2, NT * E])
        ws_ps = psum("ws_ps", [P, DC, SIMS])
        token_ps = psum("token_ps", [P, 512])
        ws_in, ws_done, ws_ready = sem("r_wsi"), sem("r_wsd"), sem("r_wsr")
        w_in, steps, exped, both_ready, cnt_done = sem("r_w"), sem("r_steps"), sem("r_exp"), sem("r_both"), sem("r_cnt")
        slots_ready = sem("r_slots")
        hot_ready, hot_used, token_ready = sem("r_hr"), sem("r_hu"), sem("r_tok")

        with nc.Block() as block:
            @block.sync
            def _(sp):
                for t, n in ((tri, "tri"), (ones, "ones"), (rank, "rank"), (start, "tile_start"), (iota, "iota"), (ids, "ids")):
                    sp.dma_start(t[:], io[n]).then_inc(w_in, 16)
                sp.dma_start(wq[:], io["L1_wqT"].rearrange("(a p) d -> p a d", p=P)).then_inc(ws_in, 16)
                sp.dma_start(keys[:], io["L1_keysT"].rearrange("(a p) n -> p a n", p=P)).then_inc(ws_in, 16)

            @block.scalar
            def _(act):
                act.wait_ge(exped, 1)
                nc.scalar.activation(prob[:], prob[:], ACT.Exp).then_inc(exped, 1)
                act.wait_ge(exped, 3)
                nc.scalar.activation(k.wts[:, 1, :], m[:, 3, :], ACT.Exp).then_inc(exped, 1)
                for c in range(DC):
                    act.wait_ge(ws_done, c + 1)
                    nc.scalar.copy(k.wsim[:, c, :], ws_ps[:, c, :]).then_inc(ws_ready, 1)
                act.wait_ge(ws_ready, DC)

            @block.tensor
            def _(pe):
                pe.wait_ge(w_in, 96)
                pe.wait_ge(both_ready, 1)
                flat = both[:].rearrange("p t e -> p (t e)")
                nc.tensor.matmul(cnt_ps[:, 0, :], tri[:], flat, start=True, stop=True, skip_group_check=True)
                nc.tensor.matmul(cnt_ps[:, 1, :], ones[:], flat, start=True, stop=True, skip_group_check=True).then_inc(cnt_done, 1)
                pe.wait_ge(ws_in, 32)
                for c in range(DC):
                    for a in range(2 * PH):
                        mm = nc.tensor.matmul(ws_ps[:, c, a * KEYS:(a + 1) * KEYS], wq[:, a, c * P:(c + 1) * P], keys[:, a, :],
                                              start=True, stop=True, skip_group_check=True)
                    mm.then_inc(ws_done, 1)

                def place_tokens(g, first):
                    for c in range(2):
                        pe.wait_ge(hot_ready, g * 2 + c + 1)
                        for s in range(G):
                            mm = nc.tensor.matmul(token_ps[:, 0:k.COLS], at_place[:, c, s, :], at_tile[:, c, s, :],
                                                  start=first and c == 0 and s == 0, stop=True, skip_group_check=True)
                        mm.then_inc(hot_used, 1)

                place_tokens(0, True)
                with pe.Fori(1, NG) as g:
                    place_tokens(g, False)

            @block.vector
            def _(dve):
                o = Order(dve, steps)

                def step(instruction):
                    o.mark(instruction)
                    o.settle()

                V = nc.vector
                wide = [P, NT, E]
                dve.wait_ge(w_in, 96)
                step(V.reduce_max(m[:, 0, :], k.logits[:], AX.X))
                V.tensor_tensor(prob[:], k.logits[:], m[:, 0, :].unsqueeze(2).to_broadcast(wide), ALU.subtract).then_inc(exped, 1)
                dve.wait_ge(exped, 2)
                step(V.reduce_sum(m[:, 1, :], prob[:], AX.X))
                step(V.reciprocal(m[:, 1, :], m[:, 1, :]))
                step(V.tensor_tensor(prob[:], prob[:], m[:, 1, :].unsqueeze(2).to_broadcast(wide), ALU.mult))
                for c in range(2):
                    top = m[:, 2 * c, :]
                    step(V.reduce_max(top, prob[:], AX.X))
                    step(V.tensor_tensor(key[:], prob[:], top.unsqueeze(2).to_broadcast(wide), ALU.is_equal))
                    step(V.tensor_tensor(key[:], key[:], rank[:].unsqueeze(1).to_broadcast(wide), ALU.mult))
                    step(V.reduce_max(m[:, 3, :], key[:], AX.X))
                    step(V.tensor_tensor(hot[:, c], key[:], m[:, 3, :].unsqueeze(2).to_broadcast(wide), ALU.is_equal))
                    if c == 0:
                        step(V.scalar_tensor_tensor(prob[:], hot[:, 0], -2.0, prob[:], ALU.mult, ALU.add))
                V.tensor_tensor(both[:], hot[:, 0], hot[:, 1], ALU.add).then_inc(both_ready, 1)
                V.tensor_tensor(m[:, 3, :], m[:, 2, :], m[:, 0, :], ALU.subtract).then_inc(exped, 1)
                dve.wait_ge(exped, 4)
                step(V.tensor_scalar_add(m[:, 1, :], k.wts[:, 1, :], 1.0))
                step(V.reciprocal(k.wts[:, 0, :], m[:, 1, :]))
                step(V.tensor_tensor(k.wts[:, 1, :], k.wts[:, 1, :], k.wts[:, 0, :], ALU.mult))
                dve.wait_ge(cnt_done, 1)
                counts = cnt_ps[:, 1, :].rearrange("p (t e) -> p t e", e=E)
                step(V.tensor_copy(run[:, 0], counts))
                at, by = 0, 1
                while by < NT:
                    o.mark(V.tensor_copy(run[:, 1 - at, 0:by, :], run[:, at, 0:by, :]))
                    step(V.tensor_tensor(run[:, 1 - at, by:, :], run[:, at, by:, :], run[:, at, 0:NT - by, :], ALU.add))
                    at, by = 1 - at, 2 * by
                step(V.tensor_scalar_add(cnt[:, 0, :], run[:, at, NT - 1, :], float(P - 1)))
                step(V.tensor_copy(cnti[:], cnt[:, 0, :]))
                step(V.tensor_scalar(cnti[:], cnti[:], 7, 7, ALU.arith_shift_right, ALU.logical_shift_left))
                step(V.tensor_copy(cnt[:, 3, :], cnti[:]))
                step(V.tensor_copy(cnt[:, 0, :], cnt[:, 3, :]))
                a, by = 0, 1
                while by < E:
                    o.mark(V.tensor_copy(cnt[:, 1 - a, 0:by], cnt[:, a, 0:by]))
                    step(V.tensor_tensor(cnt[:, 1 - a, by:], cnt[:, a, by:], cnt[:, a, 0:E - by], ALU.add))
                    a, by = 1 - a, 2 * by
                end = cnt[:, a, :]
                step(V.tensor_tensor(cnt[:, 2, :], end, cnt[:, 3, :], ALU.subtract))
                step(V.tensor_tensor(run[:, at], run[:, at], counts, ALU.subtract))
                step(V.tensor_tensor(run[:, at], run[:, at], cnt_ps[:, 0, :].rearrange("p (t e) -> p t e", e=E), ALU.add))
                step(V.tensor_tensor(run[:, at], run[:, at], cnt[:, 2, :].unsqueeze(1).to_broadcast(wide), ALU.add))
                for c in range(2):
                    step(V.tensor_tensor(key[:], hot[:, c], run[:, at], ALU.mult))
                    step(V.reduce_sum(slotf[:, :, c], key[:], AX.X))
                step(V.tensor_copy(k.slots[:], slotf[:]))
                row = [1, k.COLS, E]
                step(V.tensor_tensor(cmp[:], start[:].unsqueeze(2).to_broadcast(row), end[0:1, :].unsqueeze(1).to_broadcast(row), ALU.is_ge))
                step(V.reduce_sum(eidf[:], cmp[:], AX.X))
                step(V.tensor_scalar_min(eidf[:], eidf[:], float(E - 1)))
                step(V.tensor_copy(k.eid[:], eidf[:]))
                step(V.tensor_scalar(tilei[:], k.slots[:], 7, None, ALU.arith_shift_right))
                step(V.tensor_copy(tilef[:], tilei[:]))
                step(V.scalar_tensor_tensor(place[:], tilef[:], -float(P), slotf[:], ALU.mult, ALU.add))

                def one_hot(g, first):
                    for c in range(2):
                        if not first:
                            dve.wait_ge(hot_used, g * 2 + c - 1)
                        for s in range(G):
                            t = bass.ds(g * G + s, 1)
                            V.tensor_scalar(at_place[:, c, s, :], iota[:], place[:, t, c], None, ALU.is_equal)
                        for s in range(G):
                            t = bass.ds(g * G + s, 1)
                            hot_tile = V.tensor_scalar(at_tile[:, c, s, :], iota[:, 0:k.COLS], tilef[:, t, c], ids[:, t], ALU.is_equal, ALU.mult)
                        hot_tile.then_inc(hot_ready, 1)

                one_hot(0, True)
                with dve.Fori(1, NG) as g:
                    one_hot(g, False)
                dve.wait_ge(hot_used, 2 * NG)
                V.tensor_copy(k.token[:], token_ps[:, 0:k.COLS]).then_inc(token_ready, 1)


def stage_experts(k):
    nc = k.nc
    with ExitStack() as ctx:
        sb, psum, sem = scratch(k, ctx)
        X = sb("e_x", [P, D])
        sl = sb("e_sl", [P, 1], I32)
        XT = sb("e_xT", [P, DC, P])
        act_g = sb("e_silu", [P, F])
        fuse = sb("e_fuse", [P, F])
        fuseT = sb("e_fuseT", [P, FC, P])
        Y = sb("e_y", [P, D])
        xT_ps = psum("e_xT_ps", [P, DC, P])
        g_ps = psum("e_g_ps", [P, F])
        u_ps = psum("e_u_ps", [P, F])
        fT_ps = psum("e_fT_ps", [P, FC, P])
        y_ps = psum("e_y_ps", [P, 512])
        sl_ready = sem("e_sl")
        x_in, xT_done, xT_ready = sem("e_xin"), sem("e_xTd"), sem("e_xTr")
        g_done, u_done, silu_done, fuse_ready = sem("e_gd"), sem("e_ud"), sem("e_sd"), sem("e_fr")
        fT_done, fT_ready, y_done, y_ready, y_out = sem("e_fTd"), sem("e_fTr"), sem("e_yd"), sem("e_yr"), sem("e_yo")
        TILES = k.TILES

        with nc.Block() as block:
            @block.gpsimd
            def _(pool):
                def gather(j):
                    wait_alone(pool, sl_ready, j + 1)
                    nc.gpsimd.indirect_dma_start(X[:], None, k.h2_dram, bass.IndirectOffsetOnAxis(ap=sl[:, 0:1], axis=0)).then_inc(x_in, 16)

                gather(0)
                with pool.Fori(0, TILES) as j:
                    pool.wait_ge(xT_done, j + 1)
                    gather(j + 1)

            @block.tensor
            def _(pe):
                pe.wait_ge(k.w_moe_in, 48 * E)

                def transpose_x(j):
                    pe.wait_ge(x_in, 16 * (j + 1))
                    for c in range(DC):
                        mm = nc.tensor.transpose(xT_ps[:, c, :], X[:, c * P:(c + 1) * P], k.ident[:])
                    mm.then_inc(xT_done, 1)

                def into(j):
                    e = pe.value_load(k.eid[0:1, bass.ds(j, 1)], min_val=0, max_val=E - 1)
                    pe.wait_ge(xT_ready, j + 1)
                    for ps, w, done in ((g_ps, k.wg, g_done), (u_ps, k.wu, u_done)):
                        for c in range(DC):
                            mm = nc.tensor.matmul(ps[:], XT[:, c, :], w[:, bass.ds(e, 1), c, :], start=(c == 0), stop=(c == DC - 1))
                        mm.then_inc(done, 1)

                def out_of(j, first):
                    e = pe.value_load(k.eid[0:1, bass.ds(j, 1)], min_val=0, max_val=E - 1)
                    pe.wait_ge(fT_ready, j + 1)
                    if not first:
                        pe.wait_ge(y_ready, j)
                    for c in range(FC):
                        mm = nc.tensor.matmul(y_ps[:, 0:D], fuseT[:, c, :], k.wd[:, bass.ds(e, 1), c, :], start=(c == 0), stop=(c == FC - 1))
                    mm.then_inc(y_done, 1)

                def transpose_fuse(j):
                    pe.wait_ge(fuse_ready, j + 1)
                    for c in range(FC):
                        mm = nc.tensor.transpose(fT_ps[:, c, :], fuse[:, c * P:(c + 1) * P], k.ident[:])
                    mm.then_inc(fT_done, 1)

                transpose_x(0)
                into(0)
                transpose_x(1)
                transpose_fuse(0)
                into(1)
                out_of(0, True)
                transpose_x(2)
                transpose_fuse(1)
                with pe.Fori(2, TILES) as j:
                    into(j)
                    out_of(j - 1, False)
                    transpose_x(j + 1)
                    transpose_fuse(j)
                out_of(TILES - 1, False)

            @block.scalar
            def _(act):
                def silu(j):
                    act.wait_ge(g_done, j + 1)
                    nc.scalar.activation(act_g[:], g_ps[:], ACT.Silu).then_inc(silu_done, 1)

                def store(j, first):
                    act.wait_ge(y_done, j + 1)
                    if not first:
                        act.wait_ge(y_out, 16 * j)
                    nc.scalar.copy(Y[:], y_ps[:, 0:D]).then_inc(y_ready, 1)
                    act.wait_ge(y_ready, j + 1)
                    act.dma_start(k.ys_dram[bass.ts(j, P), :], Y[:]).then_inc(y_out, 16)

                silu(0)
                act.wait_ge(fuse_ready, 1)
                silu(1)
                store(0, True)
                with act.Fori(2, TILES) as j:
                    act.wait_ge(fuse_ready, j)
                    silu(j)
                    store(j - 1, False)
                store(TILES - 1, False)
                act.wait_ge(y_out, 16 * TILES)

            @block.vector
            def _(dve):
                def x_copy(j):
                    dve.wait_ge(xT_done, j + 1)
                    nc.vector.tensor_copy(XT[:], xT_ps[:]).then_inc(xT_ready, 1)

                def fuse_mul(j):
                    dve.wait_ge(silu_done, j + 1)
                    dve.wait_ge(u_done, j + 1)
                    nc.vector.tensor_tensor(fuse[:], u_ps[:], act_g[:], ALU.mult).then_inc(fuse_ready, 1)

                def fuse_copy(j):
                    dve.wait_ge(fT_done, j + 1)
                    nc.vector.tensor_copy(fuseT[:], fT_ps[:]).then_inc(fT_ready, 1)

                def ask(j):
                    nc.vector.tensor_copy(sl[:], k.token[:, bass.ds(j, 1)]).then_inc(sl_ready, 1)

                ask(0)
                x_copy(0)
                ask(1)
                with dve.Fori(0, TILES) as j:
                    fuse_mul(j)
                    x_copy(j + 1)
                    ask(j + 2)
                    fuse_copy(j)


PARTS = 3


def stage_project(k):
    nc, io = k.nc, k.io
    with ExitStack() as ctx:
        sb, psum, sem = scratch(k, ctx)
        gb0 = sb("c_gb0", [P, B, D])
        wqkv = sb("c_wqkv", [P, DC, 3 * D])
        rope = sb("c_rope", [P, 2, S // P, DH])
        Y = sb("c_y", [P, 2, G, 2, D])
        sl = sb("c_sl", [P, 2, G * 2], I32)
        mix = sb("c_mix", [P, G, D])
        stats = sb("c_stats", [P, G, 6])
        mv = sb("c_mv", [P, G, 2])
        std = sb("c_std", [P, G])
        xn = sb("c_xn", [P, G, D])
        h = sb("c_h", [P, G, D])
        hT = sb("c_hT", [P, DC, GT])
        t1 = sb("c_t1", [P, 2 * H, DH])
        t2 = sb("c_t2", [P, 2 * H, DH])
        rot = sb("c_rot", [P, 2, 2 * D])
        rest = sb("c_rest", [P, 2 * DC, GT])
        upd = sb("c_upd", [P, G, D])
        parts = sb("c_parts", [P, 2 * DC, PARTS, GT], BF16)
        hT_ps = psum("c_hT_ps", [P, DC, 512])
        qk_ps = psum("c_qk_ps", [P, 512])
        v_ps = psum("c_v_ps", [P, 512])
        T_ps = psum("c_T_ps", [P, 2 * DC, 512])
        HALF = DH // 2

        w_in, steps, sl_ready, mix_used = sem("c_w"), sem("c_steps"), sem("c_sl"), sem("c_mu")
        y_in = [sem(f"c_yin{u}") for u in range(2)]
        stats_ready, std_ready, h_ready = sem("c_st"), sem("c_std"), sem("c_h")
        hT_done, hT_ready, first_ready = sem("c_hT"), sem("c_hTr"), sem("c_first")
        qk_done, v_done, v_read, qk_read, rot_ready, T_done = sem("c_qk"), sem("c_v"), sem("c_vr"), sem("c_qkr"), sem("c_rot"), sem("c_T")
        hi_ready, rest_ready, mid_ready, low_ready, parts_out = sem("c_hi"), sem("c_rest"), sem("c_mid"), sem("c_low"), sem("c_po")

        with nc.Block() as block:
            @block.sync
            def _(sp):
                sp.dma_start(gb0[:], k.modrow_dram[0][:, GBI, :].partition_broadcast(P)).then_inc(w_in, 16)
                sp.dma_start(k.mods[:].rearrange("p b m d -> p (b m d)"),
                             k.modrow_dram[1].rearrange("b m d -> (b m d)").partition_broadcast(P)).then_inc(w_in, 16)
                sp.dma_start(wqkv[:], io["L1_Wqkv"].rearrange("(c p) n -> p c n", p=P)).then_inc(w_in, 16)
                sp.dma_start(rope[:].rearrange("p a t d -> p (a t) d"), io["rope"].rearrange("a (t p) d -> p (a t) d", p=P)).then_inc(w_in, 16)
                sp.nop().then_inc(parts_out, 16 * 2 * DC)
                with sp.Fori(0, NG) as g:
                    for c in range(2 * DC):
                        sp.wait_ge(low_ready, (g + 1) * 2 * DC + c + 1)
                        sp.dma_start(k.qk_dram[c, :, :, bass.ts(g, GT)].rearrange("a p n -> p a n"), parts[:, c]).then_inc(parts_out, 16)
                sp.wait_ge(parts_out, 16 * 2 * DC * (NG + 1))

            @block.gpsimd
            def _(pool):
                def gather(i, u):
                    wait_alone(pool, sl_ready, i * 2 + u + 1)
                    for s in range(G):
                        for c in range(2):
                            nc.gpsimd.indirect_dma_start(Y[:, u, s, c, :], None, k.ys_dram,
                                                         bass.IndirectOffsetOnAxis(ap=sl[:, u, s * 2 + c:s * 2 + c + 1], axis=0),
                                                         ).then_inc(y_in[u], 16)

                def lesser(g):
                    for c in range(2 * DC):
                        pool.wait_ge(mid_ready, g * 2 * DC + c + 1)
                        nc.gpsimd.tensor_tensor(parts[:, c, 2, :], rest[:, c, :], parts[:, c, 1, :], ALU.subtract).then_inc(low_ready, 1)

                gather(0, 0)
                gather(0, 1)
                with pool.Fori(0, NG // 2 - 1) as i:
                    for u in range(2):
                        gather(i + 1, u)
                        lesser(i * 2 + u)
                lesser(NG - 2)
                lesser(NG - 1)

            @block.vector
            def _(dve):
                o = Order(dve, steps)
                V = nc.vector
                dve.wait_ge(w_in, 64)
                mod = lambda g, t, m: t[:, bass.ds(g // GB, 1), m, :].to_broadcast([P, G, D])

                def ask(g, u):
                    V.tensor_copy(sl[:, u, :], k.slots[:, bass.ds(g * G, G), :].rearrange("p t c -> p (t c)")).then_inc(sl_ready, 1)

                def mix_second(i, u, more):
                    g = i * 2 + u
                    dve.wait_ge(first_ready, (g + 1) * G)
                    for s in range(G):
                        o.mark(V.scalar_tensor_tensor(mix[:, s, :], Y[:, u, s, 1, :], k.wts[:, 1, bass.ds(g * G + s, 1)],
                                                      mix[:, s, :], ALU.mult, ALU.add))
                    o.settle()
                    if more:
                        ask(g + 2, u)
                    V.tensor_tensor(upd[:], mix[:], gb0[:, bass.ds(g // GB, 1), :].to_broadcast([P, G, D]), ALU.mult).then_inc(mix_used, 1)

                def residual(g):
                    dve.wait_ge(mix_used, g + 2)
                    xg = k.x[:, bass.ds(g * G, G), :]
                    o.mark(V.tensor_tensor(xg, xg, upd[:], ALU.add))
                    o.settle_alone()
                    for s in range(G):
                        o.mark(V.bn_stats(stats[:, s, :], k.x[:, bass.ds(g * G + s, 1), :]))
                    o.settle_alone()
                    for s in range(G):
                        V.bn_aggr(mv[:, s, :], stats[:, s, :]).then_inc(stats_ready, 1)

                def normalise(g):
                    dve.wait_ge(std_ready, g + 1)
                    o.mark(V.reciprocal(std[:], std[:]))
                    o.settle()
                    for s in range(G):
                        o.mark(V.tensor_scalar(xn[:, s, :], k.x[:, bass.ds(g * G + s, 1), :], mv[:, s, 0:1], std[:, s:s + 1],
                                               ALU.subtract, ALU.mult))

                def shift(g):
                    o.settle()
                    o.mark(V.tensor_tensor(xn[:], xn[:], mod(g, k.mods, CA), ALU.mult))
                    o.settle()
                    dve.wait_ge(hT_done, g + 1)
                    V.tensor_tensor(h[:], xn[:], mod(g, k.mods, SA), ALU.add).then_inc(h_ready, 1)

                def rotate(g, s):
                    dve.wait_ge(qk_done, g * G + s + 1)
                    qk = qk_ps[:].rearrange("p (h d) -> p h d", d=DH)
                    tab = lambda a, lo, hi: rope[:, a, bass.ds((g % GB) * G + s, 1), lo:hi].to_broadcast([P, 2 * H, hi - lo])
                    o.mark(V.tensor_tensor(t1[:], qk, tab(0, 0, DH), ALU.mult))
                    o.mark(V.tensor_tensor(t2[:, :, 0:HALF], qk[:, :, HALF:], tab(1, 0, HALF), ALU.mult))
                    o.mark(V.tensor_tensor(t2[:, :, HALF:], qk[:, :, 0:HALF], tab(1, HALF, DH), ALU.mult))
                    o.settle()
                    if s >= 2:
                        dve.wait_ge(T_done, g * G + s - 1)
                    V.tensor_tensor(rot[:, s % 2, :].rearrange("p (h d) -> p h d", d=DH), t1[:], t2[:], ALU.add).then_inc(rot_ready, 1)
                    dve.wait_ge(rot_ready, g * G + s + 1)

                def remainders(g):
                    dve.wait_ge(T_done, (g + 1) * G)
                    for c in range(2 * DC):
                        dve.wait_ge(hi_ready, g * 2 * DC + c + 1)
                        dve.wait_ge(low_ready, g * 2 * DC + c + 1)
                        V.scalar_tensor_tensor(rest[:, c, :], T_ps[:, c, :], 0.25 if c < DC else 1.0, parts[:, c, 0, :],
                                               ALU.mult, ALU.subtract).then_inc(rest_ready, 1)

                ask(0, 0)
                ask(1, 1)
                FRONT = G + 1 + G + 1 + G + 1
                TURN = FRONT + 3 * G
                mix_second(0, 0, True)
                residual(0)
                normalise(0)
                shift(0)

                def group(i, u, ahead, more):
                    g = i * 2 + u
                    o.turn(g, FRONT, TURN)
                    rotate(g, 0)
                    if ahead:
                        mix_second(i + (u + 1) // 2, (u + 1) % 2, more)
                    rotate(g, 1)
                    if ahead:
                        residual(g + 1)
                    rotate(g, 2)
                    if ahead:
                        normalise(g + 1)
                        shift(g + 1)
                    rotate(g, 3)
                    remainders(g)

                with dve.Fori(0, NG // 2 - 2) as i:
                    for u in range(2):
                        group(i, u, True, True)
                for g in range(NG - 4, NG):
                    group(g // 2, g % 2, g + 1 < NG, g + 3 < NG)

            @block.scalar
            def _(act):
                def mix_first(i, u):
                    g = i * 2 + u
                    act.wait_ge(y_in[u], 16 * 2 * G * (i + 1))
                    act.wait_ge(mix_used, g + 1)
                    for s in range(G):
                        nc.scalar.activation(mix[:, s, :], Y[:, u, s, 0, :], ACT.Copy, scale=k.wts[:, 0, bass.ds(g * G + s, 1)]).then_inc(first_ready, 1)

                def deviation(g):
                    act.wait_ge(stats_ready, (g + 1) * G)
                    nc.scalar.activation(std[:], mv[:, :, 1], ACT.Sqrt, bias=k.eps[:, 0:1]).then_inc(std_ready, 1)

                def turned(g):
                    act.wait_ge(hT_done, g + 2)
                    nc.scalar.copy(hT[:], hT_ps[:]).then_inc(hT_ready, 1)

                def values(g, s):
                    act.wait_ge(v_done, g * G + s + 1)
                    nc.scalar.copy(k.v[:, bass.ds(g * G + s, 1), :, :].rearrange("p t h d -> p (t h d)"), v_ps[:, 0:D]).then_inc(v_read, 1)

                def high(g):
                    act.wait_ge(T_done, (g + 1) * G)
                    act.wait_ge(parts_out, 16 * 2 * DC * (g + 1))
                    for c in range(2 * DC):
                        nc.scalar.activation(parts[:, c, 0, :], T_ps[:, c, :], ACT.Copy, scale=0.25 if c < DC else 1.0).then_inc(hi_ready, 1)

                def middle(g):
                    for c in range(2 * DC):
                        act.wait_ge(rest_ready, g * 2 * DC + c + 1)
                        nc.scalar.copy(parts[:, c, 1, :], rest[:, c, :]).then_inc(mid_ready, 1)

                def group(i, u, ahead):
                    g = i * 2 + u
                    values(g, 0)
                    if ahead:
                        mix_first(i + (u + 1) // 2, (u + 1) % 2)
                    values(g, 1)
                    values(g, 2)
                    if ahead:
                        deviation(g + 1)
                    values(g, 3)
                    if ahead:
                        turned(g + 1)
                    high(g)
                    middle(g)

                mix_first(0, 0)
                deviation(0)
                turned(0)
                with act.Fori(0, NG // 2 - 1) as i:
                    group(i, 0, True)
                    group(i, 1, True)
                group(NG // 2 - 1, 0, True)
                group(NG // 2 - 1, 1, False)

            @block.tensor
            def _(pe):
                pe.wait_ge(w_in, 64)
                pe.nop().then_inc(mix_used, 1)
                pe.nop().then_inc(hT_done, 1)
                pe.nop().then_inc(low_ready, 2 * DC)

                def transposes(g):
                    pe.wait_ge(h_ready, g + 1)
                    for c in range(DC):
                        for s in range(G):
                            mm = nc.tensor.transpose(hT_ps[:, c, s * P:(s + 1) * P], h[:, s, c * P:(c + 1) * P], k.ident[:])
                    mm.then_inc(hT_done, 1)

                def turn_channels(g, s):
                    pe.wait_ge(rot_ready, g * G + s + 1)
                    for c in range(2 * DC):
                        mm = nc.tensor.transpose(T_ps[:, c, s * P:(s + 1) * P], rot[:, s % 2, c * P:(c + 1) * P], k.ident[:])
                    mm.then_inc(T_done, 1)

                def project(g, s):
                    for c in range(DC):
                        mm = nc.tensor.matmul(qk_ps[:], hT[:, c, s * P:(s + 1) * P], wqkv[:, c, 0:2 * D], start=(c == 0), stop=(c == DC - 1))
                    mm.then_inc(qk_done, 1)
                    if s >= 1:
                        pe.wait_ge(v_read, g * G + s)
                    for c in range(DC):
                        mm = nc.tensor.matmul(v_ps[:, 0:D], hT[:, c, s * P:(s + 1) * P], wqkv[:, c, 2 * D:], start=(c == 0), stop=(c == DC - 1))
                    mm.then_inc(v_done, 1)

                def group(g, ahead):
                    pe.wait_ge(hT_ready, g + 1)
                    project(g, 0)
                    if not (isinstance(g, int) and g == 0):
                        pe.wait_ge(rest_ready, g * 2 * DC)
                    for s in range(1, G):
                        pe.wait_ge(rot_ready, g * G + s)
                        project(g, s)
                        turn_channels(g, s - 1)
                    if ahead:
                        transposes(g + 1)
                    turn_channels(g, G - 1)

                transposes(0)
                group(0, True)
                with pe.Fori(1, NG - 1) as g:
                    group(g, True)
                group(NG - 1, False)


Q_BLOCKS = (0, 1, 2, 0, 1, 0)
K_BLOCKS = (0, 0, 0, 1, 1, 2)
Q_LOADS = ((0, 0, 3), (3, 0, 2), (5, 0, 1))
K_LOADS = tuple((n, part, 1) for n, part in enumerate(K_BLOCKS))
SLOTS = 4


def stage_attention(k):
    nc, io = k.nc, k.io
    ROWS = len(Q_BLOCKS) * DH
    KT, QB = S // P, S // 512
    HEADS = B * H
    VW = 2 * DH
    LEAD = 6
    BANK = (0, 1, 0, 2)
    TURN = KT - LEAD + 2
    STORED = 16 * QB
    LOADS_PER = len(Q_LOADS) + len(K_LOADS)
    with ExitStack() as ctx:
        sb, psum, sem = scratch(k, ctx)
        q = sb("t_q", [P, SLOTS, S], BF16)
        kk = sb("t_k", [P, SLOTS, S], BF16)
        v = sb("t_v", [P, SLOTS, KT, VW])
        probs = sb("t_p", [P, 2, S])
        peak = sb("t_peak", [P, 2, KT, QB])
        top = sb("t_top", [P, 2, KT])
        neg = sb("t_neg", [P, 2, KT])
        negparts = sb("t_negp", [P, PARTS, KT], BF16)
        negT = sb("t_negT", [PARTS * KT, P], BF16)
        o_sb = sb("t_o", [P, 512])
        sT_ps = psum("t_sT_ps", [P, 2, 2, 512])
        mx_ps = psum("t_mx_ps", [P, 3, 512])
        pv_ps = psum("t_pv_ps", [P, 512])
        nT_ps = mx_ps[0:PARTS * KT, 2, 0:P]

        qk_in = [sem(f"t_in{u}") for u in range(SLOTS)]
        ones_ready, v_ready = sem("t_ones"), sem("t_vr")
        mx_done, mx_read, top_ready, neg_steps, neg_ready = sem("t_mxd"), sem("t_mxr"), sem("t_top"), sem("t_ns"), sem("t_nr")
        nT_done, nT_ready, row_in = sem("t_nTd"), sem("t_nTr"), sem("t_row")
        s_done, e_done, pv_done, o_ready, o_out = sem("t_s"), sem("t_e"), sem("t_pv"), sem("t_or"), sem("t_oo")

        def turns(eng, turn):
            with eng.Fori(0, HEADS // SLOTS - 1) as i:
                for u in range(SLOTS):
                    turn(i * SLOTS + u, i, u, 2)
            i = HEADS // SLOTS - 1
            for u in range(SLOTS):
                turn(i * SLOTS + u, i, u, min(2, SLOTS - 1 - u))

        def later(i, u, by):
            return i + (u + by) // SLOTS, (u + by) % SLOTS

        with nc.Block() as block:
            @block.sync
            def _(sp):
                def load(n, u):
                    b, hd = n // H, n % H
                    for t, which, blocks in ((q, 0, Q_LOADS), (kk, 1, K_LOADS)):
                        src = k.qk_dram[bass.ds(which * DC + hd // HC, 1), :, bass.ds((hd % HC) * DH, DH), bass.ds(b * S, S)]
                        for at, part, count in blocks:
                            sp.dma_start(t[at * DH:(at + count) * DH, u, :],
                                         src[:, part:part + count].rearrange("o a d n -> (o a) d n")).then_inc(qk_in[u], 16)

                sp.nop().then_inc(o_out, STORED)
                load(0, 0)
                load(1, 1)

                def rows(n, u):
                    sp.wait_ge(nT_ready, n + 1)
                    sp.dma_start(q[ROWS:ROWS + PARTS, u, :].rearrange("a (t n) -> a t n", n=P), negT[:]).then_inc(row_in, 16)

                rows(0, 0)

                def turn(n, i, u, ahead):
                    sp.wait_ge(pv_done, n * KT + 2)
                    if ahead >= 2:
                        load(n + 2, (u + 2) % SLOTS)
                    if ahead >= 1:
                        rows(n + 1, (u + 1) % SLOTS)
                    sp.wait_ge(o_ready, n + 2)
                    b, hd = n // H, n % H
                    for j in range(QB):
                        cols = bass.ds(b * S + j * 512, 512)
                        sp.dma_start(k.od_dram[:, bass.ds(hd * DH, DH), cols], o_sb[j * VW:(j + 1) * VW, :]).then_inc(o_out, 16)

                turns(sp, turn)
                sp.wait_ge(o_out, STORED * (HEADS + 1))
                for u in range(SLOTS):
                    sp.wait_ge(qk_in[u], 16 * LOADS_PER * HEADS // SLOTS)

            @block.gpsimd
            def _(pool):
                for u in range(SLOTS):
                    nc.gpsimd.memset(kk[ROWS:ROWS + PARTS, u, :], 1.0).then_inc(ones_ready, 1)
                pool.wait_ge(ones_ready, SLOTS)
                nc.gpsimd.memset(v[:, :, :, DH:], 1.0).then_inc(ones_ready, 1)

                def copy_v(n, u):
                    b, hd = n // H, n % H
                    nc.gpsimd.tensor_copy(v[:, u, :, 0:DH], k.v[:, bass.ds(b * KT, KT), bass.ds(hd, 1), :].rearrange("p t o d -> p t (o d)")).then_inc(v_ready, 1)

                def split(n, u):
                    wait_alone(pool, top_ready, n + 1)
                    w = u % 2
                    g = nc.gpsimd
                    g.tensor_scalar_mul(neg[:, 0], top[:, w], -1.0).then_inc(neg_steps, 1)
                    pool.wait_ge(nT_done, n + 1)
                    wait_alone(pool, neg_steps, n * 4 + 1)
                    g.tensor_copy(negparts[:, 0], neg[:, 0]).then_inc(neg_steps, 1)
                    pool.wait_ge(neg_steps, n * 4 + 2)
                    g.tensor_tensor(neg[:, 1], neg[:, 0], negparts[:, 0], ALU.subtract).then_inc(neg_steps, 1)
                    wait_alone(pool, neg_steps, n * 4 + 3)
                    g.tensor_copy(negparts[:, 1], neg[:, 1]).then_inc(neg_steps, 1)
                    pool.wait_ge(neg_steps, n * 4 + 4)
                    g.tensor_tensor(negparts[:, 2], neg[:, 1], negparts[:, 1], ALU.subtract).then_inc(neg_ready, 1)
                    pool.wait_ge(neg_ready, n + 1)

                copy_v(0, 0)
                copy_v(1, 1)
                split(0, 0)

                def turn(n, i, u, ahead):
                    pool.wait_ge(pv_done, n * KT + 2)
                    if ahead >= 2:
                        copy_v(n + 2, (u + 2) % SLOTS)
                    if ahead >= 1:
                        split(n + 1, (u + 1) % SLOTS)

                turns(pool, turn)

            @block.vector
            def _(dve):
                dve.nop().then_inc(mx_read, 4)

                def maxima(n, w, m, blocks):
                    for kb in blocks:
                        t = (n * KT + m) * QB + kb
                        dve.wait_ge(mx_done, t + 1)
                        nc.vector.reduce_max(peak[:, w, m, kb:kb + 1], mx_ps[:, BANK[kb], :], AX.X).then_inc(mx_read, 1)
                    if m == KT - 1 and kb == QB - 1:
                        dve.wait_ge(mx_read, (n + 1) * KT * QB + 4)
                        nc.vector.reduce_max(top[:, w], peak[:, w], AX.X).then_inc(top_ready, 1)

                def turned(n):
                    dve.wait_ge(nT_done, n + 2)
                    dve.wait_ge(row_in, 16 * (n + 1))
                    nc.vector.tensor_copy(negT[:], nT_ps).then_inc(nT_ready, 1)

                for m in range(KT):
                    maxima(0, 0, m, range(QB))
                for m in range(LEAD):
                    maxima(1, 1, m, (0,))
                    if m == 2:
                        turned(0)
                    maxima(1, 1, m, (1, 2, 3))

                def turn(n, i, u, ahead):
                    for kt in range(KT):
                        m = kt + LEAD
                        if m < KT:
                            lead, tile = ahead >= 1, (n + 1, (u + 1) % 2, m)
                        else:
                            lead, tile = ahead >= 2, (n + 2, u % 2, m - KT)
                        if lead:
                            maxima(*tile, (0,))
                        if kt == TURN + 1 and ahead >= 1:
                            turned(n + 1)
                        if lead:
                            maxima(*tile, (1, 2, 3))

                turns(dve, turn)

            @block.scalar
            def _(act):
                act.nop().then_inc(e_done, 2)

                def exps(n, kt):
                    for hf in range(2):
                        act.wait_ge(s_done, (n * KT + kt) * 2 + hf + 1)
                        if hf == 0:
                            act.wait_ge(pv_done, n * KT + kt + 1)
                        nc.scalar.activation(probs[:, kt % 2, hf * 1024:(hf + 1) * 1024].rearrange("p (j n) -> p j n", n=512),
                                             sT_ps[:, hf], ACT.Exp).then_inc(e_done, 1)

                exps(0, 0)

                def turn(n, i, u, ahead):
                    for kt in range(1, KT):
                        exps(n, kt)
                    if ahead >= 1:
                        exps(n + 1, 0)
                    act.wait_ge(pv_done, (n + 1) * KT + 2)
                    act.wait_ge(o_out, STORED * (n + 1))
                    nc.scalar.copy(o_sb[:], pv_ps[:]).then_inc(o_ready, 1)

                turns(act, turn)

            @block.tensor
            def _(pe):
                pe.wait_ge(ones_ready, SLOTS + 1)
                pe.nop().then_inc(pv_done, 2)
                pe.nop().then_inc(o_ready, 1)
                pe.nop().then_inc(nT_done, 1)
                pe.nop().then_inc(row_in, 16)

                def maximum(n, u, m, kb):
                    t = (n * KT + m) * QB + kb
                    pe.wait_ge(mx_read, t + 3 if BANK[kb] == 0 else t + 1)
                    nc.tensor.matmul(mx_ps[:, BANK[kb], :], q[0:ROWS, u, m * P:(m + 1) * P], kk[0:ROWS, u, kb * 512:(kb + 1) * 512],
                                     start=True, stop=True).then_inc(mx_done, 1)

                def scores(n, u, kt, qb):
                    hf, j = qb // 2, qb % 2
                    if j == 0:
                        pe.wait_ge(e_done, (n * KT + kt) * 2 + hf + 1)
                    mm = nc.tensor.matmul(sT_ps[:, hf, j, :], kk[0:ROWS + PARTS, u, kt * P:(kt + 1) * P],
                                          q[0:ROWS + PARTS, u, qb * 512:(qb + 1) * 512], start=True, stop=True)
                    if j == 1:
                        mm.then_inc(s_done, 1)

                def weigh(n, u, kt):
                    pe.wait_ge(e_done, (n * KT + kt) * 2 + 4)
                    if kt == 0:
                        pe.wait_ge(v_ready, n + 1)
                        pe.wait_ge(o_ready, n + 1)
                    for j in range(QB):
                        mm = nc.tensor.matmul(pv_ps[j * VW:(j + 1) * VW, :], v[:, u, kt, :], probs[:, kt % 2, j * 512:(j + 1) * 512],
                                              start=(kt == 0), stop=(kt == KT - 1), tile_position=(0, j * VW))
                    mm.then_inc(pv_done, 1)

                def turn_maxima(n, read):
                    wait_alone(pe, neg_ready, n + 1)
                    pe.wait_ge(mx_read, read + 4)
                    nc.tensor.matmul(nT_ps, negparts[:].rearrange("p a t -> p (a t)"), k.identb[:], start=True, stop=True).then_inc(nT_done, 1)

                pe.wait_ge(qk_in[0], 16 * LOADS_PER)
                for m in range(KT):
                    for kb in range(QB):
                        maximum(0, 0, m, kb)
                pe.wait_ge(qk_in[1], 16 * LOADS_PER)
                for m in range(LEAD):
                    for kb in range(QB):
                        if m == 2 and kb == QB - 1:
                            pe.wait_ge(nT_ready, 1)
                        maximum(1, 1, m, kb)
                    if m == 1:
                        turn_maxima(0, (KT + 2) * QB)
                pe.wait_ge(row_in, 32)
                for qb in range(QB):
                    scores(0, 0, 0, qb)

                def turn(n, i, u, ahead):
                    for kt in range(KT):
                        m = kt + LEAD
                        if m < KT:
                            lead, tile = ahead >= 1, (n + 1, (u + 1) % SLOTS, m)
                        else:
                            lead, tile = ahead >= 2, (n + 2, (u + 2) % SLOTS, m - KT)
                        if m == KT and ahead >= 2:
                            i2, u2 = later(i, u, 2)
                            pe.wait_ge(qk_in[u2], 16 * LOADS_PER * (i2 + 1))
                        if kt + 1 == KT and ahead >= 1:
                            pe.wait_ge(row_in, 16 * (n + 3))
                        def peak_at(kb):
                            if lead:
                                maximum(*tile, kb)

                        def next_scores(*blocks):
                            for qb in blocks:
                                if kt + 1 < KT:
                                    scores(n, u, kt + 1, qb)
                                elif ahead >= 1:
                                    scores(n + 1, (u + 1) % SLOTS, 0, qb)

                        peak_at(0)
                        next_scores(0, 1)
                        peak_at(1)
                        next_scores(2)
                        peak_at(2)
                        next_scores(3)
                        if kt == TURN + 1 and ahead >= 2:
                            pe.wait_ge(nT_ready, n + 2)
                        peak_at(3)
                        weigh(n, u, kt)
                        if kt == TURN and ahead >= 1:
                            turn_maxima(n + 1, (n + 2) * KT * QB + ((TURN + LEAD - KT + 1) * QB if ahead >= 2 else 0))

                turns(pe, turn)




def stage_peer(k):
    nc, io = k.nc, k.io
    SLOTS_Y = 4
    with ExitStack() as ctx:
        sb, psum, sem = scratch(k, ctx)
        wo = sb("p_wo", [P, DC, D])
        ga_wo = sb("p_ga_wo", [P, B, DC, D])
        od = sb("p_od", [P, 2, DC, GT])
        at = sb("p_at", [P, DC, GT])
        shift_x = sb("p_shift", [P, G])
        stats = sb("p_stats", [P, G, 6])
        mv = sb("p_mv", [P, G, 2])
        std = sb("p_std", [P, G])
        xn = sb("p_xn", [P, G, D])
        h = sb("p_h", [P, G, D])
        hu = sb("p_hu", [P, G, D])
        hT = sb("p_hT", [P, DC, GT])
        val = sb("p_val", [P, 2, PH])
        arg = sb("p_arg", [P, 2, PH, 8], U32)
        score = sb("p_score", [P, SLOTS_Y, PH])
        sl = sb("p_sl", [P, SLOTS_Y, PH], I32)
        Y = sb("p_Y", [P, SLOTS_Y, PH, 2 * D])
        dump = sb("p_dump", [P, PH, D])
        dot = sb("p_dot", [P, 2, PH])
        act_dot = sb("p_gelu", [P, 2, PH])
        gk = sb("p_gk", [P, 2, PH])
        diag = sb("p_diag", [P, 2, PH, P])
        part = sb("p_part", [P, D])

        score_ready, w_in, wo_ready, ln_ready, inv_ready, xn_ready = sem("p_sc"), sem("p_w"), sem("p_wo"), sem("p_ln"), sem("p_inv"), sem("p_xn")
        od_in, at_ready, proj_done, steps = sem("p_od"), sem("p_at"), sem("p_proj"), sem("p_steps")
        stats_ready, std_ready, rstd_ready, h_ready, h_kept = sem("p_st"), sem("p_std"), sem("p_rstd"), sem("p_h"), sem("p_hk")
        hT_done, hT_ready, sim_done, val_ready, arg_ready, idx_ready = sem("p_hTd"), sem("p_hTr"), sem("p_sim"), sem("p_val"), sem("p_arg"), sem("p_idx")
        y_in = [sem(f"p_y{u}") for u in range(SLOTS_Y)]
        dots_done, gelu_ready, gk_ready, diag_ready, sums_done, part_ready, x_ready, x_out = (
            sem("p_dots"), sem("p_gelu"), sem("p_gk"), sem("p_diag"), sem("p_sums"), sem("p_part"), sem("p_x"), sem("p_xo"))

        tmp_ps = psum("p_tmp_ps", [P, 2, 512])
        sim_ps = psum("p_sim_ps", [P, 2, SIMS])
        out_ps = psum("p_out_ps", [P, 512])

        def inside(g, u):
            return not isinstance(g, int) or 0 <= g * G + u < NT

        def run(eng, step, ahead):
            for u in range(G):
                step(0, u)
                ahead(0, u)
            with eng.Fori(1, NG - 1) as g:
                for u in range(G):
                    step(g, u)
                    ahead(g, u)
            for u in range(G):
                step(NG - 1, u)
            for u in range(3):
                step(NG, u)

        with nc.Block() as block:
            @block.sync
            def _(sp):
                def load(g):
                    cols = bass.ds(g * GT, GT)
                    for a in range(2):
                        sp.dma_start(od[:, a], k.od_dram[a][:, cols].rearrange("(c p) n -> p c n", p=P)).then_inc(od_in, 16)

                def store(g):
                    sp.wait_ge(x_ready, (g + 1) * G)
                    sp.dma_start(k.out.rearrange("b (t p) d -> p (b t) d", p=P)[:, bass.ds(g * G, G), :],
                                 k.x[:, bass.ds(g * G, G), :]).then_inc(x_out, 16)

                load(0)
                sp.dma_start(wo[:], io["L1_Wo"].rearrange("(c p) n -> p c n", p=P)).then_inc(w_in, 16)
                sp.wait_ge(at_ready, 1)
                load(1)
                with sp.Fori(0, NG - 2) as g:
                    sp.wait_ge(at_ready, g + 2)
                    load(g + 2)
                    store(g)
                store(NG - 2)
                store(NG - 1)
                sp.wait_ge(x_out, 16 * NG)

            @block.gpsimd
            def _(pool):
                def step(g, u):
                    if not inside(g, u):
                        return
                    t = g * G + u
                    if inside(g, u - SLOTS_Y):
                        pool.wait_ge(sums_done, t - SLOTS_Y + 1)
                    wait_alone(pool, idx_ready, t + 1)
                    for j in range(PH):
                        nc.gpsimd.indirect_dma_start(Y[:, u, j, :], None, io["L1_table"],
                                                     bass.IndirectOffsetOnAxis(ap=sl[:, u, j:j + 1], axis=0)).then_inc(y_in[u], 16)

                run(pool, step, lambda g, u: None)

            @block.vector
            def _(dve):
                o = Order(dve, steps)
                V = nc.vector
                mod = lambda g, m: k.mods[:, bass.ds(g // GB, 1), m, :]

                def attended(g):
                    dve.wait_ge(inv_ready, g + 1)
                    V.tensor_tensor(at[:], od[:, 0], od[:, 1], ALU.mult).then_inc(at_ready, 1)

                def residual(g):
                    dve.wait_ge(proj_done, g + 1)
                    xg = k.x[:, bass.ds(g * G, G), :]
                    o.mark(V.tensor_tensor(xg, xg, tmp_ps[:].rearrange("p a (s d) -> p (a s) d", d=D), ALU.add))
                    o.settle_alone()
                    for s in range(G):
                        o.mark(V.bn_stats(stats[:, s, :], k.x[:, bass.ds(g * G + s, 1), :]))
                    o.settle_alone()
                    for s in range(G):
                        V.bn_aggr(mv[:, s, :], stats[:, s, :]).then_inc(stats_ready, 1)

                def deviation(g):
                    dve.wait_ge(std_ready, g + 1)
                    o.mark(V.reciprocal(std[:], std[:]))
                    o.settle()
                    V.scalar_tensor_tensor(shift_x[:], mv[:, :, 0], -1.0, std[:], ALU.mult, ALU.mult).then_inc(rstd_ready, 1)

                def normalise(g):
                    dve.wait_ge(xn_ready, (g + 1) * G)
                    o.mark(V.tensor_tensor(xn[:], xn[:], mod(g, CB).to_broadcast([P, G, D]), ALU.mult))
                    o.settle()
                    if not isinstance(g, int) or g > 0:
                        dve.wait_ge(h_kept, 2 * g)
                    V.tensor_tensor(h[:], xn[:], mod(g, SB).to_broadcast([P, G, D]), ALU.add).then_inc(h_ready, 1)

                def dots(g, u):
                    v, t = u % SLOTS_Y, g * G + u
                    turn = g + u // SLOTS_Y
                    dve.wait_ge(y_in[v], 16 * PH * (turn + 1))
                    dve.wait_ge(h_kept, 2 * turn + 1 + v // 2)
                    for j in range(PH):
                        V.tensor_tensor_reduce(dump[:, j, :], hu[:, v, :], Y[:, v, j, 0:D], 1.0, 0.0, ALU.mult, ALU.add,
                                               dot[:, v % 2, j:j + 1]).then_inc(dots_done, 1)

                def choose(g, u):
                    t = g * G + u
                    dve.wait_ge(sim_done, t + 1)
                    sims = sim_ps[:, u % 2, :].rearrange("p (a n) -> p a n", n=KEYS)
                    if not (isinstance(g, int) and t == 0):
                        dve.wait_ge(score_ready, t)
                    V.reduce_max(val[:].rearrange("p a j -> p (a j)"), sims, AX.X).then_inc(val_ready, 1)
                    wait_alone(dve, val_ready, t + 1)
                    for a in range(2):
                        for j in range(PH):
                            V.max_index(arg[:, a, j, :], val[:, a, j:j + 1].to_broadcast([P, 8]), sims[:, a * PH + j, :]).then_inc(arg_ready, 1)
                    V.tensor_tensor(score[:, u, :], val[:, 0, :], val[:, 1, :], ALU.add).then_inc(score_ready, 1)
                    dve.wait_ge(arg_ready, 2 * PH * (t + 1))
                    V.scalar_tensor_tensor(sl[:, u, :], arg[:, 0, :, 0], float(KEYS), arg[:, 1, :, 0], ALU.mult, ALU.add).then_inc(idx_ready, 1)

                def weights(g, u):
                    v, t = u % SLOTS_Y, g * G + u
                    dve.wait_ge(gelu_ready, t + 1)
                    V.scalar_tensor_tensor(gk[:, v % 2, :], score[:, v, :], 0.0, act_dot[:, v % 2, :], ALU.max, ALU.mult).then_inc(gk_ready, 1)

                def finish(g, u):
                    t = g * G + u
                    dve.wait_ge(sums_done, t + 1)
                    V.tensor_tensor(part[:], out_ps[:, 0:D], k.mods[:, bass.ds(t // (NT // B), 1), GBI, :].rearrange("p o d -> p (o d)"), ALU.mult).then_inc(part_ready, 1)
                    dve.wait_ge(part_ready, t + 1)
                    xt = k.x[:, bass.ds(t, 1), :].rearrange("p o d -> p (o d)")
                    V.tensor_tensor(xt, xt, part[:], ALU.add).then_inc(x_ready, 1)
                    dve.wait_ge(x_ready, t + 1)

                def step(g, u):
                    if inside(g, u - 2):
                        dots(g, u - 2)
                    if u == 2 and inside(g + 1, 0):
                        deviation(g + 1)
                    if inside(g, u):
                        choose(g, u)
                    if inside(g, u - 2):
                        weights(g, u - 2)
                    if inside(g, u - 3):
                        finish(g, u - 3)

                AHEAD = 1 + G + 1 + 1

                def ahead(g, u):
                    if u == 0:
                        attended(g + 1)
                    if u == 1:
                        residual(g + 1)
                    if u == 2:
                        normalise(g + 1)

                dve.wait_ge(w_in, 16)
                for b in range(B):
                    V.tensor_tensor(ga_wo[:, b], wo[:], k.mods[:, b, GA, :].unsqueeze(1).to_broadcast([P, DC, D]), ALU.mult).then_inc(wo_ready, 1)
                attended(0)
                residual(0)
                deviation(0)
                normalise(0)
                first = o.n

                def counted(g, u):
                    if u == 0:
                        o.turn(g, first, AHEAD)
                    step(g, u)

                run(dve, counted, ahead)

            @block.scalar
            def _(act):
                def deviation(g):
                    act.wait_ge(stats_ready, (g + 1) * G)
                    nc.scalar.activation(std[:], mv[:, :, 1], ACT.Sqrt, bias=k.eps[:, 0:1]).then_inc(std_ready, 1)

                def inverse(g):
                    act.wait_ge(od_in, 32 * (g + 1))
                    nc.scalar.activation(od[:, 1], od[:, 1], ACT.Ln).then_inc(ln_ready, 1)
                    act.wait_ge(ln_ready, g + 1)
                    nc.scalar.activation(od[:, 1], od[:, 1], ACT.Exp, scale=-1.0).then_inc(inv_ready, 1)

                def normalise(g):
                    act.wait_ge(rstd_ready, g + 1)
                    for s in range(G):
                        nc.scalar.activation(xn[:, s, :], k.x[:, bass.ds(g * G + s, 1), :].rearrange("p o d -> p (o d)"), ACT.Identity,
                                             bias=shift_x[:, s:s + 1], scale=std[:, s:s + 1]).then_inc(xn_ready, 1)

                def turned(g, last):
                    act.wait_ge(hT_done, g + 1)
                    if last:
                        act.wait_ge(sim_done, g * G)
                    nc.scalar.copy(hT[:], tmp_ps[:]).then_inc(hT_ready, 1)

                def keep(g, half):
                    if inside(g, 2 * half - G):
                        act.wait_ge(dots_done, PH * (g * G + 2 * half - 2))
                    nc.scalar.copy(hu[:, 2 * half:2 * half + 2, :], h[:, 2 * half:2 * half + 2, :]).then_inc(h_kept, 1)

                def step(g, u):
                    more = not isinstance(g, int) or g + 1 < NG
                    if u == 0 and more:
                        inverse(g + 1)
                    if u == 2 and more:
                        normalise(g + 1)
                    if inside(g, u - 2):
                        v, t = (u - 2) % SLOTS_Y, g * G + u - 2
                        act.wait_ge(dots_done, PH * (t + 1))
                        nc.scalar.activation(act_dot[:, v % 2, :], dot[:, v % 2, :], ACT.Gelu).then_inc(gelu_ready, 1)
                        act.wait_ge(gk_ready, t + 1)
                        if inside(g, u - 4):
                            act.wait_ge(sums_done, t - 1)
                        for j in range(PH):
                            nc.scalar.activation(diag[:, v % 2, j, :], k.ident[:], ACT.Copy, scale=gk[:, v % 2, j:j + 1]).then_inc(diag_ready, 1)
                    if inside(g, u) and u == 1:
                        keep(g, 1)

                def ahead(g, u):
                    if u == 1:
                        deviation(g + 1)
                    if u == 2:
                        turned(g + 1, True)
                    if u == 3:
                        keep(g + 1, 0)

                inverse(0)
                deviation(0)
                normalise(0)
                turned(0, False)
                keep(0, 0)
                run(act, step, ahead)

            @block.tensor
            def _(pe):
                pe.wait_ge(wo_ready, B)

                def project(g):
                    pe.wait_ge(at_ready, g + 1)
                    if not isinstance(g, int) or g > 0:
                        pe.wait_ge(hT_ready, g)
                    for s in range(G):
                        for c in range(DC):
                            mm = nc.tensor.matmul(tmp_ps[:, s // 2, (s % 2) * D:(s % 2 + 1) * D], at[:, c, s * P:(s + 1) * P], ga_wo[:, bass.ds(g // GB, 1), c, :],
                                                  start=(c == 0), stop=(c == DC - 1))
                    mm.then_inc(proj_done, 1)

                def transposes(g):
                    pe.wait_ge(h_ready, g + 1)
                    for c in range(DC):
                        for s in range(G):
                            mm = nc.tensor.transpose(tmp_ps[:, c, s * P:(s + 1) * P], h[:, s, c * P:(c + 1) * P], k.ident[:])
                    mm.then_inc(hT_done, 1)

                def similarities(g, u):
                    t = g * G + u
                    if u == 0:
                        pe.wait_ge(hT_ready, g + 1)
                    if inside(g, u - 2):
                        pe.wait_ge(arg_ready, 2 * PH * (t - 1))
                    for n in range(2):
                        for c in range(DC):
                            mm = nc.tensor.matmul(sim_ps[:, u % 2, n * 512:(n + 1) * 512], hT[:, c, u * P:(u + 1) * P],
                                                  k.wsim[:, c, n * 512:(n + 1) * 512], start=(c == 0), stop=(c == DC - 1))
                    mm.then_inc(sim_done, 1)

                def sums(g, u):
                    v, t = u % SLOTS_Y, g * G + u
                    pe.wait_ge(diag_ready, PH * (t + 1))
                    if inside(g, u - 1):
                        pe.wait_ge(part_ready, t)
                    for j in range(PH):
                        mm = nc.tensor.matmul(out_ps[:, 0:D], diag[:, v % 2, j, :], Y[:, v, j, D:], start=(j == 0), stop=(j == PH - 1))
                    mm.then_inc(sums_done, 1)

                def step(g, u):
                    if u < G - 1 and inside(g, u + 1):
                        similarities(g, u + 1)
                    elif u == G - 1 and inside(g + 1, 0):
                        similarities(g + 1, 0)
                    if inside(g, u - 2):
                        sums(g, u - 2)

                def ahead(g, u):
                    if u == 0:
                        project(g + 1)
                    if u == 2:
                        transposes(g + 1)

                project(0)
                transposes(0)
                similarities(0, 0)
                run(pe, step, ahead)


def build(nc, io, out, upto=99):
    ctx = ExitStack()
    with ctx:
        k = setup(nc, ctx, io)
        k.out = out
        k.TILES = 2 * NT + E
        k.COLS = k.TILES + 2
        k.token = ctx.enter_context(nc.sbuf_tensor("token", [P, k.COLS], I32))
        dram = lambda name, shape, dt=F32: nc.dram_tensor(name, shape, dt, kind="Internal").ap()
        k.h2_dram = dram("h2_dram", [T, D])
        k.ys_dram = dram("ys_dram", [k.TILES * P, D])
        k.qk_dram = dram("qk_dram", [2 * DC, PARTS, P, T], BF16)
        k.od_dram = dram("od_dram", [2, D, T])
        k.w_moe_in = ctx.enter_context(nc.semaphore("w_moe_in"))
        k.slots = ctx.enter_context(nc.sbuf_tensor("slots", [P, NT, 2], I32))
        k.wts = ctx.enter_context(nc.sbuf_tensor("wts", [P, 2, NT], F32))
        k.wsim = ctx.enter_context(nc.sbuf_tensor("wsim", [P, DC, SIMS], F32))
        k.eid = ctx.enter_context(nc.sbuf_tensor("eid", [1, k.COLS], I32))
        with ExitStack() as l0:
            def sb(name, shape):
                return l0.enter_context(nc.sbuf_tensor(name, shape, F32))
            k.kvsum = sb("kvsum", [P, B, DC, P + 1])
            k.logits = sb("logits", [P, NT, E])
            stage_modulation(k)
            stage_linear_attention_sums(k)
            k.wg = sb("wg", [P, E, DC, F])
            k.wu = sb("wu", [P, E, DC, F])
            k.wd = sb("wd", [P, E, FC, D])
            stage_linear_attention_apply(k)
            if upto >= 3:
                stage_route(k)
            if upto >= 4:
                stage_experts(k)
        if upto >= 5:
            with ExitStack() as l1:
                k.v = l1.enter_context(nc.sbuf_tensor("v", [P, NT, H, DH], F32))
                stage_project(k)
                if upto >= 6:
                    stage_attention(k)
        if upto >= 7:
            stage_peer(k)


def layout(inputs):
    def plain(a):
        return np.ascontiguousarray(np.asarray(a))

    arrays = {"L0_attn_x": plain(inputs["L0_attn_x"])}
    for l in (0, 1):
        arrays[f"L{l}_cT"] = plain(np.asarray(inputs[f"L{l}_c"]).T)
        arrays[f"L{l}_wmod"] = plain(inputs[f"L{l}_wmod"])
    for n in "qkv":
        arrays[f"L0_W{n}T"] = plain(np.asarray(inputs[f"L0_attn_W{n}"]).T)
        arrays[f"L0_attn_b{n}"] = plain(inputs[f"L0_attn_b{n}"])
    for n in ("gamma", "beta"):
        arrays[f"L0_attn_{n}"] = plain(inputs[f"L0_attn_{n}"])
    arrays["L0_router"] = plain(inputs["L0_ffn_router_kernel_DE"])
    for n, source in (("gate", "gating_EDF"), ("up", "up_EDF"), ("down", "down_EFD")):
        arrays[f"L0_{n}"] = plain(inputs[f"L0_ffn_kernel_{source}"])
    arrays["L1_Wqkv"] = plain(inputs["L1_attn_Wqkv"])
    arrays["L1_Wo"] = plain(inputs["L1_attn_Wo"])
    arrays["L1_wqT"] = plain(np.asarray(inputs["L1_ffn_w_q"]).T)
    arrays["L1_keysT"] = plain(np.asarray(inputs["L1_ffn_keys"]).transpose(2, 0, 3, 1).reshape(2 * PH * P, KEYS))
    arrays["L1_table"] = plain(np.concatenate([np.asarray(inputs["L1_ffn_w_down"]), np.asarray(inputs["L1_ffn_w_up"])], axis=1))

    lane = np.arange(P)
    arrays["ident"] = np.eye(P, dtype=np.float32)
    arrays["ones"] = np.ones((P, P), np.float32)
    arrays["tri"] = np.triu(np.ones((P, P), np.float32), 1)
    arrays["head_mask"] = np.concatenate([lane[:, None] // DH == lane[None, :] // DH,
                                          lane[:, None] // DH == np.arange(HC)[None, :]], axis=1).astype(np.float32)
    arrays["rank"] = np.tile(E - np.arange(E, dtype=np.float32), (P, 1))
    arrays["tile_start"] = (np.arange(2 * NT + E + 2, dtype=np.float32) * P)[None]
    arrays["iota"] = np.tile(lane.astype(np.float32), (P, 1))
    arrays["ids"] = (lane[:, None] + P * np.arange(NT)[None, :]).astype(np.float32)
    freq = (1.0 / np.float32(10000.0) ** (np.arange(0, DH, 2, dtype=np.float32) / np.float32(DH))).astype(np.float32)
    angle = np.outer(np.arange(S, dtype=np.float32), freq).astype(np.float32)
    arrays["rope"] = np.stack([np.concatenate([np.cos(angle), np.cos(angle)], 1),
                               np.concatenate([-np.sin(angle), np.sin(angle)], 1)]).astype(np.float32)
    return arrays


def kernel(**inputs):
    import concourse.bacc as bacc
    from concourse.bass_utils import run_bass_kernel_spmd

    nc = bacc.Bacc("TRN2", target_bir_lowering=False, num_devices=1)
    arrays, io = {}, {}
    for name, a in layout(inputs).items():
        arrays[f"in_{name}_dram"] = a
        io[name] = nc.dram_tensor(f"in_{name}_dram", a.shape, mybir.dt.from_np(a.dtype), kind="ExternalInput").ap()
    out = nc.dram_tensor("out_0_dram", (B, S, D), F32, kind="ExternalOutput").ap()
    build(nc, io, out)
    r = run_bass_kernel_spmd(nc, [arrays], core_ids=[0])
    return r.results[0]["out_0_dram"]
```

```python
from contextlib import ExitStack

import numpy as np

import concourse.bass as bass
from concourse import mybir

F32 = mybir.dt.float32
BF16 = mybir.dt.bfloat16
I32 = mybir.dt.int32
U32 = mybir.dt.uint32
ALU = mybir.AluOpType
ACT = mybir.ActivationFunctionType
AX = mybir.AxisListType

P = 128
B, S, D = 2, 2048, 256
T = B * S
NT = T // P
G = 4
GT = G * P
NG = NT // G
GB = NG // B
DC = D // P
H, DH = 16, 16
HC = P // DH
E, F = 8, 512
FC = F // P
KEYS, PH = 64, 8
SIMS = 2 * PH * KEYS
LN_EPS = 1e-5
DENOM_EPS = 1e-6
GATE_MIN = 0.25
SA, CA, GA, SB, CB, GBI = range(6)


class Order:

    def __init__(self, eng, sem):
        self.eng, self.sem, self.base, self.n = eng, sem, 0, 0

    def mark(self, instruction):
        self.n += 1
        return instruction.then_inc(self.sem, 1)

    def settle(self):
        self.eng.wait_ge(self.sem, self.base + self.n)

    def settle_alone(self):
        wait_alone(self.eng, self.sem, self.base + self.n)

    def turn(self, i, start, per):
        self.base, self.n = i * per + start, 0


def wait_alone(eng, sem, value):
    r = eng.to_reg(value)
    eng.wait_ge(sem, 1)
    eng.wait_ge(sem, r)


class Kernel:
    pass


def setup(nc, ctx, io):
    k = Kernel()
    k.nc, k.ctx, k.io = nc, ctx, io

    def sb(name, shape, dt=F32):
        return ctx.enter_context(nc.sbuf_tensor(name, shape, dt))

    k.x = sb("x_res", [P, NT, D])
    k.mods = sb("mods", [P, B, 6, D])
    k.ident = sb("ident", [P, P])
    k.identb = sb("identb", [P, P], BF16)
    k.eps = sb("eps", [P, 1])
    k.modrow_dram = [nc.dram_tensor(f"modrow_dram{l}", [B, 6, D], F32, kind="Internal").ap() for l in range(2)]
    k.h_dram = nc.dram_tensor("h_dram", [T, D], F32, kind="Internal").ap()
    k.qT_dram = nc.dram_tensor("qT_dram", [DC, P, T], F32, kind="Internal").ap()
    return k


def stage_modulation(k):
    nc, io = k.nc, k.io
    with ExitStack() as ctx:
        def sb(name, shape, dt=F32):
            return ctx.enter_context(nc.sbuf_tensor(name, shape, dt))

        def sem(name):
            return k.ctx.enter_context(nc.semaphore(name))

        cT = sb("cT", [P, 2, DC, B])
        scT = sb("scT", [P, 2, DC, B])
        wmod = sb("wmod", [P, 2, DC, 6 * D])
        row = sb("modrow", [B, 2, 6, D])
        sign = sb("modsign", [B, 2, 2, D])
        neg = sb("modneg", [B, 2, 2, D])
        ps = ctx.enter_context(nc.psum_tensor("mod_ps", [P, 6, 512], F32))
        w_in = [sem(f"m_w_in{l}") for l in range(2)]
        c_in, x_in, id_in = sem("m_c_in"), sem("m_x_in"), sem("m_id_in")
        silu_done, mod_done = sem("m_silu"), sem("m_mod")
        dve_steps, row_ready, row_out, bc_in = sem("m_dve"), sem("m_row"), sem("m_rowout"), sem("m_bc")
        with nc.Block() as block:
            @block.sync
            def _(sp):
                for l in range(2):
                    for c in range(DC):
                        sp.dma_start(cT[:, l, c, :], io[f"L{l}_cT"][c * P:(c + 1) * P, :]).then_inc(c_in, 16)
                for l in range(2):
                    sp.dma_start(wmod[:, l, :, :], io[f"L{l}_wmod"].rearrange("(c p) n -> p c n", p=P)).then_inc(w_in[l], 16)
                sp.dma_start(k.ident[:], io["ident"]).then_inc(id_in, 16)
                sp.dma_start(k.x[:], io["L0_attn_x"].rearrange("b (t p) d -> p (b t) d", p=P)).then_inc(x_in, 16)
                sp.wait_ge(row_ready, 1)
                sp.dma_start(k.modrow_dram[0], row[:, 0, :, :]).then_inc(row_out, 16)
                sp.wait_ge(row_out, 16)
                sp.dma_start(k.mods[:].rearrange("p b m d -> p (b m d)"),
                             k.modrow_dram[0].rearrange("b m d -> (b m d)").partition_broadcast(P)).then_inc(bc_in, 16)
                sp.wait_ge(row_ready, 2)
                sp.dma_start(k.modrow_dram[1], row[:, 1, :, :]).then_inc(row_out, 16)
                sp.wait_ge(row_out, 32)
                sp.wait_ge(bc_in, 16)
                sp.wait_ge(x_in, 16)

            @block.scalar
            def _(act):
                act.wait_ge(c_in, 64)
                nc.scalar.activation(scT[:], cT[:], ACT.Silu).then_inc(silu_done, 1)

            @block.tensor
            def _(pe):
                pe.wait_ge(silu_done, 1)
                for l in range(2):
                    pe.wait_ge(w_in[l], 16)
                    for n in range(3):
                        for c in range(DC):
                            mm = nc.tensor.matmul(ps[0:B, 3 * l + n, :], scT[:, l, c, :], wmod[:, l, c, n * 512:(n + 1) * 512],
                                                  start=(c == 0), stop=(c == DC - 1))
                    mm.then_inc(mod_done, 1)

            @block.vector
            def _(dve):
                o = Order(dve, dve_steps)
                o.mark(nc.vector.memset(k.eps[:], LN_EPS))
                for l in range(2):
                    dve.wait_ge(mod_done, l + 1)
                    o.mark(nc.vector.tensor_copy(row[:, l, :, :].rearrange("b m d -> b (m d)"),
                                                 ps[0:B, 3 * l:3 * l + 3, :].rearrange("b n f -> b (n f)")))
                    o.settle()
                    scales = row[:, l, CA:CB + 1:3, :]
                    gates = row[:, l, GA:GBI + 1:3, :]
                    o.mark(nc.vector.tensor_scalar_add(scales, scales, 1.0))
                    o.mark(nc.vector.tensor_scalar(sign[:, l], gates, 0.0, 2.0, ALU.is_ge, ALU.mult))
                    o.mark(nc.vector.scalar_tensor_tensor(neg[:, l], gates, -1.0, gates, ALU.mult, ALU.max))
                    o.settle()
                    o.mark(nc.vector.tensor_scalar_max(neg[:, l], neg[:, l], GATE_MIN))
                    o.settle()
                    nc.vector.scalar_tensor_tensor(gates, sign[:, l], 1.0, neg[:, l], ALU.subtract, ALU.mult).then_inc(row_ready, 1)
                dve.wait_ge(id_in, 16)
                nc.vector.tensor_copy(k.identb[:], k.ident[:])


def stage_linear_attention_sums(k):
    nc, io = k.nc, k.io
    with ExitStack() as ctx:
        def sb(name, shape, dt=F32):
            return ctx.enter_context(nc.sbuf_tensor(name, shape, dt))

        def psum(name, shape):
            return ctx.enter_context(nc.psum_tensor(name, shape, F32))

        def sem(name):
            return k.ctx.enter_context(nc.semaphore(name))

        KV = P + 1
        wq = sb("wq", [P, DC, D])
        wkv = sb("wkv", [P, DC, 2 * D])
        bq = sb("bq", [P, DC])
        bkv = sb("bkv", [P, 2 * D])
        stats = sb("a_stats", [P, G, 6])
        mv = sb("a_mv", [P, G, 2])
        std = sb("a_std", [P, G])
        xn = sb("a_xn", [P, G, D])
        h = sb("a_h", [P, G, D])
        hT = sb("a_hT", [P, DC, GT])
        qT = sb("a_qT", [P, DC, GT])
        kv = sb("a_kv", [P, 2, 2 * D + 1])
        hT_ps = psum("hT_ps", [P, DC, 512])
        q_ps = psum("q_ps", [P, DC, 512])
        kv_ps = psum("kv_ps", [P, 2, 512])
        sum_ps = psum("sum_ps", [P, DC, 512])

        w_in, const_ready = sem("a_w_in"), sem("a_const")
        dve_steps, stats_ready, std_ready, h_ready = sem("a_dve"), sem("a_stats"), sem("a_std"), sem("a_h")
        hT_done, hT_ready, q_done, q_ready = sem("a_hT"), sem("a_hTr"), sem("a_q"), sem("a_qr")
        kv_done, kv_added, kv_ready = sem("a_kvd"), sem("a_kva"), sem("a_kvr")
        sums_done, sums_read = sem("a_sd"), sem("a_sr")
        h_out, q_out = sem("a_ho"), sem("a_qo")
        W_IN = 16 * (3 + DC + 2)
        with nc.Block() as block:
            @block.sync
            def _(sp):
                sp.dma_start(wq[:], io["L0_WqT"].rearrange("(c p) n -> p c n", p=P)).then_inc(w_in, 16)
                sp.dma_start(wkv[:, :, 0:D], io["L0_WkT"].rearrange("(c p) n -> p c n", p=P)).then_inc(w_in, 16)
                sp.dma_start(wkv[:, :, D:2 * D], io["L0_WvT"].rearrange("(c p) n -> p c n", p=P)).then_inc(w_in, 16)
                for c in range(DC):
                    sp.dma_start(bq[:, c:c + 1], io["L0_attn_bq"][c * P:(c + 1) * P].rearrange("(p o) -> p o", o=1)).then_inc(w_in, 16)
                sp.dma_start(bkv[:, 0:D], io["L0_attn_bk"].partition_broadcast(P)).then_inc(w_in, 16)
                sp.dma_start(bkv[:, D:2 * D], io["L0_attn_bv"].partition_broadcast(P)).then_inc(w_in, 16)
                sp.nop().then_inc(h_out, 16)
                sp.nop().then_inc(q_out, 16)
                with sp.Fori(0, NG) as g:
                    sp.wait_ge(h_ready, g + 1)
                    sp.dma_start(k.h_dram[bass.ts(g, GT), :].rearrange("(s p) d -> p s d", p=P), h[:]).then_inc(h_out, 16)
                    wait_alone(sp, q_ready, DC * (g + 1))
                    sp.dma_start(k.qT_dram[:, :, bass.ts(g, GT)].rearrange("c p n -> p c n"), qT[:]).then_inc(q_out, 16)
                sp.wait_ge(h_out, 16 * (NG + 1))
                sp.wait_ge(q_out, 16 * (NG + 1))

            @block.vector
            def _(dve):
                o = Order(dve, dve_steps)
                nc.vector.memset(k.kvsum[:], 0.0).then_inc(const_ready, 1)
                nc.vector.memset(kv[:, :, 2 * D:], 1.0).then_inc(const_ready, 1)
                dve.wait_ge(const_ready, 2)
                LN_STEPS = G + 1 + G + 1

                def statistics(g):
                    for s in range(G):
                        o.mark(nc.vector.bn_stats(stats[:, s, :], k.x[:, bass.ds(g * G + s, 1), :]))
                    o.settle_alone()
                    for s in range(G):
                        nc.vector.bn_aggr(mv[:, s, :], stats[:, s, :]).then_inc(stats_ready, 1)

                def normalise(g):
                    dve.wait_ge(std_ready, g + 1)
                    o.mark(nc.vector.reciprocal(std[:], std[:]))
                    o.settle()
                    for s in range(G):
                        o.mark(nc.vector.tensor_scalar(xn[:, s, :], k.x[:, bass.ds(g * G + s, 1), :], mv[:, s, 0:1],
                                                       std[:, s:s + 1], ALU.subtract, ALU.mult))

                def scale(g):
                    o.settle()
                    by = k.mods[:, bass.ds(g // GB, 1), CA, :].to_broadcast([P, G, D])
                    o.mark(nc.vector.tensor_tensor(xn[:], xn[:], by, ALU.mult))

                def shift(g):
                    o.settle()
                    dve.wait_ge(h_out, 16 * (g + 1))
                    by = k.mods[:, bass.ds(g // GB, 1), SA, :].to_broadcast([P, G, D])
                    nc.vector.tensor_tensor(h[:], xn[:], by, ALU.add).then_inc(h_ready, 1)

                def tile(g, s):
                    dve.wait_ge(kv_done, g * G + s + 1)
                    if s >= 2:
                        dve.wait_ge(sums_done, g * G + s - 1)
                    nc.vector.tensor_tensor(kv[:, s % 2, 0:2 * D], kv_ps[:, s % 2, :], bkv[:], ALU.add).then_inc(kv_added, 1)
                    dve.wait_ge(kv_added, g * G + s + 1)
                    nc.vector.tensor_scalar_max(kv[:, s % 2, 0:D], kv[:, s % 2, 0:D], 0.0).then_inc(kv_ready, 1)

                def collect(g):
                    dve.wait_ge(sums_done, (g + 1) * G)
                    acc = k.kvsum[:, bass.ds(g // GB, 1), :, :]
                    nc.vector.tensor_tensor(acc, sum_ps[:, :, 0:KV], acc, ALU.add).then_inc(sums_read, 1)
                    dve.wait_ge(sums_read, g + 1)

                statistics(0)
                normalise(0)
                scale(0)
                shift(0)
                dve.wait_ge(w_in, W_IN)
                with dve.Fori(0, NG - 1) as g:
                    o.turn(g, LN_STEPS, LN_STEPS)
                    statistics(g + 1)
                    tile(g, 0)
                    normalise(g + 1)
                    tile(g, 1)
                    scale(g + 1)
                    tile(g, 2)
                    shift(g + 1)
                    tile(g, 3)
                    collect(g)
                    assert o.n == LN_STEPS
                for s in range(G):
                    tile(NG - 1, s)
                collect(NG - 1)

            @block.scalar
            def _(act):

                def deviation(g):
                    act.wait_ge(stats_ready, (g + 1) * G)
                    nc.scalar.activation(std[:], mv[:, :, 1], ACT.Sqrt, bias=k.eps[:, 0:1]).then_inc(std_ready, 1)

                def turned(g):
                    act.wait_ge(hT_done, g + 1)
                    nc.scalar.copy(hT[:], hT_ps[:]).then_inc(hT_ready, 1)

                def queries(g):
                    act.wait_ge(q_done, g + 1)
                    act.wait_ge(q_out, 16 * (g + 1))
                    for c in range(DC):
                        nc.scalar.activation(qT[:, c, :], q_ps[:, c, :], ACT.Relu, bias=bq[:, c:c + 1]).then_inc(q_ready, 1)

                deviation(0)
                turned(0)
                act.wait_ge(w_in, W_IN)
                with act.Fori(0, NG - 1) as g:
                    deviation(g + 1)
                    queries(g)
                    turned(g + 1)
                queries(NG - 1)

            @block.tensor
            def _(pe):

                def transposes(g):
                    pe.wait_ge(h_ready, g + 1)
                    for c in range(DC):
                        for s in range(G):
                            mm = nc.tensor.transpose(hT_ps[:, c, s * P:(s + 1) * P], h[:, s, c * P:(c + 1) * P], k.ident[:])
                    mm.then_inc(hT_done, 1)

                def queries(g):
                    pe.wait_ge(hT_ready, g + 1)
                    if not (isinstance(g, int) and g == 0):
                        pe.wait_ge(q_ready, DC * g)
                    for m in range(DC):
                        for c in range(DC):
                            mm = nc.tensor.matmul(q_ps[:, m, :], wq[:, c, m * P:(m + 1) * P], hT[:, c, :],
                                                  start=(c == 0), stop=(c == DC - 1))
                    mm.then_inc(q_done, 1)

                def sums(g, s):
                    pe.wait_ge(kv_ready, g * G + s + 1)
                    for c in range(DC):
                        for lo, hi, col in ((0, P, D + c * P), (P, KV, 2 * D)):
                            mm = nc.tensor.matmul(sum_ps[:, c, lo:hi], kv[:, s % 2, c * P:(c + 1) * P],
                                                  kv[:, s % 2, col:col + hi - lo], start=(s == 0 and lo == 0),
                                                  stop=(s == G - 1), skip_group_check=True)
                    mm.then_inc(sums_done, 1)

                def keys_values(g, s):
                    if s >= 2:
                        pe.wait_ge(kv_added, g * G + s - 1)
                    for c in range(DC):
                        mm = nc.tensor.matmul(kv_ps[:, s % 2, :], hT[:, c, s * P:(s + 1) * P], wkv[:, c, :],
                                              start=(c == 0), stop=(c == DC - 1))
                    mm.then_inc(kv_done, 1)

                def group(g, ahead):
                    for s in range(G):
                        keys_values(g, s)
                        if s == 1 and not (isinstance(g, int) and g == 0):
                            pe.wait_ge(sums_read, g)
                        if s >= 1:
                            sums(g, s - 1)
                    if ahead:
                        transposes(g + 1)
                    sums(g, G - 1)
                    if ahead:
                        queries(g + 1)

                transposes(0)
                pe.wait_ge(w_in, W_IN)
                queries(0)
                group(0, True)
                with pe.Fori(1, NG - 1) as g:
                    group(g, True)
                group(NG - 1, False)


def scratch(k, ctx):
    nc = k.nc

    def sb(name, shape, dt=F32):
        return ctx.enter_context(nc.sbuf_tensor(name, shape, dt))

    def psum(name, shape, dt=F32):
        return ctx.enter_context(nc.psum_tensor(name, shape, dt))

    def sem(name):
        return k.ctx.enter_context(nc.semaphore(name))

    return sb, psum, sem


def stage_linear_attention_apply(k):
    nc, io = k.nc, k.io
    with ExitStack() as ctx:
        sb, psum, sem = scratch(k, ctx)
        mask = sb("b_mask", [P, P + HC])
        kvd = sb("b_kvd", [P, B, DC, P + HC])
        router = sb("b_router", [P, DC, E])
        gamma = sb("b_gamma", [P, B, D])
        beta = sb("b_beta", [P, B, D])
        h = sb("b_h", [P, G, D])
        qT = sb("b_qT", [P, DC, GT])
        rden = sb("b_rden", [P, G, H])
        y = sb("b_y", [P, G, D])
        stats = sb("b_stats", [P, 2, G, 6])
        mv = sb("b_mv", [P, 2, G, 2])
        std = sb("b_std", [P, 2, G])
        shift = sb("b_shift", [P, 2, G])
        xn = sb("b_xn", [P, 2, G, D])
        h2 = sb("b_h2", [P, G, D])
        h2T = sb("b_h2T", [P, DC, GT])
        ctx_ps = psum("ctx_ps", [P, G, 512])
        hT_ps = psum("b_hT_ps", [P, DC, 512])
        lg_ps = psum("lg_ps", [P, 512])

        w_in = sem("b_w_in")
        y_steps, x_steps, kvd_ready, beta_ready, x_based = sem("b_ysteps"), sem("b_xsteps"), sem("b_kvd"), sem("b_beta"), sem("b_xb")
        h_in, q_in, ctx_done, ctx_read, h_used = sem("b_hin"), sem("b_qin"), sem("b_ctx"), sem("b_ctxr"), sem("b_hu")
        stats_ready, std_ready, rstd_ready, xn_ready = ([sem(f"b_{n}{w}") for w in "yx"] for n in ("st", "std", "rstd", "xn"))
        h2_ready, h2_out = sem("b_h2"), sem("b_h2o")
        hT_done, hT_ready, lg_done, lg_read = sem("b_hT"), sem("b_hTr"), sem("b_lg"), sem("b_lgr")

        with nc.Block() as block:
            @block.sync
            def _(sp):
                sp.dma_start(mask[:], io["head_mask"]).then_inc(w_in, 16)
                sp.dma_start(router[:], io["L0_router"].rearrange("(c p) n -> p c n", p=P)).then_inc(w_in, 16)
                for b in range(B):
                    sp.dma_start(gamma[:, b, :], io["L0_attn_gamma"].partition_broadcast(P)).then_inc(w_in, 16)
                    sp.dma_start(beta[:, b, :], io["L0_attn_beta"].partition_broadcast(P)).then_inc(w_in, 16)
                sp.nop().then_inc(h2_out, 16)

                def load(g):
                    wait_alone(sp, ctx_done, g + 1)
                    sp.dma_start(qT[:], k.qT_dram[:, :, bass.ts(g, GT)].rearrange("c p n -> p c n")).then_inc(q_in, 16)
                    sp.wait_ge(h_used, g + 1)
                    sp.dma_start(h[:], k.h_dram[bass.ts(g, GT), :].rearrange("(s p) d -> p s d", p=P)).then_inc(h_in, 16)

                def store(g):
                    sp.wait_ge(h2_ready, g + 1)
                    sp.dma_start(k.h2_dram[bass.ts(g, GT), :].rearrange("(s p) d -> p s d", p=P), h2[:]).then_inc(h2_out, 16)

                def weights(e):
                    if not isinstance(e, int):
                        sp.wait_ge(k.w_moe_in, 48 * e)
                    for n, t in (("L0_gate", k.wg), ("L0_up", k.wu), ("L0_down", k.wd)):
                        sp.dma_start(t[:, bass.ds(e, 1)].rearrange("p e c f -> p (e c) f"),
                                     io[n][bass.ds(e, 1)].rearrange("e (c p) f -> p (e c) f", p=P)).then_inc(k.w_moe_in, 16)

                load(0)
                weights(0)
                load(1)
                with sp.Fori(2, NG) as g:
                    load(g)
                    weights(g - 1)
                    store(g - 2)
                weights(NG - 1)
                store(NG - 2)
                store(NG - 1)
                sp.wait_ge(k.w_moe_in, 48 * E)
                sp.wait_ge(h2_out, 16 * (NG + 1))

            @block.gpsimd
            def _(pool):
                pool.wait_ge(beta_ready, 1)

                def base(g):
                    by = beta[:, bass.ds(g // GB, 1), :].to_broadcast([P, G, D])
                    xg = k.x[:, bass.ds(g * G, G), :]
                    nc.gpsimd.tensor_tensor(xg, xg, by, ALU.add).then_inc(x_based, 1)

                def add_h(g):
                    pool.wait_ge(ctx_read, g + 1)
                    wait_alone(pool, h_in, 16 * (g + 1))
                    nc.gpsimd.tensor_tensor(y[:], y[:], h[:], ALU.add).then_inc(h_used, 1)

                base(0)
                with pool.Fori(0, NG - 1) as g:
                    add_h(g)
                    base(g + 1)
                add_h(NG - 1)

            @block.vector
            def _(dve):
                oy, ox = Order(dve, y_steps), Order(dve, x_steps)
                dve.wait_ge(w_in, 16 * (2 + 2 * B))
                for b in range(B):
                    for c in range(DC):
                        nc.vector.tensor_tensor(kvd[:, b, c, 0:P], k.kvsum[:, b, c, 0:P], mask[:, 0:P], ALU.mult).then_inc(kvd_ready, 1)
                        nc.vector.tensor_scalar_mul(kvd[:, b, c, P:], mask[:, P:], k.kvsum[:, b, c, P:P + 1]).then_inc(kvd_ready, 1)
                    ox.mark(nc.vector.tensor_tensor(gamma[:, b, :], gamma[:, b, :], k.mods[:, b, GA, :], ALU.mult))
                nc.vector.tensor_tensor(beta[:], beta[:], k.mods[:, :, GA, :], ALU.mult).then_inc(beta_ready, 1)
                Y_STEPS, X_STEPS = 2 + G + 1, 2 + G + 1 + 1

                def statistics(o, w, src):
                    for s in range(G):
                        o.mark(nc.vector.bn_stats(stats[:, w, s, :], src(s)))
                    o.settle_alone()
                    for s in range(G):
                        nc.vector.bn_aggr(mv[:, w, s, :], stats[:, w, s, :]).then_inc(stats_ready[w], 1)

                def deviation(o, w, g):
                    dve.wait_ge(std_ready[w], g + 1)
                    o.mark(nc.vector.reciprocal(std[:, w], std[:, w]))
                    o.settle()
                    nc.vector.scalar_tensor_tensor(shift[:, w], mv[:, w, :, 0], -1.0, std[:, w], ALU.mult, ALU.mult).then_inc(rstd_ready[w], 1)

                def attended(g):
                    oy.turn(g, 0, Y_STEPS)
                    dve.wait_ge(ctx_done, g + 2)
                    den = ctx_ps[:, :, D:D + H]
                    oy.mark(nc.vector.tensor_scalar_max(rden[:], den, DENOM_EPS))
                    oy.settle()
                    oy.mark(nc.vector.reciprocal(rden[:], rden[:]))
                    oy.settle()
                    nc.vector.tensor_tensor(y[:].rearrange("p s (h d) -> p s h d", d=DH),
                                            ctx_ps[:, :, 0:D].rearrange("p s (h d) -> p s h d", d=DH),
                                            rden[:].unsqueeze(3).to_broadcast([P, G, H, DH]), ALU.mult).then_inc(ctx_read, 1)

                def y_statistics(g):
                    wait_alone(dve, h_used, g + 2)
                    statistics(oy, 0, lambda s: y[:, s, :])

                def residual(g):
                    ox.turn(g, B, X_STEPS)
                    dve.wait_ge(xn_ready[0], (g + 1) * G)
                    ox.mark(nc.vector.tensor_tensor(xn[:, 0], xn[:, 0], gamma[:, bass.ds(g // GB, 1), :].to_broadcast([P, G, D]), ALU.mult))
                    ox.settle()
                    dve.wait_ge(x_based, g + 1)
                    xg = k.x[:, bass.ds(g * G, G), :]
                    ox.mark(nc.vector.tensor_tensor(xg, xg, xn[:, 0], ALU.add))

                def x_statistics(g):
                    ox.settle_alone()
                    statistics(ox, 1, lambda s: k.x[:, bass.ds(g * G + s, 1), :])

                def ffn_input(g):
                    dve.wait_ge(xn_ready[1], (g + 1) * G)
                    ox.mark(nc.vector.tensor_tensor(xn[:, 1], xn[:, 1], k.mods[:, bass.ds(g // GB, 1), CB, :].to_broadcast([P, G, D]), ALU.mult))
                    ox.settle()
                    dve.wait_ge(h2_out, 16 * (g + 1))
                    dve.wait_ge(hT_done, g + 1)
                    by = k.mods[:, bass.ds(g // GB, 1), SB, :].to_broadcast([P, G, D])
                    nc.vector.tensor_tensor(h2[:], xn[:, 1], by, ALU.add).then_inc(h2_ready, 1)

                def logits(g):
                    dve.wait_ge(lg_done, g + 1)
                    nc.vector.tensor_copy(k.logits[:, bass.ds(g * G, G), :], lg_ps[:, 0:G * E].rearrange("p (s e) -> p s e", e=E)).then_inc(lg_read, 1)

                def group(g, ahead):
                    residual(g)
                    if ahead:
                        attended(g + 1)
                    x_statistics(g)
                    if ahead:
                        y_statistics(g + 1)
                    deviation(ox, 1, g)
                    if ahead:
                        deviation(oy, 0, g + 1)
                    if not (isinstance(g, int) and g == 0):
                        logits(g - 1)
                    ffn_input(g)

                attended(0)
                y_statistics(0)
                deviation(oy, 0, 0)
                group(0, True)
                with dve.Fori(1, NG - 1) as g:
                    group(g, True)
                group(NG - 1, False)
                logits(NG - 1)

            @block.scalar
            def _(act):
                def deviation(w, g):
                    act.wait_ge(stats_ready[w], (g + 1) * G)
                    nc.scalar.activation(std[:, w], mv[:, w, :, 1], ACT.Sqrt, bias=k.eps[:, 0:1]).then_inc(std_ready[w], 1)

                def normalise(w, g, src):
                    act.wait_ge(rstd_ready[w], g + 1)
                    for s in range(G):
                        nc.scalar.activation(xn[:, w, s, :], src(s), ACT.Identity, bias=shift[:, w, s:s + 1],
                                             scale=std[:, w, s:s + 1]).then_inc(xn_ready[w], 1)

                def group(g, ahead):
                    deviation(1, g)
                    if ahead:
                        deviation(0, g + 1)
                    normalise(1, g, lambda s: k.x[:, bass.ds(g * G + s, 1), :].rearrange("p o d -> p (o d)"))
                    if ahead:
                        normalise(0, g + 1, lambda s: y[:, s, :])
                    act.wait_ge(hT_done, g + 2)
                    nc.scalar.copy(h2T[:], hT_ps[:]).then_inc(hT_ready, 1)

                deviation(0, 0)
                normalise(0, 0, lambda s: y[:, s, :])
                with act.Fori(0, NG - 1) as g:
                    group(g, True)
                group(NG - 1, False)

            @block.tensor
            def _(pe):
                pe.wait_ge(w_in, 16 * (2 + 2 * B))
                pe.wait_ge(kvd_ready, B * DC * 2)
                pe.nop().then_inc(ctx_done, 1)
                pe.nop().then_inc(h_used, 1)
                pe.nop().then_inc(hT_done, 1)
                pe.nop().then_inc(lg_read, 1)

                def context(g):
                    pe.wait_ge(q_in, 16 * (g + 1))
                    if not (isinstance(g, int) and g == 0):
                        pe.wait_ge(ctx_read, g)
                    for s in range(G):
                        for c in range(DC):
                            q = qT[:, c, s * P:(s + 1) * P]
                            nc.tensor.matmul(ctx_ps[:, s, c * P:(c + 1) * P], q, kvd[:, bass.ds(g // GB, 1), c, 0:P],
                                             start=True, stop=True, skip_group_check=True)
                            mm = nc.tensor.matmul(ctx_ps[:, s, D + c * HC:D + (c + 1) * HC], q, kvd[:, bass.ds(g // GB, 1), c, P:],
                                                  start=True, stop=True, skip_group_check=True)
                    mm.then_inc(ctx_done, 1)

                def route(g):
                    pe.wait_ge(h2_ready, g + 1)
                    for c in range(DC):
                        for s in range(G):
                            mm = nc.tensor.transpose(hT_ps[:, c, s * P:(s + 1) * P], h2[:, s, c * P:(c + 1) * P], k.ident[:])
                    mm.then_inc(hT_done, 1)
                    pe.wait_ge(hT_ready, g + 1)
                    pe.wait_ge(lg_read, g + 1)
                    for s in range(G):
                        for c in range(DC):
                            mm = nc.tensor.matmul(lg_ps[:, s * E:(s + 1) * E], h2T[:, c, s * P:(s + 1) * P], router[:, c, :],
                                                  start=(c == 0), stop=(c == DC - 1), skip_group_check=True)
                    mm.then_inc(lg_done, 1)

                context(0)
                context(1)
                with pe.Fori(0, NG - 2) as g:
                    context(g + 2)
                    route(g)
                route(NG - 2)
                route(NG - 1)


def stage_route(k):
    nc, io = k.nc, k.io
    with ExitStack() as ctx:
        sb, psum, sem = scratch(k, ctx)
        tri = sb("r_tri", [P, P])
        ones = sb("r_ones", [P, P])
        rank = sb("r_rank", [P, E])
        start = sb("r_start", [1, k.COLS])
        m = sb("r_m", [P, 4, NT])
        prob = sb("r_prob", [P, NT, E])
        key = sb("r_key", [P, NT, E])
        hot = sb("r_hot", [P, 2, NT, E])
        both = sb("r_both", [P, NT, E])
        run = sb("r_run", [P, 2, NT, E])
        cnt = sb("r_cnt", [P, 4, E])
        cnti = sb("r_cnti", [P, E], I32)
        slotf = sb("r_slotf", [P, NT, 2])
        cmp = sb("r_cmp", [1, k.COLS, E])
        eidf = sb("r_eidf", [1, k.COLS])
        iota = sb("r_iota", [P, P])
        ids = sb("r_ids", [P, NT])
        tilei = sb("r_tilei", [P, NT, 2], I32)
        tilef = sb("r_tilef", [P, NT, 2])
        place = sb("r_place", [P, NT, 2])
        at_place = sb("r_at_place", [P, 4, G, P])
        at_tile = sb("r_at_tile", [P, 4, G, k.COLS])
        wq = sb("r_wq", [P, 2 * PH, D])
        keys = sb("r_keys", [P, 2 * PH, KEYS])
        cnt_ps = psum("cnt_ps", [P, 2, NT * E])
        ws_ps = psum("ws_ps", [P, DC, SIMS])
        token_ps = psum("token_ps", [P, 512])
        ws_in, ws_done, ws_ready = sem("r_wsi"), sem("r_wsd"), sem("r_wsr")
        w_in, steps, exped, both_ready, cnt_done = sem("r_w"), sem("r_steps"), sem("r_exp"), sem("r_both"), sem("r_cnt")
        hot_ready, numbered, hot_used, token_ready = sem("r_hr"), sem("r_num"), sem("r_hu"), sem("r_tok")

        with nc.Block() as block:
            @block.sync
            def _(sp):
                for t, n in ((tri, "tri"), (ones, "ones"), (rank, "rank"), (start, "tile_start"), (iota, "iota"), (ids, "ids")):
                    sp.dma_start(t[:], io[n]).then_inc(w_in, 16)
                sp.dma_start(wq[:], io["L1_wqT"].rearrange("(a p) d -> p a d", p=P)).then_inc(ws_in, 16)
                sp.dma_start(keys[:], io["L1_keysT"].rearrange("(a p) n -> p a n", p=P)).then_inc(ws_in, 16)

            @block.gpsimd
            def _(pool):
                def number(g, u):
                    for c in range(2):
                        wait_alone(pool, hot_ready, (g * 2 + c + 1) * 2)
                        nc.gpsimd.tensor_tensor(at_tile[:, 2 * u + c], at_tile[:, 2 * u + c],
                                                ids[:, bass.ds(g * G, G)].unsqueeze(2).to_broadcast([P, G, k.COLS]), ALU.mult).then_inc(numbered, 1)

                with pool.Fori(0, NG // 2) as i:
                    for u in range(2):
                        number(i * 2 + u, u)

            @block.scalar
            def _(act):
                act.wait_ge(exped, 1)
                nc.scalar.activation(prob[:], prob[:], ACT.Exp).then_inc(exped, 1)
                act.wait_ge(exped, 3)
                nc.scalar.activation(k.wts[:, 1, :], m[:, 3, :], ACT.Exp).then_inc(exped, 1)
                for c in range(DC):
                    act.wait_ge(ws_done, c + 1)
                    nc.scalar.copy(k.wsim[:, c, :], ws_ps[:, c, :]).then_inc(ws_ready, 1)
                act.wait_ge(ws_ready, DC)

            @block.tensor
            def _(pe):
                pe.wait_ge(w_in, 96)
                pe.wait_ge(both_ready, 1)
                flat = both[:].rearrange("p t e -> p (t e)")
                nc.tensor.matmul(cnt_ps[:, 0, :], tri[:], flat, start=True, stop=True, skip_group_check=True)
                nc.tensor.matmul(cnt_ps[:, 1, :], ones[:], flat, start=True, stop=True, skip_group_check=True).then_inc(cnt_done, 1)
                pe.wait_ge(ws_in, 32)
                for c in range(DC):
                    for a in range(2 * PH):
                        mm = nc.tensor.matmul(ws_ps[:, c, a * KEYS:(a + 1) * KEYS], wq[:, a, c * P:(c + 1) * P], keys[:, a, :],
                                              start=True, stop=True, skip_group_check=True)
                    mm.then_inc(ws_done, 1)

                def place_tokens(g, u, first):
                    for c in range(2):
                        pe.wait_ge(numbered, g * 2 + c + 1)
                        for s in range(G):
                            mm = nc.tensor.matmul(token_ps[:, 0:k.COLS], at_place[:, 2 * u + c, s, :], at_tile[:, 2 * u + c, s, :],
                                                  start=first and u == 0 and c == 0 and s == 0, stop=True, skip_group_check=True)
                        mm.then_inc(hot_used, 1)

                for u in range(2):
                    place_tokens(u, u, True)
                with pe.Fori(1, NG // 2) as i:
                    for u in range(2):
                        place_tokens(i * 2 + u, u, False)

            @block.vector
            def _(dve):
                o = Order(dve, steps)

                def step(instruction):
                    o.mark(instruction)
                    o.settle()

                V = nc.vector
                wide = [P, NT, E]
                dve.wait_ge(w_in, 96)
                step(V.reduce_max(m[:, 0, :], k.logits[:], AX.X))
                V.tensor_tensor(prob[:], k.logits[:], m[:, 0, :].unsqueeze(2).to_broadcast(wide), ALU.subtract).then_inc(exped, 1)
                dve.wait_ge(exped, 2)
                step(V.reduce_sum(m[:, 1, :], prob[:], AX.X))
                step(V.reciprocal(m[:, 1, :], m[:, 1, :]))
                step(V.tensor_tensor(prob[:], prob[:], m[:, 1, :].unsqueeze(2).to_broadcast(wide), ALU.mult))
                for c in range(2):
                    top = m[:, 2 * c, :]
                    step(V.reduce_max(top, prob[:], AX.X))
                    step(V.tensor_tensor(key[:], prob[:], top.unsqueeze(2).to_broadcast(wide), ALU.is_equal))
                    step(V.tensor_tensor(key[:], key[:], rank[:].unsqueeze(1).to_broadcast(wide), ALU.mult))
                    step(V.reduce_max(m[:, 3, :], key[:], AX.X))
                    step(V.tensor_tensor(hot[:, c], key[:], m[:, 3, :].unsqueeze(2).to_broadcast(wide), ALU.is_equal))
                    if c == 0:
                        step(V.scalar_tensor_tensor(prob[:], hot[:, 0], -2.0, prob[:], ALU.mult, ALU.add))
                V.tensor_tensor(both[:], hot[:, 0], hot[:, 1], ALU.add).then_inc(both_ready, 1)
                V.tensor_tensor(m[:, 3, :], m[:, 2, :], m[:, 0, :], ALU.subtract).then_inc(exped, 1)
                dve.wait_ge(exped, 4)
                step(V.tensor_scalar_add(m[:, 1, :], k.wts[:, 1, :], 1.0))
                step(V.reciprocal(k.wts[:, 0, :], m[:, 1, :]))
                step(V.tensor_tensor(k.wts[:, 1, :], k.wts[:, 1, :], k.wts[:, 0, :], ALU.mult))
                dve.wait_ge(cnt_done, 1)
                counts = cnt_ps[:, 1, :].rearrange("p (t e) -> p t e", e=E)
                step(V.tensor_copy(run[:, 0], counts))
                at, by = 0, 1
                while by < NT:
                    o.mark(V.tensor_copy(run[:, 1 - at, 0:by, :], run[:, at, 0:by, :]))
                    step(V.tensor_tensor(run[:, 1 - at, by:, :], run[:, at, by:, :], run[:, at, 0:NT - by, :], ALU.add))
                    at, by = 1 - at, 2 * by
                step(V.tensor_scalar_add(cnt[:, 0, :], run[:, at, NT - 1, :], float(P - 1)))
                step(V.tensor_copy(cnti[:], cnt[:, 0, :]))
                step(V.tensor_scalar(cnti[:], cnti[:], 7, 7, ALU.arith_shift_right, ALU.logical_shift_left))
                step(V.tensor_copy(cnt[:, 3, :], cnti[:]))
                step(V.tensor_copy(cnt[:, 0, :], cnt[:, 3, :]))
                a, by = 0, 1
                while by < E:
                    o.mark(V.tensor_copy(cnt[:, 1 - a, 0:by], cnt[:, a, 0:by]))
                    step(V.tensor_tensor(cnt[:, 1 - a, by:], cnt[:, a, by:], cnt[:, a, 0:E - by], ALU.add))
                    a, by = 1 - a, 2 * by
                end = cnt[:, a, :]
                step(V.tensor_tensor(cnt[:, 2, :], end, cnt[:, 3, :], ALU.subtract))
                step(V.tensor_tensor(run[:, at], run[:, at], counts, ALU.subtract))
                step(V.tensor_tensor(run[:, at], run[:, at], cnt_ps[:, 0, :].rearrange("p (t e) -> p t e", e=E), ALU.add))
                step(V.tensor_tensor(run[:, at], run[:, at], cnt[:, 2, :].unsqueeze(1).to_broadcast(wide), ALU.add))
                for c in range(2):
                    step(V.tensor_tensor(key[:], hot[:, c], run[:, at], ALU.mult))
                    step(V.reduce_sum(slotf[:, :, c], key[:], AX.X))
                step(V.tensor_copy(k.slots[:], slotf[:]))
                row = [1, k.COLS, E]
                step(V.tensor_tensor(cmp[:], start[:].unsqueeze(2).to_broadcast(row), end[0:1, :].unsqueeze(1).to_broadcast(row), ALU.is_ge))
                step(V.reduce_sum(eidf[:], cmp[:], AX.X))
                step(V.tensor_scalar_min(eidf[:], eidf[:], float(E - 1)))
                step(V.tensor_copy(k.eid[:], eidf[:]))
                step(V.tensor_scalar(tilei[:], k.slots[:], 7, None, ALU.arith_shift_right))
                step(V.tensor_copy(tilef[:], tilei[:]))
                step(V.scalar_tensor_tensor(place[:], tilef[:], -float(P), slotf[:], ALU.mult, ALU.add))

                def one_hot(g, u, first):
                    for c in range(2):
                        if not first:
                            dve.wait_ge(hot_used, g * 2 + c - 3)
                        tiles = bass.ds(g * G, G)
                        V.tensor_tensor(at_place[:, 2 * u + c], iota[:].unsqueeze(1).to_broadcast([P, G, P]),
                                        place[:, tiles, c].unsqueeze(2).to_broadcast([P, G, P]), ALU.is_equal).then_inc(hot_ready, 1)
                        V.tensor_tensor(at_tile[:, 2 * u + c], iota[:, 0:k.COLS].unsqueeze(1).to_broadcast([P, G, k.COLS]),
                                        tilef[:, tiles, c].unsqueeze(2).to_broadcast([P, G, k.COLS]), ALU.is_equal).then_inc(hot_ready, 1)

                for u in range(2):
                    one_hot(u, u, True)
                with dve.Fori(1, NG // 2) as i:
                    for u in range(2):
                        one_hot(i * 2 + u, u, False)
                dve.wait_ge(hot_used, 2 * NG)
                V.tensor_copy(k.token[:], token_ps[:, 0:k.COLS]).then_inc(token_ready, 1)


def stage_experts(k):
    nc = k.nc
    with ExitStack() as ctx:
        sb, psum, sem = scratch(k, ctx)
        X = sb("e_x", [P, D])
        sl = sb("e_sl", [P, 1], I32)
        XT = sb("e_xT", [P, DC, P])
        act_g = sb("e_silu", [P, F])
        fuse = sb("e_fuse", [P, F])
        fuseT = sb("e_fuseT", [P, FC, P])
        Y = sb("e_y", [P, D])
        xT_ps = psum("e_xT_ps", [P, DC, P])
        g_ps = psum("e_g_ps", [P, F])
        u_ps = psum("e_u_ps", [P, F])
        fT_ps = psum("e_fT_ps", [P, FC, P])
        y_ps = psum("e_y_ps", [P, 512])
        sl_ready = sem("e_sl")
        x_in, xT_done, xT_ready = sem("e_xin"), sem("e_xTd"), sem("e_xTr")
        g_done, u_done, silu_done, fuse_ready = sem("e_gd"), sem("e_ud"), sem("e_sd"), sem("e_fr")
        fT_done, fT_ready, y_done, y_ready, y_out = sem("e_fTd"), sem("e_fTr"), sem("e_yd"), sem("e_yr"), sem("e_yo")
        TILES = k.TILES

        with nc.Block() as block:
            @block.gpsimd
            def _(pool):
                def gather(j):
                    wait_alone(pool, sl_ready, j + 1)
                    nc.gpsimd.indirect_dma_start(X[:], None, k.h2_dram, bass.IndirectOffsetOnAxis(ap=sl[:, 0:1], axis=0)).then_inc(x_in, 16)

                gather(0)
                with pool.Fori(0, TILES) as j:
                    pool.wait_ge(xT_done, j + 1)
                    gather(j + 1)

            @block.tensor
            def _(pe):
                pe.wait_ge(k.w_moe_in, 48 * E)

                def transpose_x(j):
                    pe.wait_ge(x_in, 16 * (j + 1))
                    for c in range(DC):
                        mm = nc.tensor.transpose(xT_ps[:, c, :], X[:, c * P:(c + 1) * P], k.ident[:])
                    mm.then_inc(xT_done, 1)

                def into(j):
                    e = pe.value_load(k.eid[0:1, bass.ds(j, 1)], min_val=0, max_val=E - 1)
                    pe.wait_ge(xT_ready, j + 1)
                    for ps, w, done in ((g_ps, k.wg, g_done), (u_ps, k.wu, u_done)):
                        for c in range(DC):
                            mm = nc.tensor.matmul(ps[:], XT[:, c, :], w[:, bass.ds(e, 1), c, :], start=(c == 0), stop=(c == DC - 1))
                        mm.then_inc(done, 1)

                def out_of(j, first):
                    e = pe.value_load(k.eid[0:1, bass.ds(j, 1)], min_val=0, max_val=E - 1)
                    pe.wait_ge(fT_ready, j + 1)
                    if not first:
                        pe.wait_ge(y_ready, j)
                    for c in range(FC):
                        mm = nc.tensor.matmul(y_ps[:, 0:D], fuseT[:, c, :], k.wd[:, bass.ds(e, 1), c, :], start=(c == 0), stop=(c == FC - 1))
                    mm.then_inc(y_done, 1)

                def transpose_fuse(j):
                    pe.wait_ge(fuse_ready, j + 1)
                    for c in range(FC):
                        mm = nc.tensor.transpose(fT_ps[:, c, :], fuse[:, c * P:(c + 1) * P], k.ident[:])
                    mm.then_inc(fT_done, 1)

                transpose_x(0)
                into(0)
                transpose_x(1)
                transpose_fuse(0)
                into(1)
                out_of(0, True)
                transpose_x(2)
                transpose_fuse(1)
                with pe.Fori(2, TILES) as j:
                    into(j)
                    out_of(j - 1, False)
                    transpose_x(j + 1)
                    transpose_fuse(j)
                out_of(TILES - 1, False)

            @block.scalar
            def _(act):
                def silu(j):
                    act.wait_ge(g_done, j + 1)
                    nc.scalar.activation(act_g[:], g_ps[:], ACT.Silu).then_inc(silu_done, 1)

                def store(j, first):
                    act.wait_ge(y_done, j + 1)
                    if not first:
                        act.wait_ge(y_out, 16 * j)
                    nc.scalar.copy(Y[:], y_ps[:, 0:D]).then_inc(y_ready, 1)
                    act.wait_ge(y_ready, j + 1)
                    act.dma_start(k.ys_dram[bass.ts(j, P), :], Y[:]).then_inc(y_out, 16)

                silu(0)
                act.wait_ge(fuse_ready, 1)
                silu(1)
                store(0, True)
                with act.Fori(2, TILES) as j:
                    act.wait_ge(fuse_ready, j)
                    silu(j)
                    store(j - 1, False)
                store(TILES - 1, False)
                act.wait_ge(y_out, 16 * TILES)

            @block.vector
            def _(dve):
                def x_copy(j):
                    dve.wait_ge(xT_done, j + 1)
                    nc.vector.tensor_copy(XT[:], xT_ps[:]).then_inc(xT_ready, 1)

                def fuse_mul(j):
                    dve.wait_ge(silu_done, j + 1)
                    dve.wait_ge(u_done, j + 1)
                    nc.vector.tensor_tensor(fuse[:], u_ps[:], act_g[:], ALU.mult).then_inc(fuse_ready, 1)

                def fuse_copy(j):
                    dve.wait_ge(fT_done, j + 1)
                    nc.vector.tensor_copy(fuseT[:], fT_ps[:]).then_inc(fT_ready, 1)

                def ask(j):
                    nc.vector.tensor_copy(sl[:], k.token[:, bass.ds(j, 1)]).then_inc(sl_ready, 1)

                ask(0)
                x_copy(0)
                ask(1)
                with dve.Fori(0, TILES) as j:
                    fuse_mul(j)
                    x_copy(j + 1)
                    ask(j + 2)
                    fuse_copy(j)


PARTS = 3


def stage_project(k):
    nc, io = k.nc, k.io
    with ExitStack() as ctx:
        sb, psum, sem = scratch(k, ctx)
        gb0 = sb("c_gb0", [P, B, D])
        wqkv = sb("c_wqkv", [P, DC, 3 * D])
        rope = sb("c_rope", [P, 2, S // P, DH])
        Y = sb("c_y", [P, 2, G, 2, D])
        sl = sb("c_sl", [P, 2, G * 2], I32)
        mix = sb("c_mix", [P, G, D])
        stats = sb("c_stats", [P, G, 6])
        mv = sb("c_mv", [P, G, 2])
        std = sb("c_std", [P, G])
        xn = sb("c_xn", [P, G, D])
        h = sb("c_h", [P, G, D])
        hT = sb("c_hT", [P, DC, GT])
        t1 = sb("c_t1", [P, 2 * H, DH])
        t2 = sb("c_t2", [P, 2 * H, DH])
        rot = sb("c_rot", [P, 2, 2 * D])
        rest = sb("c_rest", [P, 2 * DC, GT])
        upd = sb("c_upd", [P, G, D])
        parts = sb("c_parts", [P, 2 * DC, PARTS, GT], BF16)
        hT_ps = psum("c_hT_ps", [P, DC, 512])
        qk_ps = psum("c_qk_ps", [P, 512])
        v_ps = psum("c_v_ps", [P, 512])
        T_ps = psum("c_T_ps", [P, 2 * DC, 512])
        HALF = DH // 2

        w_in, steps, sl_ready, mix_used = sem("c_w"), sem("c_steps"), sem("c_sl"), sem("c_mu")
        y_in = [sem(f"c_yin{u}") for u in range(2)]
        stats_ready, std_ready, h_ready = sem("c_st"), sem("c_std"), sem("c_h")
        hT_done, hT_ready, first_ready = sem("c_hT"), sem("c_hTr"), sem("c_first")
        qk_done, v_done, v_read, rot_ready, T_done = sem("c_qk"), sem("c_v"), sem("c_vr"), sem("c_rot"), sem("c_T")
        hi_ready, rest_ready, mid_ready, low_ready, parts_out = sem("c_hi"), sem("c_rest"), sem("c_mid"), sem("c_low"), sem("c_po")

        with nc.Block() as block:
            @block.sync
            def _(sp):
                sp.dma_start(gb0[:], k.modrow_dram[0][:, GBI, :].partition_broadcast(P)).then_inc(w_in, 16)
                sp.dma_start(k.mods[:].rearrange("p b m d -> p (b m d)"),
                             k.modrow_dram[1].rearrange("b m d -> (b m d)").partition_broadcast(P)).then_inc(w_in, 16)
                sp.dma_start(wqkv[:], io["L1_Wqkv"].rearrange("(c p) n -> p c n", p=P)).then_inc(w_in, 16)
                sp.dma_start(rope[:].rearrange("p a t d -> p (a t) d"), io["rope"].rearrange("a (t p) d -> p (a t) d", p=P)).then_inc(w_in, 16)
                sp.nop().then_inc(parts_out, 16 * 2 * DC)
                with sp.Fori(0, NG) as g:
                    for c in range(2 * DC):
                        sp.wait_ge(low_ready, (g + 1) * 2 * DC + c + 1)
                        sp.dma_start(k.qk_dram[c, :, :, bass.ts(g, GT)].rearrange("a p n -> p a n"), parts[:, c]).then_inc(parts_out, 16)
                sp.wait_ge(parts_out, 16 * 2 * DC * (NG + 1))

            @block.gpsimd
            def _(pool):
                def gather(i, u):
                    wait_alone(pool, sl_ready, i * 2 + u + 1)
                    for s in range(G):
                        for c in range(2):
                            nc.gpsimd.indirect_dma_start(Y[:, u, s, c, :], None, k.ys_dram,
                                                         bass.IndirectOffsetOnAxis(ap=sl[:, u, s * 2 + c:s * 2 + c + 1], axis=0),
                                                         ).then_inc(y_in[u], 16)

                def lesser(g):
                    for c in range(2 * DC):
                        pool.wait_ge(mid_ready, g * 2 * DC + c + 1)
                        nc.gpsimd.tensor_tensor(parts[:, c, 2, :], rest[:, c, :], parts[:, c, 1, :], ALU.subtract).then_inc(low_ready, 1)

                gather(0, 0)
                gather(0, 1)
                with pool.Fori(0, NG // 2 - 1) as i:
                    for u in range(2):
                        gather(i + 1, u)
                        lesser(i * 2 + u)
                lesser(NG - 2)
                lesser(NG - 1)

            @block.vector
            def _(dve):
                o = Order(dve, steps)
                V = nc.vector
                mod = lambda g, t, m: t[:, bass.ds(g // GB, 1), m, :].to_broadcast([P, G, D])

                def ask(g, u):
                    V.tensor_copy(sl[:, u, :], k.slots[:, bass.ds(g * G, G), :].rearrange("p t c -> p (t c)")).then_inc(sl_ready, 1)

                def mix_second(i, u, more):
                    g = i * 2 + u
                    dve.wait_ge(first_ready, (g + 1) * G)
                    for s in range(G):
                        o.mark(V.scalar_tensor_tensor(mix[:, s, :], Y[:, u, s, 1, :], k.wts[:, 1, bass.ds(g * G + s, 1)],
                                                      mix[:, s, :], ALU.mult, ALU.add))
                    o.settle()
                    if more:
                        ask(g + 2, u)
                    V.tensor_tensor(upd[:], mix[:], gb0[:, bass.ds(g // GB, 1), :].to_broadcast([P, G, D]), ALU.mult).then_inc(mix_used, 1)

                def residual(g):
                    dve.wait_ge(mix_used, g + 2)
                    xg = k.x[:, bass.ds(g * G, G), :]
                    o.mark(V.tensor_tensor(xg, xg, upd[:], ALU.add))
                    o.settle_alone()
                    for s in range(G):
                        o.mark(V.bn_stats(stats[:, s, :], k.x[:, bass.ds(g * G + s, 1), :]))
                    o.settle_alone()
                    for s in range(G):
                        V.bn_aggr(mv[:, s, :], stats[:, s, :]).then_inc(stats_ready, 1)

                def normalise(g):
                    dve.wait_ge(std_ready, g + 1)
                    o.mark(V.reciprocal(std[:], std[:]))
                    o.settle()
                    for s in range(G):
                        o.mark(V.tensor_scalar(xn[:, s, :], k.x[:, bass.ds(g * G + s, 1), :], mv[:, s, 0:1], std[:, s:s + 1],
                                               ALU.subtract, ALU.mult))

                def shift(g):
                    o.settle()
                    o.mark(V.tensor_tensor(xn[:], xn[:], mod(g, k.mods, CA), ALU.mult))
                    o.settle()
                    dve.wait_ge(hT_done, g + 1)
                    V.tensor_tensor(h[:], xn[:], mod(g, k.mods, SA), ALU.add).then_inc(h_ready, 1)

                def rotate(g, s):
                    dve.wait_ge(qk_done, g * G + s + 1)
                    qk = qk_ps[:].rearrange("p (h d) -> p h d", d=DH)
                    tab = lambda a, lo, hi: rope[:, a, bass.ds((g % GB) * G + s, 1), lo:hi].to_broadcast([P, 2 * H, hi - lo])
                    o.mark(V.tensor_tensor(t1[:], qk, tab(0, 0, DH), ALU.mult))
                    o.mark(V.tensor_tensor(t2[:, :, 0:HALF], qk[:, :, HALF:], tab(1, 0, HALF), ALU.mult))
                    o.mark(V.tensor_tensor(t2[:, :, HALF:], qk[:, :, 0:HALF], tab(1, HALF, DH), ALU.mult))
                    o.settle()
                    if s >= 2:
                        dve.wait_ge(T_done, g * G + s - 1)
                    V.tensor_tensor(rot[:, s % 2, :].rearrange("p (h d) -> p h d", d=DH), t1[:], t2[:], ALU.add).then_inc(rot_ready, 1)
                    dve.wait_ge(rot_ready, g * G + s + 1)

                def remainders(g):
                    dve.wait_ge(T_done, (g + 1) * G)
                    for c in range(2 * DC):
                        dve.wait_ge(hi_ready, g * 2 * DC + c + 1)
                        dve.wait_ge(low_ready, g * 2 * DC + c + 1)
                        V.scalar_tensor_tensor(rest[:, c, :], T_ps[:, c, :], 0.25 if c < DC else 1.0, parts[:, c, 0, :],
                                               ALU.mult, ALU.subtract).then_inc(rest_ready, 1)

                ask(0, 0)
                ask(1, 1)
                dve.wait_ge(w_in, 64)
                FRONT = G + 1 + G + 1 + G + 1
                TURN = FRONT + 3 * G
                mix_second(0, 0, True)
                residual(0)
                normalise(0)
                shift(0)

                def group(i, u, ahead, more):
                    g = i * 2 + u
                    o.turn(g, FRONT, TURN)
                    rotate(g, 0)
                    if ahead:
                        mix_second(i + (u + 1) // 2, (u + 1) % 2, more)
                    rotate(g, 1)
                    if ahead:
                        residual(g + 1)
                    rotate(g, 2)
                    if ahead:
                        normalise(g + 1)
                        shift(g + 1)
                    rotate(g, 3)
                    remainders(g)

                with dve.Fori(0, NG // 2 - 2) as i:
                    for u in range(2):
                        group(i, u, True, True)
                for g in range(NG - 4, NG):
                    group(g // 2, g % 2, g + 1 < NG, g + 3 < NG)

            @block.scalar
            def _(act):
                def mix_first(i, u):
                    g = i * 2 + u
                    act.wait_ge(y_in[u], 16 * 2 * G * (i + 1))
                    act.wait_ge(mix_used, g + 1)
                    for s in range(G):
                        nc.scalar.activation(mix[:, s, :], Y[:, u, s, 0, :], ACT.Copy, scale=k.wts[:, 0, bass.ds(g * G + s, 1)]).then_inc(first_ready, 1)

                def deviation(g):
                    act.wait_ge(stats_ready, (g + 1) * G)
                    nc.scalar.activation(std[:], mv[:, :, 1], ACT.Sqrt, bias=k.eps[:, 0:1]).then_inc(std_ready, 1)

                def turned(g):
                    act.wait_ge(hT_done, g + 2)
                    nc.scalar.copy(hT[:], hT_ps[:]).then_inc(hT_ready, 1)

                def values(g, s):
                    act.wait_ge(v_done, g * G + s + 1)
                    nc.scalar.copy(k.v[:, bass.ds(g * G + s, 1), :, :].rearrange("p t h d -> p (t h d)"), v_ps[:, 0:D]).then_inc(v_read, 1)

                def high(g):
                    act.wait_ge(T_done, (g + 1) * G)
                    act.wait_ge(parts_out, 16 * 2 * DC * (g + 1))
                    for c in range(2 * DC):
                        nc.scalar.activation(parts[:, c, 0, :], T_ps[:, c, :], ACT.Copy, scale=0.25 if c < DC else 1.0).then_inc(hi_ready, 1)

                def middle(g):
                    for c in range(2 * DC):
                        act.wait_ge(rest_ready, g * 2 * DC + c + 1)
                        nc.scalar.copy(parts[:, c, 1, :], rest[:, c, :]).then_inc(mid_ready, 1)

                def group(i, u, ahead):
                    g = i * 2 + u
                    values(g, 0)
                    if ahead:
                        mix_first(i + (u + 1) // 2, (u + 1) % 2)
                    values(g, 1)
                    values(g, 2)
                    if ahead:
                        deviation(g + 1)
                    values(g, 3)
                    if ahead:
                        turned(g + 1)
                    high(g)
                    middle(g)

                mix_first(0, 0)
                deviation(0)
                turned(0)
                with act.Fori(0, NG // 2 - 1) as i:
                    group(i, 0, True)
                    group(i, 1, True)
                group(NG // 2 - 1, 0, True)
                group(NG // 2 - 1, 1, False)

            @block.tensor
            def _(pe):
                pe.wait_ge(w_in, 64)
                pe.nop().then_inc(mix_used, 1)
                pe.nop().then_inc(hT_done, 1)
                pe.nop().then_inc(low_ready, 2 * DC)

                def transposes(g):
                    pe.wait_ge(h_ready, g + 1)
                    for c in range(DC):
                        for s in range(G):
                            mm = nc.tensor.transpose(hT_ps[:, c, s * P:(s + 1) * P], h[:, s, c * P:(c + 1) * P], k.ident[:])
                    mm.then_inc(hT_done, 1)

                def turn_channels(g, s):
                    pe.wait_ge(rot_ready, g * G + s + 1)
                    for c in range(2 * DC):
                        mm = nc.tensor.transpose(T_ps[:, c, s * P:(s + 1) * P], rot[:, s % 2, c * P:(c + 1) * P], k.ident[:])
                    mm.then_inc(T_done, 1)

                def project(g, s):
                    for c in range(DC):
                        mm = nc.tensor.matmul(qk_ps[:], hT[:, c, s * P:(s + 1) * P], wqkv[:, c, 0:2 * D], start=(c == 0), stop=(c == DC - 1))
                    mm.then_inc(qk_done, 1)
                    if s >= 1:
                        pe.wait_ge(v_read, g * G + s)
                    for c in range(DC):
                        mm = nc.tensor.matmul(v_ps[:, 0:D], hT[:, c, s * P:(s + 1) * P], wqkv[:, c, 2 * D:], start=(c == 0), stop=(c == DC - 1))
                    mm.then_inc(v_done, 1)

                def group(g, ahead):
                    pe.wait_ge(hT_ready, g + 1)
                    project(g, 0)
                    if not (isinstance(g, int) and g == 0):
                        pe.wait_ge(rest_ready, g * 2 * DC)
                    for s in range(1, G):
                        pe.wait_ge(rot_ready, g * G + s)
                        project(g, s)
                        turn_channels(g, s - 1)
                    if ahead:
                        transposes(g + 1)
                    turn_channels(g, G - 1)

                transposes(0)
                group(0, True)
                with pe.Fori(1, NG - 1) as g:
                    group(g, True)
                group(NG - 1, False)


Q_BLOCKS = (0, 1, 2, 0, 1, 0)
K_BLOCKS = (0, 0, 0, 1, 1, 2)
Q_LOADS = ((0, 0, 3), (3, 0, 2), (5, 0, 1))
K_LOADS = tuple((n, part, 1) for n, part in enumerate(K_BLOCKS))
SLOTS = 4


def load_attended(k, sp, g):
    for a in range(2):
        sp.dma_start(k.od[:, a], k.od_dram[a][:, bass.ds(g * GT, GT)].rearrange("(c p) n -> p c n", p=P)).then_inc(k.od_in, 16)


def invert_denominators(k, act, g):
    act.wait_ge(k.od_in, 32 * (g + 1))
    k.nc.scalar.activation(k.od[:, 1], k.od[:, 1], ACT.Ln).then_inc(k.ln_ready, 1)
    act.wait_ge(k.ln_ready, g + 1)
    k.nc.scalar.activation(k.od[:, 1], k.od[:, 1], ACT.Exp, scale=-1.0).then_inc(k.inv_ready, 1)


def stage_attention(k):
    nc = k.nc
    ROWS = len(Q_BLOCKS) * DH
    KT, QB = S // P, S // 512
    HEADS = B * H
    VW = 2 * DH
    LEAD = 6
    BANK = (0, 1, 0, 2)
    TURN = KT - LEAD + 2
    STORED = 16 * QB
    LOADS_PER = len(Q_LOADS) + len(K_LOADS)
    with ExitStack() as ctx:
        sb, psum, sem = scratch(k, ctx)
        q = sb("t_q", [P, SLOTS, S], BF16)
        kk = sb("t_k", [P, SLOTS, S], BF16)
        v = sb("t_v", [P, SLOTS, KT, VW])
        probs = sb("t_p", [P, 2, S])
        peak = sb("t_peak", [P, 2, KT, QB])
        top = sb("t_top", [P, 2, KT])
        neg = sb("t_neg", [P, 2, KT])
        negparts = sb("t_negp", [P, PARTS, KT], BF16)
        negT = sb("t_negT", [PARTS * KT, P], BF16)
        o_sb = sb("t_o", [P, 512])
        wo = sb("t_wo", [P, DC, D])
        sT_ps = psum("t_sT_ps", [P, 2, 2, 512])
        mx_ps = psum("t_mx_ps", [P, 3, 512])
        pv_ps = psum("t_pv_ps", [P, 512])
        nT_ps = mx_ps[0:PARTS * KT, 2, 0:P]

        qk_in = [sem(f"t_in{u}") for u in range(SLOTS)]
        ones_ready, v_ready, wo_in, wo_ready = sem("t_ones"), sem("t_vr"), sem("t_woi"), sem("t_wor")
        mx_done, mx_read, top_ready, neg_steps, neg_ready = sem("t_mxd"), sem("t_mxr"), sem("t_top"), sem("t_ns"), sem("t_nr")
        nT_done, nT_ready, row_in = sem("t_nTd"), sem("t_nTr"), sem("t_row")
        s_done, e_done, pv_done, o_ready, o_out = sem("t_s"), sem("t_e"), sem("t_pv"), sem("t_or"), sem("t_oo")

        def turns(eng, turn):
            with eng.Fori(0, HEADS // SLOTS - 1) as i:
                for u in range(SLOTS):
                    turn(i * SLOTS + u, i, u, 2)
            i = HEADS // SLOTS - 1
            for u in range(SLOTS):
                turn(i * SLOTS + u, i, u, min(2, SLOTS - 1 - u))

        def later(i, u, by):
            return i + (u + by) // SLOTS, (u + by) % SLOTS

        with nc.Block() as block:
            @block.sync
            def _(sp):
                def load(n, u):
                    b, hd = n // H, n % H
                    for t, which, blocks in ((q, 0, Q_LOADS), (kk, 1, K_LOADS)):
                        src = k.qk_dram[bass.ds(which * DC + hd // HC, 1), :, bass.ds((hd % HC) * DH, DH), bass.ds(b * S, S)]
                        for at, part, count in blocks:
                            sp.dma_start(t[at * DH:(at + count) * DH, u, :],
                                         src[:, part:part + count].rearrange("o a d n -> (o a) d n")).then_inc(qk_in[u], 16)

                sp.nop().then_inc(o_out, STORED)
                load(0, 0)
                load(1, 1)
                sp.dma_start(wo[:], k.io["L1_Wo"].rearrange("(c p) n -> p c n", p=P)).then_inc(wo_in, 16)

                def rows(n, u):
                    sp.wait_ge(nT_ready, n + 1)
                    sp.dma_start(q[ROWS:ROWS + PARTS, u, :].rearrange("a (t n) -> a t n", n=P), negT[:]).then_inc(row_in, 16)

                rows(0, 0)

                def turn(n, i, u, ahead):
                    sp.wait_ge(pv_done, n * KT + 2)
                    if ahead >= 2:
                        load(n + 2, (u + 2) % SLOTS)
                    if ahead >= 1:
                        rows(n + 1, (u + 1) % SLOTS)
                    if ahead == 0:
                        sp.wait_ge(o_out, STORED * (n + 1))
                        load_attended(k, sp, 0)
                    sp.wait_ge(o_ready, n + 2)
                    b, hd = n // H, n % H
                    for j in range(QB):
                        cols = bass.ds(b * S + j * 512, 512)
                        sp.dma_start(k.od_dram[:, bass.ds(hd * DH, DH), cols], o_sb[j * VW:(j + 1) * VW, :]).then_inc(o_out, 16)

                turns(sp, turn)
                sp.wait_ge(o_out, STORED * (HEADS + 1))
                for u in range(SLOTS):
                    sp.wait_ge(qk_in[u], 16 * LOADS_PER * HEADS // SLOTS)

            @block.gpsimd
            def _(pool):
                for u in range(SLOTS):
                    nc.gpsimd.memset(kk[ROWS:ROWS + PARTS, u, :], 1.0).then_inc(ones_ready, 1)
                pool.wait_ge(ones_ready, SLOTS)
                nc.gpsimd.memset(v[:, :, :, DH:], 1.0).then_inc(ones_ready, 1)

                def copy_v(n, u):
                    b, hd = n // H, n % H
                    nc.gpsimd.tensor_copy(v[:, u, :, 0:DH], k.v[:, bass.ds(b * KT, KT), bass.ds(hd, 1), :].rearrange("p t o d -> p t (o d)")).then_inc(v_ready, 1)

                def split(n, u):
                    wait_alone(pool, top_ready, n + 1)
                    w = u % 2
                    g = nc.gpsimd
                    g.tensor_scalar_mul(neg[:, 0], top[:, w], -1.0).then_inc(neg_steps, 1)
                    pool.wait_ge(nT_done, n + 1)
                    wait_alone(pool, neg_steps, n * 4 + 1)
                    g.tensor_copy(negparts[:, 0], neg[:, 0]).then_inc(neg_steps, 1)
                    pool.wait_ge(neg_steps, n * 4 + 2)
                    g.tensor_tensor(neg[:, 1], neg[:, 0], negparts[:, 0], ALU.subtract).then_inc(neg_steps, 1)
                    wait_alone(pool, neg_steps, n * 4 + 3)
                    g.tensor_copy(negparts[:, 1], neg[:, 1]).then_inc(neg_steps, 1)
                    pool.wait_ge(neg_steps, n * 4 + 4)
                    g.tensor_tensor(negparts[:, 2], neg[:, 1], negparts[:, 1], ALU.subtract).then_inc(neg_ready, 1)
                    pool.wait_ge(neg_ready, n + 1)

                copy_v(0, 0)
                copy_v(1, 1)
                split(0, 0)

                def turn(n, i, u, ahead):
                    pool.wait_ge(pv_done, n * KT + 2)
                    if ahead >= 2:
                        copy_v(n + 2, (u + 2) % SLOTS)
                    if ahead >= 1:
                        split(n + 1, (u + 1) % SLOTS)

                turns(pool, turn)

            @block.vector
            def _(dve):
                dve.nop().then_inc(mx_read, 4)

                def maxima(n, w, m, blocks):
                    for kb in blocks:
                        t = (n * KT + m) * QB + kb
                        dve.wait_ge(mx_done, t + 1)
                        nc.vector.reduce_max(peak[:, w, m, kb:kb + 1], mx_ps[:, BANK[kb], :], AX.X).then_inc(mx_read, 1)
                    if m == KT - 1 and kb == QB - 1:
                        dve.wait_ge(mx_read, (n + 1) * KT * QB + 4)
                        nc.vector.reduce_max(top[:, w], peak[:, w], AX.X).then_inc(top_ready, 1)

                def turned(n):
                    dve.wait_ge(nT_done, n + 2)
                    dve.wait_ge(row_in, 16 * (n + 1))
                    nc.vector.tensor_copy(negT[:], nT_ps).then_inc(nT_ready, 1)

                for m in range(KT):
                    maxima(0, 0, m, range(QB))
                for m in range(LEAD):
                    maxima(1, 1, m, (0,))
                    if m == 2:
                        turned(0)
                    maxima(1, 1, m, (1, 2, 3))

                def turn(n, i, u, ahead):
                    for kt in range(KT):
                        m = kt + LEAD
                        if m < KT:
                            lead, tile = ahead >= 1, (n + 1, (u + 1) % 2, m)
                        else:
                            lead, tile = ahead >= 2, (n + 2, u % 2, m - KT)
                        if lead:
                            maxima(*tile, (0,))
                        if kt == TURN + 1 and ahead >= 1:
                            turned(n + 1)
                        if lead:
                            maxima(*tile, (1, 2, 3))

                turns(dve, turn)
                dve.wait_ge(wo_in, 16)
                for b in range(B):
                    ga = k.mods[:, b, GA, :].unsqueeze(1).to_broadcast([P, DC, D])
                    nc.vector.tensor_tensor(k.ga_wo[:, b], wo[:], ga, ALU.mult).then_inc(wo_ready, 1)
                dve.wait_ge(wo_ready, B)

            @block.scalar
            def _(act):
                act.nop().then_inc(e_done, 2)

                def exps(n, kt):
                    for hf in range(2):
                        act.wait_ge(s_done, (n * KT + kt) * 2 + hf + 1)
                        if hf == 0:
                            act.wait_ge(pv_done, n * KT + kt + 1)
                        nc.scalar.activation(probs[:, kt % 2, hf * 1024:(hf + 1) * 1024].rearrange("p (j n) -> p j n", n=512),
                                             sT_ps[:, hf], ACT.Exp).then_inc(e_done, 1)

                exps(0, 0)

                def turn(n, i, u, ahead):
                    for kt in range(1, KT):
                        exps(n, kt)
                    if ahead >= 1:
                        exps(n + 1, 0)
                    act.wait_ge(pv_done, (n + 1) * KT + 2)
                    act.wait_ge(o_out, STORED * (n + 1))
                    nc.scalar.copy(o_sb[:], pv_ps[:]).then_inc(o_ready, 1)

                turns(act, turn)
                invert_denominators(k, act, 0)

            @block.tensor
            def _(pe):
                pe.nop().then_inc(pv_done, 2)
                pe.nop().then_inc(o_ready, 1)
                pe.nop().then_inc(nT_done, 1)
                pe.nop().then_inc(row_in, 16)

                def maximum(n, u, m, kb):
                    t = (n * KT + m) * QB + kb
                    pe.wait_ge(mx_read, t + 3 if BANK[kb] == 0 else t + 1)
                    nc.tensor.matmul(mx_ps[:, BANK[kb], :], q[0:ROWS, u, m * P:(m + 1) * P], kk[0:ROWS, u, kb * 512:(kb + 1) * 512],
                                     start=True, stop=True).then_inc(mx_done, 1)

                def scores(n, u, kt, qb):
                    hf, j = qb // 2, qb % 2
                    if j == 0:
                        pe.wait_ge(e_done, (n * KT + kt) * 2 + hf + 1)
                    mm = nc.tensor.matmul(sT_ps[:, hf, j, :], kk[0:ROWS + PARTS, u, kt * P:(kt + 1) * P],
                                          q[0:ROWS + PARTS, u, qb * 512:(qb + 1) * 512], start=True, stop=True)
                    if j == 1:
                        mm.then_inc(s_done, 1)

                def weigh(n, u, kt):
                    pe.wait_ge(e_done, (n * KT + kt) * 2 + 4)
                    if kt == 0:
                        pe.wait_ge(v_ready, n + 1)
                        pe.wait_ge(o_ready, n + 1)
                    for j in range(QB):
                        mm = nc.tensor.matmul(pv_ps[j * VW:(j + 1) * VW, :], v[:, u, kt, :], probs[:, kt % 2, j * 512:(j + 1) * 512],
                                              start=(kt == 0), stop=(kt == KT - 1), tile_position=(0, j * VW))
                    mm.then_inc(pv_done, 1)

                def turn_maxima(n, read):
                    wait_alone(pe, neg_ready, n + 1)
                    pe.wait_ge(mx_read, read + 4)
                    nc.tensor.matmul(nT_ps, negparts[:].rearrange("p a t -> p (a t)"), k.identb[:], start=True, stop=True).then_inc(nT_done, 1)

                pe.wait_ge(qk_in[0], 16 * LOADS_PER)
                for m in range(KT):
                    for kb in range(QB):
                        maximum(0, 0, m, kb)
                pe.wait_ge(qk_in[1], 16 * LOADS_PER)
                for m in range(LEAD):
                    for kb in range(QB):
                        if m == 2 and kb == QB - 1:
                            pe.wait_ge(nT_ready, 1)
                        maximum(1, 1, m, kb)
                    if m == 1:
                        turn_maxima(0, (KT + 2) * QB)
                pe.wait_ge(ones_ready, SLOTS + 1)
                pe.wait_ge(row_in, 32)
                for qb in range(QB):
                    scores(0, 0, 0, qb)

                def turn(n, i, u, ahead):
                    for kt in range(KT):
                        m = kt + LEAD
                        if m < KT:
                            lead, tile = ahead >= 1, (n + 1, (u + 1) % SLOTS, m)
                        else:
                            lead, tile = ahead >= 2, (n + 2, (u + 2) % SLOTS, m - KT)
                        if m == KT and ahead >= 2:
                            i2, u2 = later(i, u, 2)
                            pe.wait_ge(qk_in[u2], 16 * LOADS_PER * (i2 + 1))
                        if kt + 1 == KT and ahead >= 1:
                            pe.wait_ge(row_in, 16 * (n + 3))
                        def peak_at(kb):
                            if lead:
                                maximum(*tile, kb)

                        def next_scores(*blocks):
                            for qb in blocks:
                                if kt + 1 < KT:
                                    scores(n, u, kt + 1, qb)
                                elif ahead >= 1:
                                    scores(n + 1, (u + 1) % SLOTS, 0, qb)

                        peak_at(0)
                        next_scores(0, 1)
                        peak_at(1)
                        next_scores(2)
                        peak_at(2)
                        next_scores(3)
                        if kt == TURN + 1 and ahead >= 2:
                            pe.wait_ge(nT_ready, n + 2)
                        peak_at(3)
                        weigh(n, u, kt)
                        if kt == TURN and ahead >= 1:
                            turn_maxima(n + 1, (n + 2) * KT * QB + ((TURN + LEAD - KT + 1) * QB if ahead >= 2 else 0))

                turns(pe, turn)



def stage_peer(k):
    nc, io = k.nc, k.io
    SLOTS_Y = 4
    with ExitStack() as ctx:
        sb, psum, sem = scratch(k, ctx)
        at = sb("p_at", [P, DC, GT])
        shift_x = sb("p_shift", [P, G])
        stats = sb("p_stats", [P, G, 6])
        mv = sb("p_mv", [P, G, 2])
        std = sb("p_std", [P, G])
        xn = sb("p_xn", [P, G, D])
        h = sb("p_h", [P, G, D])
        hu = sb("p_hu", [P, G, D])
        hT = sb("p_hT", [P, DC, GT])
        val = sb("p_val", [P, 2, PH])
        arg = sb("p_arg", [P, 2, PH, 8], U32)
        score = sb("p_score", [P, SLOTS_Y, PH])
        sl = sb("p_sl", [P, SLOTS_Y, PH], I32)
        Y = sb("p_Y", [P, SLOTS_Y, PH, 2 * D])
        dump = sb("p_dump", [P, PH, D])
        dot = sb("p_dot", [P, 2, PH])
        act_dot = sb("p_gelu", [P, 2, PH])
        gk = sb("p_gk", [P, 2, PH])
        diag = sb("p_diag", [P, 2, PH, P])
        part = sb("p_part", [P, D])

        score_ready, xn_ready = sem("p_sc"), sem("p_xn")
        at_ready, proj_done, steps = sem("p_at"), sem("p_proj"), sem("p_steps")
        stats_ready, std_ready, rstd_ready, h_ready, h_kept = sem("p_st"), sem("p_std"), sem("p_rstd"), sem("p_h"), sem("p_hk")
        hT_done, hT_ready, sim_done = sem("p_hTd"), sem("p_hTr"), sem("p_sim")
        val_ready, arg_ready, idx_ready = sem("p_val"), sem("p_arg"), sem("p_idx")
        y_in = [sem(f"p_y{u}") for u in range(SLOTS_Y)]
        dots_done, gelu_ready, gk_ready, diag_ready, sums_done, part_ready, x_ready, x_out = (
            sem("p_dots"), sem("p_gelu"), sem("p_gk"), sem("p_diag"), sem("p_sums"), sem("p_part"), sem("p_x"), sem("p_xo"))

        tmp_ps = psum("p_tmp_ps", [P, 2, 512])
        sim_ps = psum("p_sim_ps", [P, 2, SIMS])
        out_ps = psum("p_out_ps", [P, 512])

        def inside(g, u):
            return not isinstance(g, int) or 0 <= g * G + u < NT

        def run(eng, step, ahead):
            for u in range(G):
                step(0, u)
                ahead(0, u)
            with eng.Fori(1, NG - 1) as g:
                for u in range(G):
                    step(g, u)
                    ahead(g, u)
            for u in range(G):
                step(NG - 1, u)
            for u in range(G):
                step(NG, u)

        with nc.Block() as block:
            @block.sync
            def _(sp):
                def store(g):
                    sp.wait_ge(x_ready, (g + 1) * G)
                    sp.dma_start(k.out.rearrange("b (t p) d -> p (b t) d", p=P)[:, bass.ds(g * G, G), :],
                                 k.x[:, bass.ds(g * G, G), :]).then_inc(x_out, 16)

                sp.wait_ge(at_ready, 1)
                load_attended(k, sp, 1)
                with sp.Fori(0, NG - 2) as g:
                    sp.wait_ge(at_ready, g + 2)
                    load_attended(k, sp, g + 2)
                    store(g)
                store(NG - 2)
                store(NG - 1)
                sp.wait_ge(x_out, 16 * NG)

            @block.gpsimd
            def _(pool):
                def step(g, u):
                    if not inside(g, u):
                        return
                    t = g * G + u
                    if inside(g, u - SLOTS_Y):
                        pool.wait_ge(sums_done, t - SLOTS_Y + 2)
                    wait_alone(pool, idx_ready, t + 1)
                    for j in range(PH):
                        nc.gpsimd.indirect_dma_start(Y[:, u, j, :], None, io["L1_table"],
                                                     bass.IndirectOffsetOnAxis(ap=sl[:, u, j:j + 1], axis=0)).then_inc(y_in[u], 16)

                run(pool, step, lambda g, u: None)

            @block.vector
            def _(dve):
                o = Order(dve, steps)
                V = nc.vector
                mod = lambda g, m: k.mods[:, bass.ds(g // GB, 1), m, :]

                def attended(g):
                    dve.wait_ge(k.inv_ready, g + 1)
                    V.tensor_tensor(at[:], k.od[:, 0], k.od[:, 1], ALU.mult).then_inc(at_ready, 1)

                def residual(g):
                    dve.wait_ge(proj_done, g + 1)
                    xg = k.x[:, bass.ds(g * G, G), :]
                    o.mark(V.tensor_tensor(xg, xg, tmp_ps[:].rearrange("p a (s d) -> p (a s) d", d=D), ALU.add))

                def statistics(g):
                    o.settle_alone()
                    for s in range(G):
                        o.mark(V.bn_stats(stats[:, s, :], k.x[:, bass.ds(g * G + s, 1), :]))
                    o.settle_alone()
                    for s in range(G):
                        V.bn_aggr(mv[:, s, :], stats[:, s, :]).then_inc(stats_ready, 1)

                def deviation(g):
                    dve.wait_ge(std_ready, g + 1)
                    o.mark(V.reciprocal(std[:], std[:]))
                    o.settle()
                    V.scalar_tensor_tensor(shift_x[:], mv[:, :, 0], -1.0, std[:], ALU.mult, ALU.mult).then_inc(rstd_ready, 1)

                def scale(g):
                    dve.wait_ge(xn_ready, (g + 1) * G)
                    o.mark(V.tensor_tensor(xn[:], xn[:], mod(g, CB).to_broadcast([P, G, D]), ALU.mult))

                def shift(g):
                    o.settle()
                    if not isinstance(g, int) or g > 0:
                        dve.wait_ge(h_kept, 2 * g)
                    V.tensor_tensor(h[:], xn[:], mod(g, SB).to_broadcast([P, G, D]), ALU.add).then_inc(h_ready, 1)

                def dots(g, u):
                    v, t = u % SLOTS_Y, g * G + u
                    turn = g + u // SLOTS_Y
                    dve.wait_ge(y_in[v], 16 * PH * (turn + 1))
                    dve.wait_ge(h_kept, 2 * turn + 1 + v // 2)
                    for j in range(PH):
                        V.tensor_tensor_reduce(dump[:, j, :], hu[:, v, :], Y[:, v, j, 0:D], 1.0, 0.0, ALU.mult, ALU.add,
                                               dot[:, v % 2, j:j + 1]).then_inc(dots_done, 1)

                def by_head(u):
                    return sim_ps[:, u % 2, :].rearrange("p (a n) -> p a n", n=KEYS)

                def maxima(g, u):
                    t = g * G + u
                    dve.wait_ge(sim_done, t + 1)
                    if not (isinstance(g, int) and t == 0):
                        dve.wait_ge(score_ready, t)
                    V.reduce_max(val[:].rearrange("p a j -> p (a j)"), by_head(u), AX.X).then_inc(val_ready, 1)

                def places(g, u):
                    sims = by_head(u)
                    wait_alone(dve, val_ready, g * G + u + 1)
                    for a in range(2):
                        for j in range(PH):
                            V.max_index(arg[:, a, j, :], val[:, a, j:j + 1].to_broadcast([P, 8]), sims[:, a * PH + j, :]).then_inc(arg_ready, 1)

                def rows(g, u):
                    V.tensor_tensor(score[:, u, :], val[:, 0, :], val[:, 1, :], ALU.add).then_inc(score_ready, 1)
                    dve.wait_ge(arg_ready, 2 * PH * (g * G + u + 1))
                    V.scalar_tensor_tensor(sl[:, u, :], arg[:, 0, :, 0], float(KEYS), arg[:, 1, :, 0], ALU.mult, ALU.add).then_inc(idx_ready, 1)

                def weights(g, u):
                    v, t = u % SLOTS_Y, g * G + u
                    dve.wait_ge(gelu_ready, t + 1)
                    V.scalar_tensor_tensor(gk[:, v % 2, :], score[:, v, :], 0.0, act_dot[:, v % 2, :], ALU.max, ALU.mult).then_inc(gk_ready, 1)

                def weighted(g, u):
                    t = g * G + u
                    dve.wait_ge(sums_done, t + 2)
                    if not (isinstance(g, int) and t == 0):
                        dve.wait_ge(x_ready, t)
                    gb = k.mods[:, bass.ds(t // (NT // B), 1), GBI, :].rearrange("p o d -> p (o d)")
                    V.tensor_tensor(part[:], out_ps[:, 0:D], gb, ALU.mult).then_inc(part_ready, 1)

                def finish(g, u):
                    t = g * G + u
                    dve.wait_ge(part_ready, t + 1)
                    xt = k.x[:, bass.ds(t, 1), :].rearrange("p o d -> p (o d)")
                    V.tensor_tensor(xt, xt, part[:], ALU.add).then_inc(x_ready, 1)

                def step(g, u):
                    more = inside(g + 1, 0)
                    if inside(g, u):
                        maxima(g, u)
                    if u == 2 and more:
                        deviation(g + 1)
                    if inside(g, u - 3):
                        weights(g, u - 3)
                    if inside(g, u - 4):
                        weighted(g, u - 4)
                    if inside(g, u):
                        places(g, u)
                        rows(g, u)
                    if u == 1 and more:
                        residual(g + 1)
                    if u == 2 and more:
                        scale(g + 1)
                    if inside(g, u - 4):
                        finish(g, u - 4)
                    if u == 2 and more:
                        shift(g + 1)
                    if inside(g, u - 2):
                        dots(g, u - 2)

                AHEAD = 1 + G + 1 + 1

                def ahead(g, u):
                    if u == 0:
                        attended(g + 1)
                    if u == 1:
                        statistics(g + 1)

                attended(0)
                residual(0)
                statistics(0)
                deviation(0)
                scale(0)
                shift(0)
                first = o.n

                def counted(g, u):
                    if u == 0:
                        o.turn(g, first, AHEAD)
                    step(g, u)

                run(dve, counted, ahead)

            @block.scalar
            def _(act):
                def deviation(g):
                    act.wait_ge(stats_ready, (g + 1) * G)
                    nc.scalar.activation(std[:], mv[:, :, 1], ACT.Sqrt, bias=k.eps[:, 0:1]).then_inc(std_ready, 1)

                def normalise(g):
                    act.wait_ge(rstd_ready, g + 1)
                    for s in range(G):
                        nc.scalar.activation(xn[:, s, :], k.x[:, bass.ds(g * G + s, 1), :].rearrange("p o d -> p (o d)"), ACT.Identity,
                                             bias=shift_x[:, s:s + 1], scale=std[:, s:s + 1]).then_inc(xn_ready, 1)

                def turned(g, last):
                    act.wait_ge(hT_done, g + 1)
                    if last:
                        act.wait_ge(sim_done, g * G)
                    nc.scalar.copy(hT[:], tmp_ps[:]).then_inc(hT_ready, 1)

                def keep(g, half):
                    if inside(g, 2 * half - G):
                        act.wait_ge(dots_done, PH * (g * G + 2 * half - 2))
                    nc.scalar.copy(hu[:, 2 * half:2 * half + 2, :], h[:, 2 * half:2 * half + 2, :]).then_inc(h_kept, 1)

                def diagonals(g, u):
                    v, t = u % SLOTS_Y, g * G + u
                    act.wait_ge(gk_ready, t + 1)
                    if inside(g, u - 1):
                        act.wait_ge(sums_done, t)
                    for j in range(PH):
                        nc.scalar.activation(diag[:, v % 2, j, :], k.ident[:], ACT.Copy, scale=gk[:, v % 2, j:j + 1]).then_inc(diag_ready, 1)

                def step(g, u):
                    more = not isinstance(g, int) or g + 1 < NG
                    if u == 2 and more:
                        normalise(g + 1)
                    if inside(g, u - 3):
                        diagonals(g, u - 3)
                    if u == 0 and more:
                        invert_denominators(k, act, g + 1)
                    if inside(g, u - 2):
                        v, t = (u - 2) % SLOTS_Y, g * G + u - 2
                        act.wait_ge(dots_done, PH * (t + 1))
                        nc.scalar.activation(act_dot[:, v % 2, :], dot[:, v % 2, :], ACT.Gelu).then_inc(gelu_ready, 1)
                    if inside(g, u) and u == 1:
                        keep(g, 1)

                def ahead(g, u):
                    if u == 1:
                        deviation(g + 1)
                    if u == 2:
                        turned(g + 1, True)
                    if u == 3:
                        keep(g + 1, 0)

                deviation(0)
                normalise(0)
                turned(0, False)
                keep(0, 0)
                run(act, step, ahead)

            @block.tensor
            def _(pe):
                pe.nop().then_inc(sums_done, 1)

                def project(g):
                    pe.wait_ge(at_ready, g + 1)
                    if not isinstance(g, int) or g > 0:
                        pe.wait_ge(hT_ready, g)
                    for s in range(G):
                        for c in range(DC):
                            mm = nc.tensor.matmul(tmp_ps[:, s // 2, (s % 2) * D:(s % 2 + 1) * D],
                                                  at[:, c, s * P:(s + 1) * P], k.ga_wo[:, bass.ds(g // GB, 1), c, :],
                                                  start=(c == 0), stop=(c == DC - 1))
                    mm.then_inc(proj_done, 1)

                def transposes(g):
                    pe.wait_ge(h_ready, g + 1)
                    for c in range(DC):
                        for s in range(G):
                            mm = nc.tensor.transpose(tmp_ps[:, c, s * P:(s + 1) * P], h[:, s, c * P:(c + 1) * P], k.ident[:])
                    mm.then_inc(hT_done, 1)

                def similarities(g, u):
                    t = g * G + u
                    if u == 0:
                        pe.wait_ge(hT_ready, g + 1)
                    if inside(g, u - 2):
                        pe.wait_ge(arg_ready, 2 * PH * (t - 1))
                    for n in range(2):
                        for c in range(DC):
                            mm = nc.tensor.matmul(sim_ps[:, u % 2, n * 512:(n + 1) * 512], hT[:, c, u * P:(u + 1) * P],
                                                  k.wsim[:, c, n * 512:(n + 1) * 512], start=(c == 0), stop=(c == DC - 1))
                    mm.then_inc(sim_done, 1)

                def sums(g, u):
                    v, t = u % SLOTS_Y, g * G + u
                    pe.wait_ge(diag_ready, PH * (t + 1))
                    if inside(g, u - 1):
                        pe.wait_ge(part_ready, t)
                    for j in range(PH):
                        mm = nc.tensor.matmul(out_ps[:, 0:D], diag[:, v % 2, j, :], Y[:, v, j, D:], start=(j == 0), stop=(j == PH - 1))
                    mm.then_inc(sums_done, 1)

                def step(g, u):
                    if u < G - 1 and inside(g, u + 1):
                        similarities(g, u + 1)
                    elif u == G - 1 and inside(g + 1, 0):
                        similarities(g + 1, 0)
                    if inside(g, u - 3):
                        sums(g, u - 3)

                def ahead(g, u):
                    if u == 0:
                        project(g + 1)
                    if u == 2:
                        transposes(g + 1)

                project(0)
                transposes(0)
                similarities(0, 0)
                run(pe, step, ahead)


def build(nc, io, out, upto=99):
    ctx = ExitStack()
    with ctx:
        k = setup(nc, ctx, io)
        k.out = out
        k.TILES = 2 * NT + E
        k.COLS = k.TILES + 2
        k.token = ctx.enter_context(nc.sbuf_tensor("token", [P, k.COLS], I32))
        dram = lambda name, shape, dt=F32: nc.dram_tensor(name, shape, dt, kind="Internal").ap()
        k.h2_dram = dram("h2_dram", [T, D])
        k.ys_dram = dram("ys_dram", [k.TILES * P, D])
        k.qk_dram = dram("qk_dram", [2 * DC, PARTS, P, T], BF16)
        k.od_dram = dram("od_dram", [2, D, T])
        k.w_moe_in = ctx.enter_context(nc.semaphore("w_moe_in"))
        k.slots = ctx.enter_context(nc.sbuf_tensor("slots", [P, NT, 2], I32))
        k.wts = ctx.enter_context(nc.sbuf_tensor("wts", [P, 2, NT], F32))
        k.wsim = ctx.enter_context(nc.sbuf_tensor("wsim", [P, DC, SIMS], F32))
        k.eid = ctx.enter_context(nc.sbuf_tensor("eid", [1, k.COLS], I32))
        with ExitStack() as l0:
            def sb(name, shape):
                return l0.enter_context(nc.sbuf_tensor(name, shape, F32))
            k.kvsum = sb("kvsum", [P, B, DC, P + 1])
            k.logits = sb("logits", [P, NT, E])
            stage_modulation(k)
            stage_linear_attention_sums(k)
            k.wg = sb("wg", [P, E, DC, F])
            k.wu = sb("wu", [P, E, DC, F])
            k.wd = sb("wd", [P, E, FC, D])
            stage_linear_attention_apply(k)
            if upto >= 3:
                stage_route(k)
            if upto >= 4:
                stage_experts(k)
        if upto >= 5:
            k.od = ctx.enter_context(nc.sbuf_tensor("od", [P, 2, DC, GT], F32))
            k.od_in, k.ln_ready, k.inv_ready = (ctx.enter_context(nc.semaphore(n)) for n in ("od_in", "ln_ready", "inv_ready"))
            k.ga_wo = ctx.enter_context(nc.sbuf_tensor("ga_wo", [P, B, DC, D], F32))
            with ExitStack() as l1:
                k.v = l1.enter_context(nc.sbuf_tensor("v", [P, NT, H, DH], F32))
                stage_project(k)
                if upto >= 6:
                    stage_attention(k)
        if upto >= 7:
            stage_peer(k)


def layout(inputs):
    def plain(a):
        return np.ascontiguousarray(np.asarray(a))

    arrays = {"L0_attn_x": plain(inputs["L0_attn_x"])}
    for l in (0, 1):
        arrays[f"L{l}_cT"] = plain(np.asarray(inputs[f"L{l}_c"]).T)
        arrays[f"L{l}_wmod"] = plain(inputs[f"L{l}_wmod"])
    for n in "qkv":
        arrays[f"L0_W{n}T"] = plain(np.asarray(inputs[f"L0_attn_W{n}"]).T)
        arrays[f"L0_attn_b{n}"] = plain(inputs[f"L0_attn_b{n}"])
    for n in ("gamma", "beta"):
        arrays[f"L0_attn_{n}"] = plain(inputs[f"L0_attn_{n}"])
    arrays["L0_router"] = plain(inputs["L0_ffn_router_kernel_DE"])
    for n, source in (("gate", "gating_EDF"), ("up", "up_EDF"), ("down", "down_EFD")):
        arrays[f"L0_{n}"] = plain(inputs[f"L0_ffn_kernel_{source}"])
    arrays["L1_Wqkv"] = plain(inputs["L1_attn_Wqkv"])
    arrays["L1_Wo"] = plain(inputs["L1_attn_Wo"])
    arrays["L1_wqT"] = plain(np.asarray(inputs["L1_ffn_w_q"]).T)
    arrays["L1_keysT"] = plain(np.asarray(inputs["L1_ffn_keys"]).transpose(2, 0, 3, 1).reshape(2 * PH * P, KEYS))
    arrays["L1_table"] = plain(np.concatenate([np.asarray(inputs["L1_ffn_w_down"]), np.asarray(inputs["L1_ffn_w_up"])], axis=1))

    lane = np.arange(P)
    arrays["ident"] = np.eye(P, dtype=np.float32)
    arrays["ones"] = np.ones((P, P), np.float32)
    arrays["tri"] = np.triu(np.ones((P, P), np.float32), 1)
    arrays["head_mask"] = np.concatenate([lane[:, None] // DH == lane[None, :] // DH,
                                          lane[:, None] // DH == np.arange(HC)[None, :]], axis=1).astype(np.float32)
    arrays["rank"] = np.tile(E - np.arange(E, dtype=np.float32), (P, 1))
    arrays["tile_start"] = (np.arange(2 * NT + E + 2, dtype=np.float32) * P)[None]
    arrays["iota"] = np.tile(lane.astype(np.float32), (P, 1))
    arrays["ids"] = (lane[:, None] + P * np.arange(NT)[None, :]).astype(np.float32)
    freq = (1.0 / np.float32(10000.0) ** (np.arange(0, DH, 2, dtype=np.float32) / np.float32(DH))).astype(np.float32)
    angle = np.outer(np.arange(S, dtype=np.float32), freq).astype(np.float32)
    arrays["rope"] = np.stack([np.concatenate([np.cos(angle), np.cos(angle)], 1),
                               np.concatenate([-np.sin(angle), np.sin(angle)], 1)]).astype(np.float32)
    return arrays


def kernel(**inputs):
    import concourse.bacc as bacc
    from concourse.bass_utils import run_bass_kernel_spmd

    nc = bacc.Bacc("TRN2", target_bir_lowering=False, num_devices=1)
    arrays, io = {}, {}
    for name, a in layout(inputs).items():
        arrays[f"in_{name}_dram"] = a
        io[name] = nc.dram_tensor(f"in_{name}_dram", a.shape, mybir.dt.from_np(a.dtype), kind="ExternalInput").ap()
    out = nc.dram_tensor("out_0_dram", (B, S, D), F32, kind="ExternalOutput").ap()
    build(nc, io, out)
    r = run_bass_kernel_spmd(nc, [arrays], core_ids=[0])
    return r.results[0]["out_0_dram"]
```
